# Optimizing a Trainium2 kernel written in Bass

```python
import numpy as np
import jax
import jax.numpy as jnp

def _softmax(x, axis=-1):
    return jax.nn.softmax(x, axis=axis)

def _gelu(x):
    return jax.nn.gelu(x, approximate=True)

def _silu(x):
    return jax.nn.silu(x)

def _sigmoid(x):
    return jax.nn.sigmoid(x)

def _layernorm(x, axis=-1, eps=1e-05):
    m = jnp.mean(x, axis=axis, keepdims=True)
    v = jnp.var(x, axis=axis, keepdims=True)
    return (x - m) / jnp.sqrt(v + eps)

def _scatter_add(tgt, idx, src, axis=0):
    return tgt.at[idx].add(src)

def _segment_sum(src, seg, n):
    return jax.ops.segment_sum(src, seg, n)
kernel_name = 'mk_gnn_ffn_d1_gnn_r8_3e4a1e'

def setup_inputs(seed: int=0):
    np.random.seed(seed)
    _w = jnp.asarray

    def _rec_inputs():
        import jax
        import jax.numpy as jnp
        _gk = jax.random.key(seed)
        x = -0.0006008 + 1.001 * jax.random.normal(jax.random.fold_in(_gk, 1), (6250, 256), jnp.float32)
        src = jax.random.randint(jax.random.fold_in(_gk, 2), (200000,), 0, 6250, jnp.int32)
        dst = jnp.minimum((6250 * jax.random.uniform(jax.random.fold_in(_gk, 3), (200000,)) ** 2.0).astype(jnp.int32), 49999)
        _o = jnp.argsort(dst, stable=True)
        src = src[_o]
        dst = dst[_o]
        edge_weight = jax.random.uniform(jax.random.fold_in(_gk, 12), (200000,), jnp.float32, 0.0, 0.999994)
        return (x, src, dst, edge_weight)
    x, src, dst, edge_weight = _rec_inputs()

    def _L0_gnn_setup():
        import jax, jax.numpy as jnp
        import numpy as np
        N_NODES, N_EDGES, F_IN, F_OUT = (1250, 40000, 256, 256)
        key = jax.random.key(seed)
        k1, k2, k3, k4, k5, k6 = jax.random.split(key, 6)
        feature = jax.random.normal(k1, (N_NODES, F_IN), jnp.float32)
        ew = jax.random.uniform(k2, (N_EDGES,), jnp.float32)
        src = jax.random.randint(k3, (N_EDGES,), 0, N_NODES)
        dst = jax.random.randint(k4, (N_EDGES,), 0, N_NODES)
        W = jax.random.normal(k5, (F_OUT, 2 * F_IN), jnp.float32) / np.sqrt(2 * F_IN)
        b = jax.random.normal(k6, (F_OUT,), jnp.float32) * 0.01
        return {'feature': feature, 'ew': ew, 'src': src, 'dst': dst, 'W': W, 'b': b}
    _L0_gnn_all = _L0_gnn_setup()
    _L0_gnn_in = {k: v for k, v in _L0_gnn_all.items() if k in ('W', 'b')}
    del _L0_gnn_all

    def _L0_ffn_setup():
        import jax, jax.numpy as jnp
        import numpy as np
        B, N, D = (16, 512, 256)
        NUM_EXPERTS, TOP_K, HEADS = (4, 2, 4)
        N_EDGES = 131072
        LN_EPS = 1e-05

        def _layernorm(x, g, b):
            mu = x.mean(-1, keepdims=True)
            var = ((x - mu) ** 2).mean(-1, keepdims=True)
            return (x - mu) * jax.lax.rsqrt(var + LN_EPS) * g + b

        def _forward(x, edge_index, W_gat, att_src, att_dst, b_gat, ln_gamma, ln_beta, W1, b1, W2, b2):
            Bc, Nc, Dc = x.shape
            M = Bc * Nc
            x_flat = x.reshape(M, Dc)
            h = (x_flat @ W_gat).reshape(M, HEADS, NUM_EXPERTS)
            loops = jnp.arange(M, dtype=edge_index.dtype)
            src = jnp.concatenate([edge_index[0], loops])
            dst = jnp.concatenate([edge_index[1], loops])
            a_src = (h * att_src).sum(-1)
            a_dst = (h * att_dst).sum(-1)
            e = jax.nn.leaky_relu(a_src[src] + a_dst[dst], negative_slope=0.2)
            e_max = jax.ops.segment_max(e, dst, num_segments=M)
            ee = jnp.exp(e - e_max[dst])
            denom = jax.ops.segment_sum(ee, dst, num_segments=M)
            alpha = ee / (denom[dst] + 1e-16)
            msg = h[src] * alpha[:, :, None]
            agg = jax.ops.segment_sum(msg, dst, num_segments=M).reshape(M, HEADS * NUM_EXPERTS) + b_gat
            scores = _layernorm(agg, ln_gamma, ln_beta).reshape(M, HEADS, NUM_EXPERTS).mean(1)
            scores = scores.reshape(Bc, Nc, NUM_EXPERTS)
            topk_s, topk_i = jax.lax.top_k(scores, TOP_K)
            w = jax.nn.softmax(topk_s, axis=-1)
            out = jnp.zeros_like(x)
            for ei in range(NUM_EXPERTS):
                g = jnp.where(topk_i == ei, w, 0.0).sum(-1)
                hh = jax.nn.gelu(x @ W1[ei] + b1[ei], approximate=False)
                out = out + g[..., None] * (hh @ W2[ei] + b2[ei])
            return out
        key = jax.random.key(seed)
        ks = jax.random.split(key, 8)
        s = 0.05
        return {'x': jax.random.normal(ks[0], (B, N, D), jnp.float32), 'W_gat': jax.random.normal(ks[1], (D, HEADS * NUM_EXPERTS), jnp.float32) * s, 'att_src': jax.random.normal(ks[2], (HEADS, NUM_EXPERTS), jnp.float32) * s, 'att_dst': jax.random.normal(ks[3], (HEADS, NUM_EXPERTS), jnp.float32) * s, 'b_gat': jnp.zeros((HEADS * NUM_EXPERTS,), jnp.float32), 'ln_gamma': jnp.ones((HEADS * NUM_EXPERTS,), jnp.float32), 'ln_beta': jnp.zeros((HEADS * NUM_EXPERTS,), jnp.float32), 'W1': jax.random.normal(ks[4], (NUM_EXPERTS, D, 2 * D), jnp.float32) * s, 'b1': jnp.zeros((NUM_EXPERTS, 2 * D), jnp.float32), 'W2': jax.random.normal(ks[5], (NUM_EXPERTS, 2 * D, D), jnp.float32) * s, 'b2': jnp.zeros((NUM_EXPERTS, D), jnp.float32), 'edge_index': jax.random.randint(ks[6], (2, N_EDGES), 0, B * N, jnp.int32)}
    _L0_ffn_all = _L0_ffn_setup()
    _L0_ffn_in = {k: v for k, v in _L0_ffn_all.items() if k in ('W_gat', 'att_src', 'att_dst', 'b_gat', 'ln_gamma', 'ln_beta', 'W1', 'b1', 'W2', 'b2', 'edge_index')}
    del _L0_ffn_all
    return {'x': x, 'src': src, 'dst': dst, 'edge_weight': edge_weight, 'L0_gnn_W': _L0_gnn_in['W'], 'L0_gnn_b': _L0_gnn_in['b'], 'L0_ffn_W_gat': _L0_ffn_in['W_gat'], 'L0_ffn_att_src': _L0_ffn_in['att_src'], 'L0_ffn_att_dst': _L0_ffn_in['att_dst'], 'L0_ffn_b_gat': _L0_ffn_in['b_gat'], 'L0_ffn_ln_gamma': _L0_ffn_in['ln_gamma'], 'L0_ffn_ln_beta': _L0_ffn_in['ln_beta'], 'L0_ffn_W1': _L0_ffn_in['W1'], 'L0_ffn_b1': _L0_ffn_in['b1'], 'L0_ffn_W2': _L0_ffn_in['W2'], 'L0_ffn_b2': _L0_ffn_in['b2'], 'L0_ffn_edge_index': _L0_ffn_in['edge_index']}

def reference(x, src, dst, edge_weight, L0_gnn_W, L0_gnn_b, L0_ffn_W_gat, L0_ffn_att_src, L0_ffn_att_dst, L0_ffn_b_gat, L0_ffn_ln_gamma, L0_ffn_ln_beta, L0_ffn_W1, L0_ffn_b1, L0_ffn_W2, L0_ffn_b2, L0_ffn_edge_index):
    import jax
    import jax.numpy as jnp

    def _L0_gnn_ref(feature, ew, src, dst, W, b):
        import jax, jax.numpy as jnp
        import numpy as np
        N_NODES, N_EDGES, F_IN, F_OUT = (1250, 40000, 256, 256)
        n = feature.shape[0]
        msg = feature[src[0]] * feature[src] * ew[:, None]
        sums = jax.ops.segment_sum(msg, dst, num_segments=n)
        cnt = jax.ops.segment_sum(jnp.ones((msg.shape[0],), msg.dtype), dst, num_segments=n)
        hm_mean = sums / jnp.maximum(cnt, 1.0)[:, None]
        x = jnp.concatenate([feature, hm_mean], axis=1)
        return jax.nn.relu(x @ W.T + b)

    def _L0_ffn_ref(x, W_gat, att_src, att_dst, b_gat, ln_gamma, ln_beta, W1, b1, W2, b2, edge_index):
        import jax, jax.numpy as jnp
        import numpy as np
        B, N, D = (16, 512, 256)
        NUM_EXPERTS, TOP_K, HEADS = (4, 2, 4)
        N_EDGES = 131072
        LN_EPS = 1e-05

        def _layernorm(x, g, b):
            mu = x.mean(-1, keepdims=True)
            var = ((x - mu) ** 2).mean(-1, keepdims=True)
            return (x - mu) * jax.lax.rsqrt(var + LN_EPS) * g + b

        def _forward(x, edge_index, W_gat, att_src, att_dst, b_gat, ln_gamma, ln_beta, W1, b1, W2, b2):
            Bc, Nc, Dc = x.shape
            M = Bc * Nc
            x_flat = x.reshape(M, Dc)
            h = (x_flat @ W_gat).reshape(M, HEADS, NUM_EXPERTS)
            loops = jnp.arange(M, dtype=edge_index.dtype)
            src = jnp.concatenate([edge_index[0], loops])
            dst = jnp.concatenate([edge_index[1], loops])
            a_src = (h * att_src).sum(-1)
            a_dst = (h * att_dst).sum(-1)
            e = jax.nn.leaky_relu(a_src[src] + a_dst[dst], negative_slope=0.2)
            e_max = jax.ops.segment_max(e, dst, num_segments=M)
            ee = jnp.exp(e - e_max[dst])
            denom = jax.ops.segment_sum(ee, dst, num_segments=M)
            alpha = ee / (denom[dst] + 1e-16)
            msg = h[src] * alpha[:, :, None]
            agg = jax.ops.segment_sum(msg, dst, num_segments=M).reshape(M, HEADS * NUM_EXPERTS) + b_gat
            scores = _layernorm(agg, ln_gamma, ln_beta).reshape(M, HEADS, NUM_EXPERTS).mean(1)
            scores = scores.reshape(Bc, Nc, NUM_EXPERTS)
            topk_s, topk_i = jax.lax.top_k(scores, TOP_K)
            w = jax.nn.softmax(topk_s, axis=-1)
            out = jnp.zeros_like(x)
            for ei in range(NUM_EXPERTS):
                g = jnp.where(topk_i == ei, w, 0.0).sum(-1)
                hh = jax.nn.gelu(x @ W1[ei] + b1[ei], approximate=False)
                out = out + g[..., None] * (hh @ W2[ei] + b2[ei])
            return out
        return _forward(x, edge_index, W_gat, att_src, att_dst, b_gat, ln_gamma, ln_beta, W1, b1, W2, b2)
    x = x + _L0_gnn_ref(_layernorm(x, axis=-1), edge_weight, src, dst, L0_gnn_W, L0_gnn_b)
    x = x + _L0_ffn_ref(_layernorm(x, axis=-1)[None], L0_ffn_W_gat, L0_ffn_att_src, L0_ffn_att_dst, L0_ffn_b_gat, L0_ffn_ln_gamma, L0_ffn_ln_beta, L0_ffn_W1, L0_ffn_b1, L0_ffn_W2, L0_ffn_b2, L0_ffn_edge_index)[0]
    return x

_drawn_inputs = setup_inputs


def setup_inputs(seed=0):
    import zlib

    import numpy as np

    out = dict(_drawn_inputs(seed))
    spreads = {'L0_ffn_b_gat': (0.0, 0.1),
     'L0_ffn_ln_gamma': (1.0, 0.2),
     'L0_ffn_ln_beta': (0.0, 0.1),
     'L0_ffn_b1': (0.0, 0.1),
     'L0_ffn_b2': (0.0, 0.1)}
    factors = {}
    for name, (base, spread) in spreads.items():
        noise = np.random.default_rng([zlib.crc32(name.encode()), seed]).standard_normal(out[name].shape)
        drawn = base * np.exp(spread * noise) if base else spread * noise
        out[name] = jnp.asarray(drawn.astype(out[name].dtype))
    for name, factor in factors.items():
        out[name] = (out[name] * factor).astype(out[name].dtype)
    return out
```

```python
from contextlib import ExitStack

import numpy as np

import concourse.bass as bass
from concourse import mybir

F32 = mybir.dt.float32
I32 = mybir.dt.int32
ALU = mybir.AluOpType
ACT = mybir.ActivationFunctionType
AX = mybir.AxisListType

P = 128
N = 6250
D = 256
T = -(-N // P)
NP = T * P
E1 = 200000
CH = -(-E1 // P)
GC = 4
BODY = 8
NG = -(-CH // (GC * BODY)) * BODY
EB = -(-CH // P)
CP = EB * P
GP = CP // GC
PAD_DST = 8191
E2 = 131072
L = E2 // P
LOG_L = L.bit_length() - 1
SHIFT = 13
KEY_BASE = 0x38000000
HE = 16
H = 4
X = 4
TW = HE + H
WX = HE + 2 * H
FF = 512
EPS = 1e-5
SLOTS = BODY * GC
SEEK = 10
ST = T + 1
NB = 2
GB = 16
NEG = -3.0e38
FB = 4
AW = D + 1


class Steps:

    def __init__(self, eng, sem, base=0):
        self.eng, self.sem, self.base, self.n = eng, sem, base, 0

    def then(self, ins):
        ins.then_inc(self.sem, 1)
        self.n += 1

    def wait(self):
        self.eng.wait_ge(self.sem, self.base + self.n)

    def __call__(self, ins):
        self.then(ins)
        self.wait()


class Mem:
    pass


def statistics(v, m, step, x):
    with v.Fori(0, T) as t:
        v.bn_stats(m.stats[:, bass.ds(t, 1), :].rearrange("p o s -> p (o s)"),
                   x[:, bass.ds(t, 1), 0:D].rearrange("p o d -> p (o d)")).then_inc(step.sem, 1)
    step.n += T
    step.wait()
    step.then(v.tensor_tensor(m.mean, m.stats[:, :, 1], m.stats[:, :, 4], ALU.add))
    step.then(v.tensor_tensor(m.tmp_s, m.stats[:, :, 1], m.stats[:, :, 4], ALU.subtract))
    step(v.tensor_tensor(m.var, m.stats[:, :, 2], m.stats[:, :, 5], ALU.add))
    step.then(v.tensor_scalar(m.mean, m.mean, 0.5, None, ALU.mult))
    step.then(v.tensor_scalar(m.var, m.var, 1.0 / D, EPS, ALU.mult, ALU.add))
    step(v.scalar_tensor_tensor(m.tmp_s, m.tmp_s, 0.25, m.tmp_s, ALU.mult, ALU.mult))
    step(v.tensor_tensor(m.var, m.var, m.tmp_s, ALU.add))


STATISTICS = T + 7


def inverse_root(v, m, step):
    step(v.reciprocal(m.rstd, m.rstd))
    step(v.tensor_tensor(m.tmp_s, m.rstd, m.rstd, ALU.mult))
    step(v.tensor_tensor(m.tmp_s, m.tmp_s, m.var, ALU.mult))
    step(v.tensor_scalar(m.tmp_s, m.tmp_s, -0.5, 1.5, ALU.mult, ALU.add))
    step(v.tensor_tensor(m.rstd, m.rstd, m.tmp_s, ALU.mult))


INVERSE_ROOT = 5
DVE_VAR = 10 + STATISTICS
DVE_FEAT = DVE_VAR + INVERSE_ROOT + T


def allocate(nc, ctx, m):
    def sb(name, shape, dt=F32):
        return ctx.enter_context(nc.sbuf_tensor(name, shape, dt))

    m.big = sb("big", [P, T * D + T * AW])
    m.mid = sb("mid", [P, ST * D])
    m.edge = sb("edge", [P, 3 * CP])
    m.skey = sb("skey", [P, L])
    m.ssrc = sb("ssrc", [P, L], I32)
    m.wgnn = sb("wgnn", [P, 4, D])
    m.b2 = sb("b2", [1, X * D])
    m.ident = sb("ident", [P, P])
    m.iota = sb("iota", [P, P])
    m.iota_x = sb("iota_x", [P, P])
    m.signs = sb("signs", [P, 8])
    m.nodekey = sb("nodekey", [P, ST])
    m.small = sb("small", [P, 24 * 64])
    m.regs = sb("regs", [1, 2, GP], I32)
    m.idx = sb("idx", [P, 2, 16], I32)
    m.work = sb("work", [P, 3072])
    m.psum = ctx.enter_context(nc.psum_tensor("ps", [P, 8, 512], F32))

    m.feat = m.big[:, 0:T * D].rearrange("p (t d) -> p t d", t=T)
    m.acc = m.big[:, T * D:].rearrange("p (t d) -> p t d", t=T)
    m.acc_flat = m.big[:, T * D:]
    m.esrc = m.edge[:, 0:CP].bitcast(I32)
    m.edst = m.edge[:, CP:2 * CP]
    m.ewt = m.edge[:, 2 * CP:3 * CP]
    m.key = [m.mid[:, 10496 + k * L:10496 + (k + 1) * L] for k in range(2)]

    def small(k, n=ST):
        return m.small[:, 64 * k:64 * k + n]

    m.mean, m.var, m.rstd, m.tmp_s = small(0, T), small(1, T), small(2, T), small(15, T)
    m.start, m.end, m.some, m.row, m.cnt = small(3), small(4, T), small(5, T), small(8), small(9)
    m.start_i, m.end_i = small(6, T).bitcast(I32), small(7, T).bitcast(I32)
    m.stats = m.small[:, 640:640 + 6 * T].rearrange("p (t s) -> p t s", s=6)
    m.prev = m.small[:, 64 * 16:64 * 16 + 4]
    m.rows = m.mid[:, 0:SLOTS * D].rearrange("p (s d) -> p s d", s=SLOTS)
    m.wrows = m.mid[:, SLOTS * D:SLOTS * D + 2 * GC * AW].rearrange("p (b c d) -> p b c d", b=2, c=GC)
    m.hot = m.work[:, 0:3 * GC * P].rearrange("p (b c n) -> p b c n", b=3, c=GC)
    m.seek = m.mid[:, 0:SEEK * L].rearrange("p (s d) -> p s d", s=SEEK)
    m.t0b = m.mid[:, 0:GP]


def load_and_normalise(nc, ctx, m, a):
    def sem(name):
        return ctx.enter_context(nc.semaphore(name))

    x_in, e_in, c_in, w_in = sem("x_in"), sem("e_in"), sem("c_in"), sem("w_in")
    pads, dve, sq, chunk_t, chunk_c = sem("pads"), sem("a_dve"), sem("a_sqrt"), sem("chunk_t"), sem("chunk_c")
    edge_f, feat_out, rng_ready, rng_out, rng_in = (sem("edge_f"), sem("feat_out"), sem("rng_ready"),
                                                   sem("rng_out"), sem("rng_in"))
    w_t, w_c = sem("w_t"), sem("w_c")
    full, rest = E1 // P, E1 % P
    whole, tail = EB - 1, full - (EB - 1) * P
    raw = [m.mid[:, k * CP:(k + 1) * CP] for k in range(3)]
    src_raw, dst_raw = raw[0].bitcast(I32), raw[1].bitcast(I32)
    src_f, dst_f, tmp = (m.mid[:, k * CP:(k + 1) * CP] for k in (3, 4, 5))
    wraw = m.skey[:, 0:1024].rearrange("p (a k) -> p a k", a=2)
    cmin, cmax = m.small[:, 64 * 20:64 * 20 + EB], m.small[:, 64 * 20 + EB:64 * 20 + 2 * EB]
    gi = m.small[0:EB, 64 * 21:64 * 21 + 64].bitcast(I32)
    gf = m.small[0:EB, 64 * 22:64 * 22 + 64]
    gb = m.small[0:EB, 64 * 23:64 * 23 + 32]

    with nc.Block() as block:
        @block.sync
        def _(sp):
            sp.wait_ge(pads, 4)
            xt = a["x"][0:(T - 1) * P, :].rearrange("(t p) d -> p t d", p=P)
            sp.dma_start(m.feat[:, 0:T - 1, :], xt).then_inc(x_in, 16)
            sp.dma_start(m.feat[0:N - (T - 1) * P, T - 1, :], a["x"][(T - 1) * P:N, :]).then_inc(x_in, 16)
            for r, name in ((src_raw, "src"), (dst_raw, "dst"), (raw[2], "edge_weight")):
                v = r.rearrange("p (b e) -> p b e", b=EB)
                s = a[name]
                sp.dma_start(v[:, 0:whole, :], s[0:whole * P * P].rearrange("(b p e) -> p b e", b=whole, p=P))\
                    .then_inc(e_in, 16)
                sp.dma_start(v[0:tail, whole, :], s[whole * P * P:full * P].rearrange("(p e) -> p e", e=P))\
                    .then_inc(e_in, 16)
                sp.dma_start(v[tail:tail + 1, whole, 0:rest], s[full * P:E1].rearrange("(p e) -> p e", p=1))\
                    .then_inc(e_in, 16)
            sp.wait_ge(rng_ready, 1)
            sp.dma_start(a["rng_i"].rearrange("k (b g) -> b k g", b=EB), gi.rearrange("b (k g) -> b k g", k=2))\
                .then_inc(rng_out, 16)
            sp.dma_start(a["rng_f"].rearrange("(b g) -> b g", b=EB), gb).then_inc(rng_out, 16)
            sp.wait_ge(rng_out, 32)
            sp.dma_start(m.regs[0:1, :, :], a["rng_i"].rearrange("(o k) g -> o k g", o=1)).then_inc(rng_in, 16)
            sp.dma_start(m.t0b, a["rng_f"].partition_broadcast(P)).then_inc(rng_in, 16)
            sp.wait_ge(dve, 0 + DVE_FEAT)
            sp.dma_start(a["feat"].rearrange("(t p) d -> p t d", p=P), m.feat).then_inc(feat_out, 16)
            sp.wait_ge(feat_out, 16)

        @block.scalar
        def _(act):
            for dst, name in ((m.ident, "c_ident"), (m.iota, "c_iota"), (m.signs, "c_signs"),
                              (m.nodekey, "c_nodekey")):
                act.dma_start(dst[:, :], a[name]).then_inc(c_in, 16)
            act.dma_start(wraw, a["L0_gnn_W"].rearrange("(a o) k -> o a k", a=2)).then_inc(w_in, 16)
            act.wait_ge(dve, DVE_VAR)
            act.activation(m.rstd, m.var, ACT.Sqrt).then_inc(sq, 1)
            act.wait_ge(w_t, 1)
            for b in range(2):
                act.activation(m.wgnn[:, 2 * b:2 * b + 2, :].rearrange("p k o -> p (k o)"), m.psum[:, b, :],
                               ACT.Copy).then_inc(w_c, 1)
            for b in range(EB):
                act.wait_ge(chunk_t, b + 1)
                for k, dst in enumerate((m.esrc, m.edst, m.ewt)):
                    act.activation(dst[:, b * P:(b + 1) * P], m.psum[:, 4 + b % 4, k * P:(k + 1) * P], ACT.Copy)\
                       .then_inc(chunk_c, 1)

        @block.tensor
        def _(pe):
            pe.wait_ge(c_in, 64)
            pe.wait_ge(w_in, 16)
            for k in range(4):
                for o in range(2):
                    last = pe.transpose(m.psum[:, k // 2, (k % 2) * D + o * P:(k % 2) * D + (o + 1) * P],
                                        wraw[:, o, k * P:(k + 1) * P], m.ident[:, :])
            last.then_inc(w_t, 1)
            pe.wait_ge(edge_f, 2)
            pe.wait_ge(dve, 3)
            pe.transpose(m.psum[0:EB, 3, 0:P], cmin, m.ident[:, :])
            pe.transpose(m.psum[0:EB, 3, P:2 * P], cmax, m.ident[:, :]).then_inc(w_t, 1)
            pe.wait_ge(e_in, 9 * 16)
            for b in range(EB):
                if b >= 4:
                    pe.wait_ge(chunk_c, (b - 3) * 3)
                for k, s in enumerate((src_f, dst_f, raw[2])):
                    last = pe.transpose(m.psum[:, 4 + b % 4, k * P:(k + 1) * P], s[:, b * P:(b + 1) * P],
                                        m.ident[:, :])
                last.then_inc(chunk_t, 1)

        @block.vector
        def _(v):
            v.memset(m.feat[:, T - 1, :], 0.0).then_inc(pads, 1)
            v.memset(src_raw[:, whole * P:], 0).then_inc(pads, 1)
            v.memset(dst_raw[:, whole * P:], PAD_DST).then_inc(pads, 1)
            v.memset(raw[2][:, whole * P:], 0.0).then_inc(pads, 1)
            step = Steps(v, dve)
            v.wait_ge(e_in, 9 * 16)
            v.tensor_copy(src_f, src_raw).then_inc(edge_f, 1)
            step(v.tensor_copy(dst_f, dst_raw))
            step.then(v.tensor_reduce(cmin, dst_f.rearrange("p (b e) -> p b e", b=EB), AX.X, ALU.min))
            step(v.scalar_tensor_tensor(tmp, dst_f, float(NP), dst_f, ALU.is_lt, ALU.mult))
            v.tensor_reduce(cmax, tmp.rearrange("p (b e) -> p b e", b=EB), AX.X, ALU.max).then_inc(edge_f, 1)
            v.wait_ge(w_t, 2)
            for k in range(2):
                step.then(v.tensor_reduce(gf[:, 32 * k:32 * k + 32],
                                          m.psum[0:EB, 3, k * P:(k + 1) * P].rearrange("b (g c) -> b g c", c=GC),
                                          AX.X, (ALU.min, ALU.max)[k]))
            step.wait()
            step(v.tensor_copy(gi, gf))
            step(v.tensor_scalar(gi, gi, 7, None, ALU.arith_shift_right))
            step(v.tensor_scalar(gi, gi, T - 1, None, ALU.min))
            step(v.tensor_tensor(gi[:, 32:64], gi[:, 32:64], gi[:, 0:32], ALU.max))
            step(v.tensor_tensor(gi[:, 32:64], gi[:, 32:64], gi[:, 0:32], ALU.subtract))
            v.tensor_scalar(gb, gi[:, 0:32], float(P), None, ALU.mult).then_inc(rng_ready, 1)
            v.wait_ge(x_in, 32)
            statistics(v, m, step, m.feat)
            assert step.n == DVE_VAR
            v.wait_ge(sq, 1)
            inverse_root(v, m, step)
            with v.Fori(0, T) as t:
                v.tensor_scalar(m.feat[:, bass.ds(t, 1), :].rearrange("p o d -> p (o d)"),
                                m.feat[:, bass.ds(t, 1), :].rearrange("p o d -> p (o d)"),
                                m.mean[:, bass.ds(t, 1)], m.rstd[:, bass.ds(t, 1)],
                                ALU.subtract, ALU.mult).then_inc(dve, 1)
            step.n += T
            assert step.n == DVE_FEAT
            v.wait_ge(chunk_c, 3 * EB)
            v.wait_ge(rng_in, 32)
            step(v.tensor_tensor(m.edst.rearrange("p (g c) -> p g c", c=GC),
                                 m.edst.rearrange("p (g c) -> p g c", c=GC),
                                 m.t0b.unsqueeze(2).to_broadcast([P, GP, GC]), ALU.subtract))




BURSTS = [(1, 2, 3, 4, 5), (6, 7), (8, 9), (10,)] + [(k,) for k in range(LOG_L + 1, LOG_L + 8)]
PARTS = [4] * len(BURSTS)
PARTS.append(NG // BODY - sum(PARTS))


def gather_and_sort(nc, ctx, m, a):
    def sem(name):
        return ctx.enter_context(nc.semaphore(name))

    idx_ready, weighted, hot_ready, sums_ready = sem("idx_ready"), sem("weighted"), sem("hot_ready"), sem("sums_ready")
    group_done, hot_x, sums_x = sem("group_done"), sem("hot_x"), sem("sums_x")
    row_in = [sem(f"row_in{k}") for k in range(SLOTS)]
    sorting, turned, turned_c, e2_in, start_sem = (sem("sorting"), sem("turned"), sem("turned_c"), sem("e2_in"),
                                                   sem("b_setup"))
    key_out, prev_in, seek_idx, start_t, start_out, end_in = (sem("key_out"), sem("prev_in"), sem("seek_idx"),
                                                              sem("start_t"), sem("start_out"), sem("end_in"))
    seek_in = [sem(f"seek_in{k}") for k in range(SEEK)]
    xstep = sem("xstep")
    iters = NG // BODY

    def parts():
        at = 1
        for n in PARTS:
            yield at, min(at + n, iters)
            at += n

    with nc.Block() as block:
        @block.gpsimd
        def _(pool):
            def body(it, first):
                for k in range(SLOTS):
                    if k % 16 == 0:
                        pool.wait_ge(idx_ready, it * 2 + k // 16 + 1)
                    if not first:
                        pool.wait_ge(weighted, used)
                        pool.reg_add(used, used, 1)
                    pool.indirect_dma_start(m.rows[:, k, :], None, a["feat"],
                                            bass.IndirectOffsetOnAxis(ap=m.idx[:, k // 16, k % 16:k % 16 + 1], axis=0))\
                        .then_inc(row_in[k], 16)
            used = pool.alloc_register("used")
            pool.reg_mov(used, 1)
            body(0, True)
            with pool.Fori(1, iters) as it:
                body(it, False)
            staged = pool.alloc_register("staged")
            pool.reg_mov(staged, 1)
            with pool.Fori(0, ST // SEEK) as it:
                pool.wait_ge(seek_idx, staged)
                pool.reg_add(staged, staged, 1)
                for k in range(SEEK):
                    pool.indirect_dma_start(m.seek[:, k, :], None, a["keys"].rearrange("(r l) -> r l", l=L),
                                            bass.IndirectOffsetOnAxis(ap=m.idx[:, 0, k:k + 1], axis=0))\
                        .then_inc(seek_in[k], 16)

        @block.scalar
        def _(act):
            for h in range(2):
                act.activation(m.idx[:, h, :], m.esrc[:, 16 * h:16 * h + 16], ACT.Copy).then_inc(idx_ready, 1)
            act.wait_ge(start_sem, 2)

            def body(it, first):
                for k in range(SLOTS):
                    g = k // GC
                    if k % GC == 0 and not (first and g < 2):
                        act.wait_ge(group_done, it * BODY + (g - 1))
                    act.wait_ge(row_in[k], it * 16 + 16)
                    act.activation(m.wrows[:, g % 2, k % GC, 0:D], m.rows[:, k, :], ACT.Copy,
                                   scale=m.ewt[:, bass.ds(it * SLOTS + k, 1)]).then_inc(weighted, 1)
                    if k % 16 == 15:
                        act.activation(m.idx[:, k // 16, :], m.esrc[:, bass.ds(it * SLOTS + (SLOTS + k - 15), 16)],
                                       ACT.Copy).then_inc(idx_ready, 1)
            body(0, True)
            turn = 0
            for (lo, hi), burst in zip(parts(), BURSTS + [()]):
                with act.Fori(lo, hi) as it:
                    body(it, False)
                for k in burst:
                    if k > LOG_L:
                        for _ in range(2):
                            act.wait_ge(turned, turn + 1)
                            cur = TURNS[turn][0]
                            act.activation(m.key[1 - cur], m.psum[:, 4:6, :].rearrange("p b n -> p (b n)"), ACT.Copy)\
                               .then_inc(turned_c, 1)
                            turn += 1

        @block.tensor
        def _(pe):
            extra = pe.alloc_register("extra_pe")
            pe.reg_mov(extra, 0)

            def sums(out, hot, buf):
                for c in range(GC):
                    last = pe.matmul(out, m.hot[:, hot, c, :], m.wrows[:, buf, c, :], start=(c == 0), stop=(c == GC - 1))
                return last

            def body(it, first):
                for g in range(BODY):
                    pe.wait_ge(weighted, it * SLOTS + (g + 1) * GC)
                    pe.wait_ge(hot_ready, it * BODY + (g + 1))
                    if not (first and g < 2):
                        pe.wait_ge(group_done, it * BODY + (g - 1))
                    sums(m.psum[:, g % 2, 0:AW], g % 2, g % 2).then_inc(sums_ready, 1)
                    more = pe.value_load(m.regs[0:1, 1, bass.ds(it * BODY + g, 1)], min_val=0, max_val=T - 1)
                    with pe.If(more > 0):
                        with pe.Fori(0, more):
                            pe.reg_add(extra, extra, 1)
                            pe.wait_ge(hot_x, pe.snap(extra))
                            sums(m.psum[:, 2, 0:AW], 2, g % 2).then_inc(sums_x, 1)
            body(0, True)
            turn = 0
            for (lo, hi), burst in zip(parts(), BURSTS + [()]):
                with pe.Fori(lo, hi) as it:
                    body(it, False)
                for k in burst:
                    if k > LOG_L:
                        for _ in range(2):
                            cur, n = TURNS[turn]
                            pe.wait_ge(sorting, n)
                            if turn:
                                pe.wait_ge(turned_c, turn)
                            for b in range(L // P):
                                last = pe.transpose(m.psum[:, 4 + b // 4, (b % 4) * P:(b % 4 + 1) * P],
                                                    m.key[cur][:, b * P:(b + 1) * P], m.ident[:, :])
                            last.then_inc(turned, 1)
                            turn += 1
            pe.wait_ge(start_t, 1)
            pe.transpose(m.psum[:, 3, 0:P], m.hot[:, 0, 0, :], m.ident[:, :]).then_inc(turned, 1)
            pe.wait_ge(start_t, 2)
            pe.transpose(m.psum[0:ST, 3, P:2 * P], m.start, m.ident[:, :]).then_inc(turned, 1)
            pe.wait_ge(end_in, 16)
            pe.transpose(m.psum[:, 3, 2 * P:2 * P + T], m.hot[0:T, 0, 2, :], m.ident[0:T, 0:T]).then_inc(turned, 1)

        @block.sync
        def _(sp):
            for k, dst in enumerate((m.skey[:, :].bitcast(I32), m.ssrc[:, :])):
                sp.dma_start(dst, a["L0_ffn_edge_index"][k, :].rearrange("(p l) -> p l", l=L)).then_inc(e2_in, 16)
            cur, n = TURNS[-1]
            sp.wait_ge(sorting, n)
            keys = a["keys"].rearrange("(r l) -> r l", l=L)
            sp.dma_start(keys, m.key[cur]).then_inc(key_out, 16)
            sp.wait_ge(key_out, 16)
            sp.dma_start(m.prev[1:P, 0:1], keys[0:P - 1, L - 1:L],
                         allow_slow_non_contiguous=True).then_inc(prev_in, 16)
            sp.wait_ge(start_t, 3)
            sp.dma_start(a["starts"].rearrange("(t p) -> t p", p=P), m.hot[0:ST, 0, 1, :]).then_inc(start_out, 16)
            sp.wait_ge(start_out, 16)
            sp.dma_start(m.hot[0:T, 0, 2, :], a["starts"][1:NP + 1].rearrange("(t p) -> t p", p=P)).then_inc(end_in, 16)

        @block.vector
        def _(v):
            step = Steps(v, sorting)
            extra, xs = v.alloc_register("extra_dve"), v.alloc_register("xs_dve")
            v.reg_mov(extra, 0)
            v.reg_mov(xs, 1)
            further = v.alloc_register("further")
            v.memset(m.acc_flat, 0.0).then_inc(start_sem, 1)
            v.memset(m.wrows[:, :, :, D:AW], 1.0).then_inc(start_sem, 1)
            v.wait_ge(start_sem, 2)

            def hot(g, buf, iota):
                return v.tensor_tensor(m.hot[:, buf, :, :], iota.unsqueeze(1).to_broadcast([P, GC, P]),
                                       m.edst[:, bass.ds(g * GC, GC)].unsqueeze(2).to_broadcast([P, GC, P]),
                                       ALU.is_equal)

            def add(tile, bank):
                out = m.acc[:, bass.ds(tile, 1), :].rearrange("p o d -> p (o d)")
                return v.tensor_tensor(out, out, m.psum[:, bank, 0:AW], ALU.add)

            hot(0, 0, m.iota[:, :]).then_inc(hot_ready, 1)

            def body(it, first):
                for g in range(BODY):
                    hot(it * BODY + (g + 1), (g + 1) % 2, m.iota[:, :]).then_inc(hot_ready, 1)
                    v.wait_ge(sums_ready, it * BODY + (g + 1))
                    if not (first and g == 0):
                        v.wait_ge(group_done, it * BODY + g)
                    tile = v.value_load(m.regs[0:1, 0, bass.ds(it * BODY + g, 1)], min_val=0, max_val=T - 1)
                    more = v.value_load(m.regs[0:1, 1, bass.ds(it * BODY + g, 1)], min_val=0, max_val=T - 1)
                    with v.If(more > 0):
                        v.reg_mov(further, tile)
                        v.tensor_scalar(m.iota_x[:, :], m.iota[:, :], float(P), None, ALU.add).then_inc(xstep, 1)
                        v.wait_ge(xstep, v.snap(xs))
                        v.reg_add(xs, xs, 1)
                        with v.Fori(0, more):
                            hot(it * BODY + g, 2, m.iota_x[:, :]).then_inc(hot_x, 1)
                            v.reg_add(extra, extra, 1)
                            v.wait_ge(sums_x, v.snap(extra))
                            v.reg_add(further, further, 1)
                            add(v.snap(further, min_val=0, max_val=T - 1), 2).then_inc(xstep, 1)
                            v.tensor_scalar(m.iota_x[:, :], m.iota_x[:, :], float(P), None, ALU.add)\
                             .then_inc(xstep, 1)
                            v.reg_add(xs, xs, 1)
                            v.wait_ge(xstep, v.snap(xs))
                            v.reg_add(xs, xs, 1)
                    add(tile, g % 2).then_inc(group_done, 1)

            cur = 0

            def merge(src, dist, mirror=False):
                nonlocal cur
                s, d = (k.rearrange("p (n two h) -> p n two h", two=2, h=dist) for k in (src, m.key[1 - cur]))
                turn = slice(None, None, -1) if mirror else slice(None)
                step.then(v.tensor_tensor(d[:, :, 0, :], s[:, :, 0, :], s[:, :, 1, turn], ALU.min))
                step(v.tensor_tensor(d[:, :, 1, :], s[:, :, 1, :], s[:, :, 0, turn], ALU.max))
                cur = 1 - cur

            def sign(k):
                nonlocal cur
                step(v.tensor_scalar(m.key[1 - cur], m.key[cur], m.signs[:, k:k + 1], None, ALU.mult))
                cur = 1 - cur

            def turn():
                nonlocal cur, turns
                assert TURNS[turns] == (cur, step.n)
                turns += 1
                v.wait_ge(turned_c, turns)
                cur = 1 - cur

            src, key_i = m.skey[:, :].bitcast(I32), m.key[0].bitcast(I32)
            v.wait_ge(e2_in, 32)
            step.then(v.tensor_scalar(src, src, N - 1, None, ALU.min))
            step(v.tensor_scalar(m.ssrc[:, :], m.ssrc[:, :], N, None, ALU.min))
            step(v.tensor_scalar(m.ssrc[:, :], m.ssrc[:, :], SHIFT, KEY_BASE, ALU.logical_shift_left, ALU.bitwise_or))
            step(v.tensor_tensor(key_i, m.ssrc[:, :], src, ALU.bitwise_or))
            sign(0)
            turns = 0
            body(0, True)
            for (lo, hi), burst in zip(parts(), BURSTS + [()]):
                with v.Fori(lo, hi) as it:
                    body(it, False)
                for k in burst:
                    if k <= LOG_L:
                        merge(m.key[cur], 1 << (k - 1), mirror=True)
                        for j in range(k - 2, -1, -1):
                            merge(m.key[cur], 1 << j)
                    else:
                        sign(k - LOG_L)
                        turn()
                        for j in range(k - LOG_L - 1, -1, -1):
                            merge(m.key[cur], 1 << j)
                        turn()
                        for j in range(LOG_L - 1, -1, -1):
                            merge(m.key[cur], 1 << j)
            assert TURNS[turns] == (cur, step.n)
            v.wait_ge(group_done, NG)

            key, run = m.key[cur], m.key[1 - cur].bitcast(I32)
            prev = m.prev.bitcast(I32)
            v.wait_ge(prev_in, 16)
            step.then(v.tensor_scalar(m.ssrc[:, :], key.bitcast(I32), (1 << SHIFT) - 1, None, ALU.bitwise_and))
            step.then(v.tensor_scalar(run, key.bitcast(I32), SHIFT, None, ALU.logical_shift_right))
            step.then(v.memset(m.prev[0:1, 0:1], 0.0))
            step(v.tensor_copy(m.hot[:, 0, 0, :], key[:, 0:1].to_broadcast([P, P])))
            v.memset(m.prev[:, 2:3], 0.0).then_inc(start_t, 1)
            step(v.tensor_scalar(prev[:, 1:2], prev[:, 0:1], SHIFT, None, ALU.logical_shift_right))
            step.then(v.tensor_tensor(m.skey[:, 1:L], run[:, 1:L], run[:, 0:L - 1], ALU.is_equal))
            step(v.tensor_tensor(m.skey[:, 0:1], run[:, 0:1], prev[:, 1:2], ALU.is_equal))
            below = m.mid[:, 0:ST * P].rearrange("p (t r) -> p t r", t=ST)
            v.wait_ge(turned, len(TURNS))
            step(v.tensor_tensor(below, m.psum[:, 3, 0:P].unsqueeze(1).to_broadcast([P, ST, P]),
                                 m.nodekey[:, :].unsqueeze(2).to_broadcast([P, ST, P]), ALU.is_lt))
            step(v.tensor_reduce(m.row, below, AX.X, ALU.add))
            step(v.tensor_scalar(m.row, m.row, -1.0, 0.0, ALU.add, ALU.max))
            seek_base = step.n
            with v.Fori(0, ST // SEEK) as it:
                s = Steps(v, sorting, seek_base + it * (SEEK + 1))
                v.tensor_copy(m.idx[:, 0, 0:SEEK], m.row[:, bass.ds(it * SEEK, SEEK)]).then_inc(seek_idx, 1)
                for k in range(SEEK):
                    v.wait_ge(seek_in[k], it * 16 + 16)
                    s.then(v.tensor_scalar(m.seek[:, k, :], m.seek[:, k, :], m.nodekey[:, bass.ds(it * SEEK + k, 1)],
                                           None, ALU.is_lt))
                s.wait()
                s(v.tensor_reduce(m.cnt[:, bass.ds(it * SEEK, SEEK)], m.seek, AX.X, ALU.add))
            step.n += ST // SEEK * (SEEK + 1)
            v.scalar_tensor_tensor(m.start, m.row, float(L), m.cnt, ALU.mult, ALU.add).then_inc(start_t, 1)
            v.wait_ge(turned, len(TURNS) + 1)
            v.tensor_copy(m.hot[0:ST, 0, 1, :], m.psum[0:ST, 3, P:2 * P]).then_inc(start_t, 1)
            v.wait_ge(turned, len(TURNS) + 2)
            step(v.tensor_copy(m.end, m.psum[:, 3, 2 * P:2 * P + T]))
            step(v.tensor_tensor(m.some, m.end, m.start[:, 0:T], ALU.is_gt))
            step(v.scalar_tensor_tensor(m.tmp_s, m.start[:, 0:T], float(-BEYOND), m.some, ALU.add, ALU.mult))
            step.then(v.tensor_scalar(m.start_i, m.tmp_s, float(BEYOND), None, ALU.add))
            step(v.tensor_scalar(m.end_i, m.end, -1.0, 0.0, ALU.add, ALU.max))


def turn_plan():
    cur, n, out = 1, 5, []
    for k in range(1, LOG_L + 1):
        cur, n = (cur + k) % 2, n + 2 * k
    for k in range(1, 8):
        cur, n = 1 - cur, n + 1
        out.append((cur, n))
        cur, n = (cur + 1 + k) % 2, n + 2 * k
        out.append((cur, n))
        cur, n = (cur + 1 + LOG_L) % 2, n + 2 * LOG_L
    return out + [(cur, n)]


TURNS = turn_plan()
BEYOND = 1 << 20


def first_layer(nc, ctx, m, a):
    def sem(name):
        return ctx.enter_context(nc.semaphore(name))

    x_in, c_in, f0_i, f0_in = sem("c_x_in"), sem("c_const"), sem("f0_i"), sem("f0_in")
    dve, sq, pad = sem("c_dve"), sem("c_sqrt"), sem("c_pad")
    feat_c, mean_c, turned, turned_c, lin, lin_read = (sem("feat_c"), sem("mean_c"), sem("c_turned"), sem("c_turned_c"),
                                                       sem("lin"), sem("lin_read"))
    normed, turned2, turned2_c, kept2, proj, proj_read = (sem("normed"), sem("turned2"), sem("turned2_c"), sem("kept2"),
                                                          sem("proj"), sem("proj_read"))
    stored, w_ready = sem("c_stored"), sem("w_ready")
    xt = m.work[:, 0:1024].rearrange("p (b k n) -> p b k n", b=2, k=4)
    f0, bias = m.work[:, 1024:1280], m.work[:, 1280:1536]
    wext = m.work[:, 1536:1584].rearrange("p (k c) -> p k c", k=2)
    att = m.work[:, 1584:1616]
    prod = m.work[:, 1616:1680].rearrange("p (s k c) -> p s k c", s=2, k=2)
    z = m.work[:, 1680:2192].rearrange("p (b d) -> p b d", b=2)
    zin = m.edge[:, 2048:3072].rearrange("p (b d) -> p b d", b=2)
    proj_sb = m.edge[:, 0:T * WX].rearrange("p (t c) -> p t c", t=T)
    x = m.mid[:, 0:T * D].rearrange("p (t d) -> p t d", t=T)
    x2 = m.acc[:, :, 0:D]
    xnt = m.mid[:, :].rearrange("p (k n) -> p k n", k=2)
    pairs = (T - 1) // 2

    def one(ap, t):
        return ap[:, bass.ds(t, 1), 0:D].rearrange("p o d -> p (o d)")

    def pipeline(eng, stage1, stage2):
        stage1(0, 0, True)
        for t in range(2):
            stage1(t + 1, (t + 1) % 2, t == 0)
            stage2(t, t, True)
        with eng.Fori(1, pairs) as i:
            for t in range(2):
                stage1(i * 2 + (t + 1), (t + 1) % 2, False)
                stage2(i * 2 + t, t, False)
        stage2(T - 1, 0, False)

    with nc.Block() as block:
        @block.sync
        def _(sp):
            sp.dma_start(m.idx[:, 0, 0:1], a["src"][0:1].partition_broadcast(P)).then_inc(f0_i, 16)
            sp.dma_start(x[:, 0:T - 1, :], a["x"][0:(T - 1) * P, :].rearrange("(t p) d -> p t d", p=P)).then_inc(x_in, 16)
            sp.wait_ge(pad, 1)
            sp.dma_start(x[0:N - (T - 1) * P, T - 1, :], a["x"][(T - 1) * P:N, :]).then_inc(x_in, 16)
            sp.wait_ge(dve, C_X2)
            sp.dma_start(a["x2"].rearrange("(t p) d -> p t d", p=P), x2).then_inc(stored, 16)
            sp.wait_ge(proj_read, T)
            sp.dma_start(a["table"].rearrange("(t p) c -> p t c", p=P), proj_sb).then_inc(stored, 16)
            sp.wait_ge(stored, 32)

        @block.gpsimd
        def _(pool):
            pool.wait_ge(f0_i, 16)
            pool.indirect_dma_start(f0, None, a["feat"], bass.IndirectOffsetOnAxis(ap=m.idx[:, 0, 0:1], axis=0))\
                .then_inc(f0_in, 16)

        @block.scalar
        def _(act):
            act.dma_start(bias, a["L0_gnn_b"].partition_broadcast(P)).then_inc(c_in, 16)
            act.dma_start(wext[:, :, 0:HE], a["L0_ffn_W_gat"].rearrange("(k p) c -> p k c", p=P)).then_inc(c_in, 16)
            for k, name in enumerate(("L0_ffn_att_src", "L0_ffn_att_dst")):
                act.dma_start(att[:, HE * k:HE * k + HE], a[name].rearrange("h e -> (h e)").partition_broadcast(P))\
                   .then_inc(c_in, 16)

            def feature(t, b, first):
                if not (first and b == 0 and isinstance(t, int) and t == 0):
                    act.wait_ge(turned, t - 1)
                act.activation(zin[:, b, 0:D], one(m.feat, t), ACT.Copy).then_inc(feat_c, 1)

            def turned_copy(t, b, first):
                act.wait_ge(turned, t + 1)
                if not first:
                    act.wait_ge(lin, t - 1)
                act.activation(xt[:, b, :, :].rearrange("p k n -> p (k n)"), m.psum[:, b, :], ACT.Copy).then_inc(turned_c, 1)

            pipeline(act, feature, turned_copy)
            act.wait_ge(dve, C_VAR)
            act.activation(m.rstd, m.var, ACT.Sqrt).then_inc(sq, 1)

            def nothing(t, b, first):
                pass

            def copies(t, b, first):
                act.wait_ge(turned2, t + 1)
                if not first:
                    act.wait_ge(proj, t - 1)
                act.activation(xt[:, b, 0:2, :].rearrange("p k n -> p (k n)"), m.psum[:, 4 + b, 0:D], ACT.Copy)\
                   .then_inc(turned2_c, 1)
                act.activation(xnt[:, :, bass.ds(t * P, P)], m.psum[:, 4 + b, 0:D].rearrange("p (k n) -> p k n", k=2),
                               ACT.Copy).then_inc(kept2, 1)

            pipeline(act, nothing, copies)

        @block.tensor
        def _(pe):
            def turn(t, b, first):
                pe.wait_ge(feat_c, t + 1)
                pe.wait_ge(mean_c, t + 1)
                if not (first and isinstance(t, int) and t == 0):
                    pe.wait_ge(turned_c, t - 1)
                for k in range(4):
                    last = pe.transpose(m.psum[:, b, k * P:(k + 1) * P], zin[:, b, k * P:(k + 1) * P], m.ident[:, :])
                last.then_inc(turned, 1)

            def linear(t, b, first):
                pe.wait_ge(turned_c, t + 1)
                if not first:
                    pe.wait_ge(lin_read, t - 1)
                for k in range(4):
                    last = pe.matmul(m.psum[:, 2 + b, 0:D], xt[:, b, k, :], m.wgnn[:, k, :], start=(k == 0), stop=(k == 3))
                last.then_inc(lin, 1)

            pipeline(pe, turn, linear)
            pe.wait_ge(w_ready, 1)

            def turn2(t, b, first):
                pe.wait_ge(normed, t + 1)
                if not (first and isinstance(t, int) and t == 0):
                    pe.wait_ge(kept2, t - 1)
                for k in range(2):
                    last = pe.transpose(m.psum[:, 4 + b, k * P:(k + 1) * P], zin[:, b, k * P:(k + 1) * P], m.ident[:, :])
                last.then_inc(turned2, 1)

            def project(t, b, first):
                pe.wait_ge(turned2_c, t + 1)
                if not first:
                    pe.wait_ge(proj_read, t - 1)
                for k in range(2):
                    last = pe.matmul(m.psum[:, 6 + b, 0:WX], xt[:, b, k, :], wext[:, k, :], start=(k == 0), stop=(k == 1))
                last.then_inc(proj, 1)

            pipeline(pe, turn2, project)

        @block.vector
        def _(v):
            step = Steps(v, dve)
            v.memset(x[:, T - 1, :], 0.0).then_inc(pad, 1)
            v.wait_ge(c_in, 64)
            for s in range(2):
                step.then(v.tensor_tensor(prod[:, s, :, :], wext[:, :, 0:HE],
                                          att[:, HE * s:HE * s + HE].unsqueeze(1).to_broadcast([P, 2, HE]), ALU.mult))
            step.wait()
            for s in range(2):
                for k in range(2):
                    step.then(v.tensor_reduce(wext[:, k, HE + H * s:HE + H * s + H],
                                              prod[:, s, k, :].rearrange("p (h e) -> p h e", e=X), AX.X, ALU.add))
            step.wait()
            step(v.tensor_scalar(m.tmp_s, m.acc[:, :, D], 1.0, None, ALU.max))
            step(v.reciprocal(m.cnt[:, 0:T], m.tmp_s))
            v.memset(m.prev[:, 3:4], 0.0).then_inc(w_ready, 1)
            v.wait_ge(f0_in, 16)
            v.wait_ge(x_in, 32)

            def mean(t, b, first):
                if not (first and isinstance(t, int) and t == 0):
                    v.wait_ge(turned, t - 1)
                v.scalar_tensor_tensor(zin[:, b, D:2 * D], one(x2, t), m.cnt[:, bass.ds(t, 1)], f0,
                                       ALU.mult, ALU.mult).then_inc(mean_c, 1)

            def residual(t, b, first):
                v.wait_ge(lin, t + 1)
                v.tensor_tensor(z[:, b, :], m.psum[:, 2 + b, 0:D], bias, ALU.add).then_inc(lin_read, 1)
                v.wait_ge(lin_read, t + 1)
                v.wait_ge(mean_c, t + 1)
                v.scalar_tensor_tensor(one(x2, t), z[:, b, :], 0.0, one(x, t), ALU.max, ALU.add).then_inc(dve, 1)

            pipeline(v, mean, residual)
            step.n += T
            assert step.n == C_X2
            step.wait()
            statistics(v, m, step, x2)
            assert step.n == C_VAR
            v.wait_ge(sq, 1)
            inverse_root(v, m, step)
            v.memset(xnt[:, :, NP:ST * P], 0.0).then_inc(pad, 1)

            def normalise(t, b, first):
                if not (first and isinstance(t, int) and t == 0):
                    v.wait_ge(turned2, t - 1)
                v.tensor_scalar(zin[:, b, 0:D], one(x2, t), m.mean[:, bass.ds(t, 1)], m.rstd[:, bass.ds(t, 1)],
                                ALU.subtract, ALU.mult).then_inc(normed, 1)

            def keep(t, b, first):
                v.wait_ge(proj, t + 1)
                v.tensor_copy(proj_sb[:, bass.ds(t, 1), :].rearrange("p o c -> p (o c)"), m.psum[:, 6 + b, 0:WX])\
                 .then_inc(proj_read, 1)

            pipeline(v, normalise, keep)


C_X2 = 8 + T
C_VAR = C_X2 + STATISTICS


def gather_and_experts(nc, ctx, m, a):
    def sem(name):
        return ctx.enter_context(nc.semaphore(name))

    w_in, idx_ready, ones = sem("d_w_in"), sem("d_idx_ready"), sem("d_ones")
    slot_in = [sem(f"slot_in{k}") for k in range(GB)]
    up, gelu, down, y_c = sem("up"), sem("gelu"), sem("down"), sem("y_c")
    y_out = [sem(f"y_out{k}") for k in range(2)]
    zeroed = sem("zeroed")
    half = GB // 2
    w1 = m.big[:, L * TW:L * TW + X * 2 * FF].rearrange("p (e k f) -> p e k f", e=X, k=2)
    stage = m.big[:, L * TW + X * 2 * FF:L * TW + X * 2 * FF + GB * WX].rearrange("p (s c) -> p s c", s=GB)
    w2 = m.edge[:, 0:X * FF // P * D].rearrange("p (e f d) -> p e f d", e=X, f=FF // P)
    b1 = m.small[:, 64 * 17:64 * 17 + X * FF // P]
    hid = m.work[:, 0:2048].rearrange("p (b f n) -> p b f n", b=2, f=FF // P)
    y = m.work[:, 2048:3072].rearrange("p (b t d) -> p b t d", b=2, t=NB)
    zero = m.wgnn[:, :, :].rearrange("p k d -> p (k d)")
    xnt = m.mid[:, :].rearrange("p (k n) -> p k n", k=2)
    steps = ST // NB
    W = NB * P

    with nc.Block() as block:
        @block.gpsimd
        def _(pool):
            staged = pool.alloc_register("staged2")
            pool.reg_mov(staged, 1)
            with pool.Fori(0, L // GB) as it:
                for k in range(GB):
                    if k % half == 0:
                        pool.wait_ge(idx_ready, staged)
                        pool.reg_add(staged, staged, 1)
                    pool.indirect_dma_start(stage[:, k, :], None, a["table"],
                                            bass.IndirectOffsetOnAxis(ap=m.idx[:, k // half, k % half:k % half + 1], axis=0))\
                        .then_inc(slot_in[k], 16)

        @block.vector
        def _(v):
            v.memset(zero, 0.0).then_inc(ones, 1)
            v.memset(m.iota_x[:, :], 1.0).then_inc(ones, 1)
            for h in range(2):
                v.tensor_copy(m.idx[:, h, 0:half], m.ssrc[:, h * half:(h + 1) * half]).then_inc(idx_ready, 1)
            copied = sem("copied")

            def take(it, h, last):
                for k in range(h * half, (h + 1) * half):
                    v.wait_ge(slot_in[k], it * 16 + 16)
                v.tensor_copy(m.big[:, bass.ds(it * (GB * TW) + h * half * TW, half * TW)].rearrange("p (s c) -> p s c", c=TW),
                              stage[:, h * half:(h + 1) * half, 0:TW]).then_inc(copied, 1)
                v.wait_ge(copied, it * 2 + h + 1)
                if not last:
                    v.tensor_copy(m.idx[:, h, 0:half], m.ssrc[:, bass.ds(it * GB + GB + h * half, half)])\
                     .then_inc(idx_ready, 1)

            with v.Fori(0, L // GB - 1) as it:
                take(it, 0, False)
                take(it, 1, False)
            take(L // GB - 1, 0, True)
            take(L // GB - 1, 1, True)

        def experts(eng, stage1, stage2):
            stage1(0, 0, True)
            
            def body(blk, first, last):
                for e in range(X):
                    if not (last and e == X - 1):
                        stage1(blk * X + (e + 1), (e + 1) % X, first and e == 0)
                    stage2(blk * X + e, e, first and e < 2)
            body(0, True, False)
            with eng.Fori(1, steps - 1) as blk:
                body(blk, False, False)
            body(steps - 1, False, True)

        @block.tensor
        def _(pe):
            pe.wait_ge(w_in, 16 * 4)
            pe.wait_ge(ones, 2)

            def hidden(s, e, first):
                if not first:
                    pe.wait_ge(gelu, (s - 1) * (FF // P))
                for f in range(FF // P):
                    for k in range(2):
                        last = pe.matmul(m.psum[:, 2 * (e % 2) + f // 2, (f % 2) * W:(f % 2) * W + W],
                                         w1[:, e, k, f * P:(f + 1) * P], xnt[:, k, bass.ds(node(s, e), W)],
                                         start=(k == 0), stop=(k == 1))
                last.then_inc(up, 1)

            def node(s, e):
                return (s - e) * (W // X)

            def out(s, e, first):
                pe.wait_ge(gelu, s * 4 + 4)
                if not first:
                    pe.wait_ge(y_c, s - 1)
                for t in range(NB):
                    o = m.psum[:, 4 + e % 2, t * D:(t + 1) * D]
                    pe.matmul(o, m.iota_x[0:1, :], m.b2[0:1, e * D:(e + 1) * D], start=True, stop=False)
                    for f in range(FF // P):
                        last = pe.matmul(o, hid[:, e % 2, f, t * P:(t + 1) * P], w2[:, e, f, :], start=False,
                                         stop=(f == FF // P - 1))
                last.then_inc(down, 1)

            experts(pe, hidden, out)

        @block.scalar
        def _(act):
            act.wait_ge(w_in, 16 * 4)

            def gelus(s, e, first):
                act.wait_ge(up, s + 1)
                if not first:
                    act.wait_ge(down, s - 1)
                for f in range(FF // P):
                    act.activation(hid[:, e % 2, f, :], m.psum[:, 2 * (e % 2) + f // 2, (f % 2) * W:(f % 2) * W + W],
                                   ACT.Gelu, bias=b1[:, e * 4 + f:e * 4 + f + 1]).then_inc(gelu, 1)

            def keep(s, e, first):
                act.wait_ge(down, s + 1)
                if not first:
                    act.wait_ge(y_out[e % 2], past(s, e))
                act.activation(y[:, e % 2, :, :].rearrange("p t d -> p (t d)"), m.psum[:, 4 + e % 2, :], ACT.Copy)\
                   .then_inc(y_c, 1)

            def past(s, e):
                return (s - e % 2) * 8

            experts(act, gelus, keep)

        @block.sync
        def _(sp):
            sp.dma_start(w1, a["L0_ffn_W1"].rearrange("e (k p) f -> p e k f", p=P)).then_inc(w_in, 16)
            sp.dma_start(w2, a["L0_ffn_W2"].rearrange("e (f p) d -> p e f d", p=P)).then_inc(w_in, 16)
            sp.dma_start(b1, a["L0_ffn_b1"].rearrange("e (f p) -> p (e f)", p=P),
                         allow_slow_non_contiguous=True).then_inc(w_in, 16)
            sp.dma_start(m.b2[:, :], a["L0_ffn_b2"].rearrange("(o e) d -> o (e d)", o=1)).then_inc(w_in, 16)
            sp.wait_ge(ones, 1)
            with sp.Fori(0, 8) as i:
                sp.dma_start(a["values"].rearrange("(p l) c -> p (l c)", p=P)[:, bass.ds(i * 1024, 1024)], zero)\
                  .then_inc(zeroed, 16)
            ys = a["y"].rearrange("(t p) e d -> p t e d", p=P)
            with sp.Fori(0, steps) as blk:
                for e in range(X):
                    sp.wait_ge(y_c, blk * X + (e + 1))
                    sp.dma_start(ys[:, bass.ds(blk * NB, NB), e, :], y[:, e % 2, :, :]).then_inc(y_out[e % 2], 16)
            sp.wait_ge(zeroed, 8 * 16)
            for k in range(2):
                sp.wait_ge(y_out[k], steps * X // 2 * 16)


def attention(nc, ctx, m, a):
    def sem(name):
        return ctx.enter_context(nc.semaphore(name))

    dve, turned, max_out, max_in, value_idx, value_out, value_in = (
        sem("e_dve"), sem("e_turned"), sem("max_out"), sem("max_in"), sem("value_idx"), sem("value_out"), sem("value_in"))
    shifted, exped, sum_ready, sum_out, sum_in, proj_in, act_done, cols = (
        sem("shifted"), sem("exped"), sem("sum_ready"), sem("sum_out"), sem("sum_in"), sem("proj_in2"), sem("e_act"), sem("cols"))
    tables, root_in, fin_in, fin_done, fin_out = (sem("tables"), sem("root_in"),
                                                 [sem(f"fin_in{k}") for k in range(FB)], sem("fin_done"),
                                                 [sem(f"fin_out{k}") for k in range(FB)])
    g = m.big[:, 0:L * TW].rearrange("p (l c) -> p l c", c=TW)
    peak = m.mid[:, 8192:12288].rearrange("p (l c) -> p l c", c=H)
    val = m.mid[:, 0:8192].rearrange("p (l c) -> p l c", c=2 * H)
    same, pre, bar = m.skey[:, :], m.edge[:, 2048:3072], m.edge[:, 3072:4096]
    own = m.edge[:, 0:T * WX].rearrange("p (t c) -> p t c", t=T)
    node = m.big[:, L * TW:]

    def by_node(at, n):
        return node[:, at:at + T * n].rearrange("p (t c) -> p t c", t=T)

    top, vals, sums = by_node(0, H), by_node(196, 2 * H), by_node(588, TW)
    agg, tmp, sq = by_node(1568, HE), by_node(2352, HE), by_node(3136, HE)
    w = m.work
    es, score, rank, gate, cmp = (w[:, k * 196:(k + 1) * 196].rearrange("p (t c) -> p t c", t=T) for k in range(5))
    inv = w[:, 980:1176].rearrange("p (t c) -> p t c", t=T)
    par = w[:, 1200:1248].rearrange("p (s c) -> p s c", s=3)
    line, carry = w[:, 1280:1408], w[:, 1408:1536 + 1]
    colp, back, flag = w[:, 1600:1624], w[:, 1624:1648], w[:, 1648:1672]
    ch = w[:, 1680:1808]
    one_col = w[:, 1810:1811]
    own_h, own_src, own_dst = own[:, :, 0:HE], own[:, :, HE:TW], own[:, :, TW:WX]
    yb = m.mid[:, 0:FB * X * D].rearrange("p (b e d) -> p b e d", b=FB, e=X)
    xb = m.mid[:, FB * X * D:FB * (X + 1) * D].rearrange("p (b d) -> p b d", b=FB)
    ob = m.mid[:, FB * (X + 1) * D:FB * (X + 2) * D].rearrange("p (b d) -> p b d", b=FB)

    def spread(ap, n):
        return ap.unsqueeze(2).to_broadcast([P, T, n])

    with nc.Block() as block:
        @block.sync
        def _(sp):
            sp.dma_start(own, a["table"].rearrange("(t p) c -> p t c", p=P)).then_inc(proj_in, 16)
            for k, name in enumerate(("L0_ffn_b_gat", "L0_ffn_ln_gamma", "L0_ffn_ln_beta")):
                sp.dma_start(par[:, k, :], a[name].partition_broadcast(P)).then_inc(proj_in, 16)
            sp.wait_ge(tables, 1)
            sp.dma_start(a["peaks"].rearrange("(p l) c -> p l c", p=P), peak).then_inc(max_out, 16)
            sp.wait_ge(value_out, 16 * T)
            sp.dma_start(val, a["values"].rearrange("(p l) c -> p l c", p=P)).then_inc(value_in, 16)
            sp.wait_ge(tables, 2)
            sp.dma_start(a["sums"].rearrange("(p l) c -> p l c", p=P), g).then_inc(sum_out, 16)

            def load(t, b):
                sp.dma_start(yb[:, b, :, :], a["y"].rearrange("(t p) e d -> p t e d", p=P)[:, bass.ds(t, 1), :, :]
                             .rearrange("p o e d -> p (o e) d")).then_inc(fin_in[b], 16)
                sp.dma_start(xb[:, b, :], a["x2"].rearrange("(t p) d -> p t d", p=P)[:, bass.ds(t, 1), :]
                             .rearrange("p o d -> p (o d)")).then_inc(fin_in[b], 16)

            for b in range(FB):
                load(b, b)
            with sp.Fori(0, T // FB - 1) as i:
                for b in range(FB):
                    sp.wait_ge(fin_done, i * FB + (b + 1))
                    load(i * FB + (b + FB), b)
            sp.wait_ge(fin_done, T - FB)
            load(T - 1, 0)

        @block.gpsimd
        def _(pool):
            def by_index(idx, table, out, done):
                for t in range(T):
                    pool.indirect_dma_start(out[:, t, :], None, table,
                                            bass.IndirectOffsetOnAxis(ap=idx[:, t:t + 1], axis=0)).then_inc(done, 16)

            pool.wait_ge(max_out, 16)
            by_index(m.end_i, a["peaks"], top, max_in)
            pool.wait_ge(value_idx, 1)
            for t in range(T):
                pool.indirect_dma_start(a["values"], bass.IndirectOffsetOnAxis(ap=m.start_i[:, t:t + 1], axis=0),
                                        vals[:, t, :], None, bounds_check=E2 - 1, oob_is_err=False)\
                    .then_inc(value_out, 16)
            pool.wait_ge(sum_out, 16)
            by_index(m.end_i, a["sums"], sums, sum_in)

        @block.tensor
        def _(pe):
            for k, n in enumerate((H, 2 * H, TW)):
                pe.wait_ge(cols, 2 * k + 1)
                pe.transpose(m.psum[0:n, 0, 0:P], colp[:, 0:n], m.ident[:, :])
                pe.transpose(m.psum[0:n, 0, P:2 * P], flag[:, 0:n], m.ident[:, :]).then_inc(turned, 1)
                pe.wait_ge(cols, 2 * k + 2)
                pe.transpose(m.psum[:, 1, 0:n], carry[0:n, 0:P], m.ident[0:n, 0:n]).then_inc(turned, 1)

        @block.scalar
        def _(act):
            act.wait_ge(shifted, 1)
            act.activation(g[:, :, HE:TW], peak, ACT.Exp).then_inc(exped, 1)
            act.wait_ge(shifted, 2)
            act.activation(es, es, ACT.Exp).then_inc(exped, 1)
            act.wait_ge(shifted, 3)
            act.activation(m.rstd, m.var, ACT.Sqrt).then_inc(exped, 1)
            act.wait_ge(shifted, 4)
            act.activation(gate, gate, ACT.Exp).then_inc(exped, 1)
            tile = a["out"][0:(T - 1) * P, :].rearrange("(t p) d -> p t d", p=P)
            with act.Fori(0, T // FB) as i:
                for b in range(FB):
                    act.wait_ge(fin_done, i * FB + (b + 1))
                    act.dma_start(tile[:, bass.ds(i * FB + b, 1), :].rearrange("p o d -> p (o d)"), ob[:, b, :])\
                       .then_inc(fin_out[b], 16)
            act.wait_ge(fin_done, T)
            act.dma_start(a["out"][(T - 1) * P:N, :], ob[0:N - (T - 1) * P, 0, :]).then_inc(fin_out[0], 16)
            for b in range(FB):
                act.wait_ge(fin_out[b], (T // FB + (b == 0)) * 16)

        @block.vector
        def _(v):
            step = Steps(v, dve)
            turns = 0

            def inherit(n, totals, op):
                nonlocal turns
                step.then(v.tensor_copy(colp[:, 0:n], totals))
                step(v.tensor_copy(flag[:, 0:n], pre[:, L - 1:L].to_broadcast([P, n])))
                v.memset(one_col, 0.0).then_inc(cols, 1)
                turns += 1
                v.wait_ge(turned, turns)
                low = NEG if op == ALU.max else 0.0
                if op == ALU.max:
                    step.then(v.tensor_scalar(line[0:n, :], m.psum[0:n, 0, P:2 * P], -1.0, -NEG, ALU.add, ALU.mult))
                else:
                    step.then(v.tensor_copy(line[0:n, :], m.psum[0:n, 0, P:2 * P]))
                step(v.memset(carry[0:n, 0:1], low))
                step(v.tensor_tensor_scan(carry[0:n, 1:P + 1], line[0:n, :], m.psum[0:n, 0, 0:P], low,
                                          ALU.add if op == ALU.max else ALU.mult, op))
                v.memset(one_col, 0.0).then_inc(cols, 1)
                turns += 1
                v.wait_ge(turned, turns)
                step(v.tensor_copy(back[:, 0:n], m.psum[:, 1, 0:n]))

            def leaky(out, z):
                step(v.scalar_tensor_tensor(out, z, 0.2, z, ALU.mult, ALU.max))

            def running_sums(x, n):
                for c in range(n):
                    step.then(v.tensor_tensor_scan(x[:, :, c], same, x[:, :, c], 0.0, ALU.mult, ALU.add))
                step.wait()
                inherit(n, x[:, L - 1, 0:n], ALU.add)
                for c in range(n):
                    step.then(v.scalar_tensor_tensor(x[:, :, c], pre, back[:, c:c + 1], x[:, :, c], ALU.mult, ALU.add))
                step.wait()

            step.then(v.tensor_scalar(bar, same, -1.0, -NEG, ALU.add, ALU.mult))
            step(v.tensor_tensor_scan(pre, same, same, 1.0, ALU.mult, ALU.min))
            for h in range(H):
                step.then(v.tensor_tensor_scan(peak[:, :, h], bar, g[:, :, HE + h], NEG, ALU.add, ALU.max))
            step.wait()
            step(v.tensor_scalar(bar, pre, -1.0, -NEG, ALU.add, ALU.mult))
            inherit(H, peak[:, L - 1, :], ALU.max)
            for h in range(H):
                step.then(v.scalar_tensor_tensor(peak[:, :, h], bar, back[:, h:h + 1], peak[:, :, h], ALU.add, ALU.max))
            step.wait()
            v.memset(one_col, 0.0).then_inc(tables, 1)
            v.wait_ge(proj_in, 64)
            v.wait_ge(max_in, 16 * T)
            step(v.tensor_tensor(top, top, spread(m.some, H), ALU.mult))
            step(v.tensor_scalar(m.tmp_s, m.some, -1.0, -NEG, ALU.add, ALU.mult))
            step(v.tensor_tensor(top, top, spread(m.tmp_s, H), ALU.add))
            step(v.tensor_tensor(top, top, own_src, ALU.max))
            step.then(v.tensor_copy(vals[:, :, 0:H], own_dst))
            step(v.tensor_tensor(top, top, own_dst, ALU.add))
            leaky(vals[:, :, H:2 * H], top)
            v.memset(one_col, 0.0).then_inc(value_idx, 1)
            v.wait_ge(value_in, 16)
            running_sums(val, 2 * H)
            step(v.tensor_tensor(peak, g[:, :, HE:TW], val[:, :, 0:H], ALU.add))
            leaky(peak, peak)
            step(v.tensor_tensor(peak, peak, val[:, :, H:2 * H], ALU.subtract))
            v.memset(one_col, 0.0).then_inc(shifted, 1)
            v.wait_ge(exped, 1)
            msg = g[:, :, 0:HE].rearrange("p l (h e) -> p l h e", e=X)
            step(v.tensor_tensor(msg, msg, g[:, :, HE:TW].unsqueeze(3).to_broadcast([P, L, H, X]), ALU.mult))
            running_sums(g, TW)
            v.memset(one_col, 0.0).then_inc(tables, 1)
            step(v.tensor_tensor(es, own_src, own_dst, ALU.add))
            leaky(es, es)
            step(v.tensor_tensor(es, es, vals[:, :, H:2 * H], ALU.subtract))
            v.memset(one_col, 0.0).then_inc(shifted, 1)
            v.wait_ge(exped, 2)
            v.wait_ge(sum_in, 16 * T)
            step(v.tensor_tensor(sums, sums, spread(m.some, TW), ALU.mult))
            step(v.scalar_tensor_tensor(inv, sums[:, :, HE:TW], 1e-16, es, ALU.add, ALU.add))
            step(v.reciprocal(inv, inv))

            def heads(ap):
                return ap.rearrange("p t (h e) -> p t h e", e=X)

            def each(ap):
                return ap.unsqueeze(3).to_broadcast([P, T, H, X])

            step(v.tensor_tensor(heads(agg), heads(own_h), each(es), ALU.mult))
            step(v.tensor_tensor(agg, agg, sums[:, :, 0:HE], ALU.add))
            step(v.tensor_tensor(heads(agg), heads(agg), each(inv), ALU.mult))

            def param(k):
                return par[:, k, :].unsqueeze(1).to_broadcast([P, T, HE])

            step(v.tensor_tensor(agg, agg, param(0), ALU.add))
            step(v.tensor_reduce(m.mean, agg, AX.X, ALU.add))
            step(v.tensor_scalar(m.mean, m.mean, 1.0 / HE, None, ALU.mult))
            step(v.tensor_tensor(agg, agg, spread(m.mean, HE), ALU.subtract))
            step(v.tensor_tensor(sq, agg, agg, ALU.mult))
            step(v.tensor_reduce(m.var, sq, AX.X, ALU.add))
            step(v.tensor_scalar(m.var, m.var, 1.0 / HE, EPS, ALU.mult, ALU.add))
            v.memset(one_col, 0.0).then_inc(shifted, 1)
            v.wait_ge(exped, 3)
            inverse_root(v, m, step)
            step(v.tensor_tensor(agg, agg, spread(m.rstd, HE), ALU.mult))
            step(v.tensor_tensor(agg, agg, param(1), ALU.mult))
            step(v.tensor_tensor(agg, agg, param(2), ALU.add))
            step(v.tensor_reduce(score, agg.rearrange("p t (h e) -> p t e h", e=X), AX.X, ALU.add))
            step(v.tensor_scalar(score, score, 1.0 / H, None, ALU.mult))
            step(v.memset(rank, 0.0))
            for hi in range(1, X):
                for lo in range(hi):
                    c = cmp[:, :, 0]
                    step(v.tensor_tensor(c, score[:, :, lo], score[:, :, hi], ALU.is_ge))
                    step.then(v.tensor_tensor(rank[:, :, hi], rank[:, :, hi], c, ALU.add))
                    step(v.scalar_tensor_tensor(rank[:, :, lo], c, -1.0, rank[:, :, lo], ALU.mult, ALU.add))
                    step(v.tensor_scalar(rank[:, :, lo], rank[:, :, lo], 1.0, None, ALU.add))
            step(v.tensor_reduce(m.mean, score, AX.X, ALU.max))
            step(v.tensor_tensor(gate, score, spread(m.mean, X), ALU.subtract))
            v.memset(one_col, 0.0).then_inc(shifted, 1)
            v.wait_ge(exped, 4)
            step(v.scalar_tensor_tensor(gate, rank, 2.0, gate, ALU.is_lt, ALU.mult))
            step(v.tensor_reduce(m.var, gate, AX.X, ALU.add))
            step(v.reciprocal(m.var, m.var))
            step(v.tensor_tensor(gate, gate, spread(m.var, X), ALU.mult))

            def combine(t, b, e, seq):
                return v.scalar_tensor_tensor(ob[:, b, :], yb[:, b, e, :],
                                              gate[:, bass.ds(t, 1), e], (xb if e == 0 else ob)[:, b, :],
                                              ALU.mult, ALU.add)

            base, per = step.n, (X - 1) * FB
            with v.Fori(0, T // FB) as i:
                for b in range(FB):
                    v.wait_ge(fin_in[b], i * 32 + 32)
                    v.wait_ge(fin_out[b], i * 16)
                for e in range(X):
                    if e:
                        v.wait_ge(dve, i * per + (base + e * FB))
                    for b in range(FB):
                        combine(i * FB + b, b, e, 0).then_inc(dve if e < X - 1 else fin_done, 1)
            step.n += T // FB * per
            v.wait_ge(fin_in[0], (T // FB + 1) * 32)
            v.wait_ge(fin_out[0], T // FB * 16)
            for e in range(X - 1):
                step(combine(T - 1, 0, e, 0))
            combine(T - 1, 0, X - 1, 0).then_inc(fin_done, 1)


def program(nc, a):
    ctx = ExitStack()
    m = Mem()
    with ctx:
        allocate(nc, ctx, m)
        load_and_normalise(nc, ctx, m, a)
        gather_and_sort(nc, ctx, m, a)
        first_layer(nc, ctx, m, a)
        gather_and_experts(nc, ctx, m, a)
        attention(nc, ctx, m, a)


def constants():
    p = np.arange(P)

    def sign(k):
        return np.where((p >> (k - LOG_L)) & 1, -1.0, 1.0)

    last = LOG_L + 7
    signs = [sign(LOG_L)] + [sign(k) * sign(k - 1) for k in range(LOG_L + 1, last)] + [sign(last - 1)]
    nodes = np.arange(ST)[None, :] * P + p[:, None]
    return {
        "c_ident": np.eye(P, dtype=np.float32),
        "c_iota": np.ascontiguousarray(np.broadcast_to(p.astype(np.float32), (P, P))),
        "c_signs": np.stack(signs, axis=1).astype(np.float32),
        "c_nodekey": ((nodes << SHIFT) | KEY_BASE).astype(np.int32).view(np.float32),
    }


SCRATCH = {"feat": ((NP, D), F32), "rng_i": ((2, GP), I32), "rng_f": ((GP,), F32), "keys": ((E2,), F32),
           "starts": ((ST * P,), F32), "x2": ((NP, D), F32), "table": ((NP, WX), F32), "values": ((E2, 2 * H), F32),
           "peaks": ((E2, H), F32), "sums": ((E2, TW), F32), "y": ((ST * P, X, D), F32)}
_INS = ["x", "src", "dst", "edge_weight", "L0_gnn_W", "L0_gnn_b", "L0_ffn_W_gat", "L0_ffn_att_src", "L0_ffn_att_dst",
        "L0_ffn_b_gat", "L0_ffn_ln_gamma", "L0_ffn_ln_beta", "L0_ffn_W1", "L0_ffn_b1", "L0_ffn_W2", "L0_ffn_b2",
        "L0_ffn_edge_index"]


def kernel(**inputs):
    import concourse.bacc as bacc
    from concourse.bass_utils import run_bass_kernel_spmd

    nc = bacc.Bacc("TRN2", target_bir_lowering=False, num_devices=1)
    arrays, a = {}, {}
    for name, value in [(n, inputs[n]) for n in _INS] + list(constants().items()):
        value = np.ascontiguousarray(value)
        arrays[f"in_{name}"] = value
        a[name] = nc.dram_tensor(f"in_{name}", value.shape, mybir.dt.from_np(value.dtype), kind="ExternalInput").ap()
    for name, (shape, dt) in SCRATCH.items():
        a[name] = nc.dram_tensor(f"s_{name}", list(shape), dt, kind="Internal").ap()
    a["out"] = nc.dram_tensor("out_0", [N, D], F32, kind="ExternalOutput").ap()
    program(nc, a)
    return run_bass_kernel_spmd(nc, [arrays], core_ids=[0]).results[0]["out_0"]
```

```python
from contextlib import ExitStack

import numpy as np

import concourse.bass as bass
from concourse import mybir

F32 = mybir.dt.float32
I32 = mybir.dt.int32
ALU = mybir.AluOpType
ACT = mybir.ActivationFunctionType
AX = mybir.AxisListType

P = 128
N = 6250
D = 256
T = -(-N // P)
NP = T * P
E1 = 200000
CH = -(-E1 // P)
GC = 4
BODY = 8
NG = -(-CH // (GC * BODY)) * BODY
EB = -(-CH // P)
CP = EB * P
GP = CP // GC
PAD_DST = 8191
E2 = 131072
L = E2 // P
LOG_L = L.bit_length() - 1
SHIFT = 13
KEY_BASE = 0x38000000
HE = 16
H = 4
X = 4
TW = HE + H
WX = HE + 2 * H
FF = 512
EPS = 1e-5
SLOTS = BODY * GC
ST = T + 1
NB = 2
GB = 16
NEG = -1.0e38
FB = 4
FG = 4
XT = 7
SUB = 32
RING = 4
AW = D + 1


class Steps:

    def __init__(self, eng, sem, base=0):
        self.eng, self.sem, self.base, self.n = eng, sem, base, 0

    def then(self, ins):
        ins.then_inc(self.sem, 1)
        self.n += 1

    def wait(self):
        self.eng.wait_ge(self.sem, self.base + self.n)

    def __call__(self, ins):
        self.then(ins)
        self.wait()


class Mem:
    pass


def moments(v, m, sem, x, lo, hi):
    with v.Fori(lo, hi) as t:
        v.bn_stats(m.stats[:, bass.ds(t, 1), :].rearrange("p o s -> p (o s)"),
                   x[:, bass.ds(t, 1), 0:D].rearrange("p o d -> p (o d)")).then_inc(sem, 1)


def statistics(v, m, step):
    step.n += T
    step.wait()
    step.then(v.tensor_tensor(m.mean, m.stats[:, :, 1], m.stats[:, :, 4], ALU.add))
    step.then(v.tensor_tensor(m.tmp_s, m.stats[:, :, 1], m.stats[:, :, 4], ALU.subtract))
    step(v.tensor_tensor(m.var, m.stats[:, :, 2], m.stats[:, :, 5], ALU.add))
    step.then(v.tensor_scalar(m.mean, m.mean, 0.5, None, ALU.mult))
    step.then(v.tensor_scalar(m.var, m.var, 1.0 / D, EPS, ALU.mult, ALU.add))
    step(v.scalar_tensor_tensor(m.tmp_s, m.tmp_s, 0.25, m.tmp_s, ALU.mult, ALU.mult))
    step(v.tensor_tensor(m.var, m.var, m.tmp_s, ALU.add))


STATISTICS = T + 7


def inverse_root(v, m, step):
    step(v.reciprocal(m.rstd, m.rstd))
    step(v.tensor_tensor(m.tmp_s, m.rstd, m.rstd, ALU.mult))
    step(v.tensor_tensor(m.tmp_s, m.tmp_s, m.var, ALU.mult))
    step(v.tensor_scalar(m.tmp_s, m.tmp_s, -0.5, 1.5, ALU.mult, ALU.add))
    step(v.tensor_tensor(m.rstd, m.rstd, m.tmp_s, ALU.mult))


INVERSE_ROOT = 5
DVE_VAR = 3 + STATISTICS
DVE_ROOT = DVE_VAR + INVERSE_ROOT + 1


def allocate(nc, ctx, m):
    def sb(name, shape, dt=F32):
        return ctx.enter_context(nc.sbuf_tensor(name, shape, dt))

    m.big = sb("big", [P, T * D + T * AW])
    m.mid = sb("mid", [P, ST * D])
    m.edge = sb("edge", [P, 3 * CP])
    m.skey = sb("skey", [P, L])
    m.ssrc = sb("ssrc", [P, L], I32)
    m.wgnn = sb("wgnn", [P, 4, D])
    m.b2 = sb("b2", [1, X * D])
    m.ident = sb("ident", [P, P])
    m.iota = sb("iota", [P, P])
    m.iota_x = sb("iota_x", [P, P])
    m.signs = sb("signs", [P, 9])
    m.nodekey = sb("nodekey", [P, ST])
    m.small = sb("small", [P, 24 * 64])
    m.regs = sb("regs", [1, 2, GP], I32)
    m.idx = sb("idx", [P, 2, 16], I32)
    m.work = sb("work", [P, 3072])
    m.psum = ctx.enter_context(nc.psum_tensor("ps", [P, 8, 512], F32))

    m.feat = m.big[:, 0:T * D].rearrange("p (t d) -> p t d", t=T)
    m.acc = m.big[:, T * D:].rearrange("p (t d) -> p t d", t=T)
    m.acc_flat = m.big[:, T * D:]
    m.esrc = m.edge[:, 0:CP].bitcast(I32)
    m.edst = m.edge[:, CP:2 * CP]
    m.ewt = m.edge[:, 2 * CP:3 * CP]
    m.key = [m.mid[:, 10496 + k * L:10496 + (k + 1) * L] for k in range(2)]

    def small(k, n=ST):
        return m.small[:, 64 * k:64 * k + n]

    m.mean, m.var, m.rstd, m.tmp_s = small(0, T), small(1, T), small(2, T), small(15, T)
    m.start, m.end, m.some, m.row, m.cnt = small(3), small(4, T), small(5, T), small(8), small(9)
    m.row_i = small(6).bitcast(I32)
    m.start_i, m.end_i = small(6, T).bitcast(I32), small(7, T).bitcast(I32)
    m.stats = m.small[:, 640:640 + 6 * T].rearrange("p (t s) -> p t s", s=6)
    m.prev = m.small[:, 64 * 16:64 * 16 + 4]
    m.rows = m.mid[:, 0:SLOTS * D].rearrange("p (s d) -> p s d", s=SLOTS)
    m.wrows = m.mid[:, SLOTS * D:SLOTS * D + 2 * GC * AW].rearrange("p (b c d) -> p b c d", b=2, c=GC)
    m.hot = m.work[:, 0:3 * GC * P].rearrange("p (b c n) -> p b c n", b=3, c=GC)
    m.seek = m.edge[:, 3072:3072 + ST * SUB].rearrange("p (t s) -> p t s", t=ST)
    m.t0b = m.mid[:, 0:GP]
    m.shift, m.tmp_s2 = small(3, T), m.small[:, 64 * 22:64 * 22 + ST]
    m.val = m.mid[:, 0:L * H].rearrange("p (l c) -> p l c", c=H)
    m.peak = m.mid[:, L * H:2 * L * H].rearrange("p (l c) -> p l c", c=H)
    m.pre, m.bar, m.e = m.mid[:, 8192:9216], m.mid[:, 9216:10240], None
    last = m.mid[:, 10240:]
    m.line, m.carry, m.line2, m.carry2 = last[:, 0:P], last[:, P:2 * P + 1], last[:, 300:300 + P], last[:, 440:441 + P]
    m.colp, m.flag, m.back, m.back2 = (last[:, 600 + 32 * k:600 + 32 * k + TW] for k in range(4))
    m.adst = m.small[:, 64 * 18:64 * 18 + H * T].rearrange("p (t h) -> p t h", t=T)


def load_and_normalise(nc, ctx, m, a):
    def sem(name):
        return ctx.enter_context(nc.semaphore(name))

    x_in = [sem(f"x_in{c}") for c in range(T // XT)]
    e_in, c_in, w_in, feat_v, feat_a = sem("e_in"), sem("c_in"), sem("w_in"), sem("feat_v"), sem("feat_a")
    pads, dve, sq, chunk_t, chunk_c = sem("pads"), sem("a_dve"), sem("a_sqrt"), sem("chunk_t"), sem("chunk_c")
    edge_f, feat_out, rng_ready, rng_out, rng_in = (sem("edge_f"), sem("feat_out"), sem("rng_ready"),
                                                   sem("rng_out"), sem("rng_in"))
    w_t, w_c = sem("w_t"), sem("w_c")
    full, rest = E1 // P, E1 % P
    whole, tail = EB - 1, full - (EB - 1) * P
    raw = [m.mid[:, k * CP:(k + 1) * CP] for k in range(3)]
    src_raw, dst_raw = raw[0].bitcast(I32), raw[1].bitcast(I32)
    src_f, dst_f, tmp = (m.mid[:, k * CP:(k + 1) * CP] for k in (3, 4, 5))
    wraw = m.skey[:, 0:1024].rearrange("p (a k) -> p a k", a=2)
    cmin, cmax = m.small[:, 64 * 20:64 * 20 + EB], m.small[:, 64 * 20 + EB:64 * 20 + 2 * EB]
    gi = m.small[0:EB, 64 * 21:64 * 21 + 64].bitcast(I32)
    gf = m.small[0:EB, 64 * 22:64 * 22 + 64]
    gb = m.small[0:EB, 64 * 23:64 * 23 + 32]

    with nc.Block() as block:
        @block.sync
        def _(sp):
            sp.wait_ge(pads, 4)
            for r, name in ((src_raw, "src"), (dst_raw, "dst"), (raw[2], "edge_weight")):
                v = r.rearrange("p (b e) -> p b e", b=EB)
                s = a[name]
                sp.dma_start(v[:, 0:whole, :], s[0:whole * P * P].rearrange("(b p e) -> p b e", b=whole, p=P))\
                    .then_inc(e_in, 16)
                sp.dma_start(v[0:tail, whole, :], s[whole * P * P:full * P].rearrange("(p e) -> p e", e=P))\
                    .then_inc(e_in, 16)
                sp.dma_start(v[tail:tail + 1, whole, 0:rest], s[full * P:E1].rearrange("(p e) -> p e", p=1))\
                    .then_inc(e_in, 16)
            xt = a["x"][0:(T - 1) * P, :].rearrange("(t p) d -> p t d", p=P)
            for c in range(T // XT):
                hi = min((c + 1) * XT, T - 1)
                sp.dma_start(m.feat[:, c * XT:hi, :], xt[:, c * XT:hi, :]).then_inc(x_in[c], 16)
            sp.dma_start(m.feat[0:N - (T - 1) * P, T - 1, :], a["x"][(T - 1) * P:N, :]).then_inc(x_in[-1], 16)
            sp.wait_ge(rng_ready, 1)
            sp.dma_start(a["rng_i"].rearrange("k (b g) -> b k g", b=EB), gi.rearrange("b (k g) -> b k g", k=2))\
                .then_inc(rng_out, 16)
            sp.dma_start(a["rng_f"].rearrange("(b g) -> b g", b=EB), gb).then_inc(rng_out, 16)
            sp.wait_ge(rng_out, 32)
            sp.dma_start(m.regs[0:1, :, :], a["rng_i"].rearrange("(o k) g -> o k g", o=1)).then_inc(rng_in, 16)
            sp.dma_start(m.t0b, a["rng_f"].partition_broadcast(P)).then_inc(rng_in, 16)
            sp.wait_ge(rng_in, 32)

        @block.gpsimd
        def _(pool):
            fo = a["feat"].rearrange("(t p) d -> p t d", p=P)
            for c in range(T // XT):
                if c % 2 == 0:
                    pool.wait_ge(feat_v, (c // 2 + 1) * XT)
                else:
                    pool.wait_ge(feat_a, (c // 2 + 1) * XT)
                pool.dma_start(fo[:, c * XT:(c + 1) * XT, :], m.feat[:, c * XT:(c + 1) * XT, :]).then_inc(feat_out, 16)
            pool.wait_ge(feat_out, T // XT * 16)

        @block.scalar
        def _(act):
            for dst, name in ((m.ident, "c_ident"), (m.iota, "c_iota"), (m.signs, "c_signs"),
                              (m.nodekey, "c_nodekey")):
                act.dma_start(dst[:, :], a[name]).then_inc(c_in, 16)
            act.dma_start(wraw, a["L0_gnn_W"].rearrange("(a o) k -> o a k", a=2)).then_inc(w_in, 16)
            act.wait_ge(w_t, 1)
            for b in range(2):
                act.activation(m.wgnn[:, 2 * b:2 * b + 2, :].rearrange("p k o -> p (k o)"), m.psum[:, b, :],
                               ACT.Copy).then_inc(w_c, 1)
            for b in range(EB):
                act.wait_ge(chunk_t, b + 1)
                for k, dst in enumerate((m.esrc, m.edst, m.ewt)):
                    act.activation(dst[:, b * P:(b + 1) * P], m.psum[:, 4 + b % 4, k * P:(k + 1) * P], ACT.Copy)\
                       .then_inc(chunk_c, 1)
            act.wait_ge(dve, DVE_VAR)
            act.activation(m.rstd, m.var, ACT.Sqrt).then_inc(sq, 1)
            act.wait_ge(dve, DVE_ROOT)
            for c in range(1, T // XT, 2):
                with act.Fori(c * XT, (c + 1) * XT) as t:
                    tile = m.feat[:, bass.ds(t, 1), :].rearrange("p o d -> p (o d)")
                    act.activation(tile, tile, ACT.Identity, scale=m.rstd[:, bass.ds(t, 1)],
                                   bias=m.shift[:, bass.ds(t, 1)]).then_inc(feat_a, 1)

        @block.tensor
        def _(pe):
            pe.wait_ge(c_in, 64)
            pe.wait_ge(w_in, 16)
            for k in range(4):
                for o in range(2):
                    last = pe.transpose(m.psum[:, k // 2, (k % 2) * D + o * P:(k % 2) * D + (o + 1) * P],
                                        wraw[:, o, k * P:(k + 1) * P], m.ident[:, :])
            last.then_inc(w_t, 1)
            pe.wait_ge(edge_f, 2)
            pe.wait_ge(dve, 3)
            pe.transpose(m.psum[0:EB, 3, 0:P], cmin, m.ident[:, :])
            pe.transpose(m.psum[0:EB, 3, P:2 * P], cmax, m.ident[:, :]).then_inc(w_t, 1)
            pe.wait_ge(e_in, 9 * 16)
            for b in range(EB):
                if b >= 4:
                    pe.wait_ge(chunk_c, (b - 3) * 3)
                for k, s in enumerate((src_f, dst_f, raw[2])):
                    last = pe.transpose(m.psum[:, 4 + b % 4, k * P:(k + 1) * P], s[:, b * P:(b + 1) * P],
                                        m.ident[:, :])
                last.then_inc(chunk_t, 1)

        @block.vector
        def _(v):
            v.memset(m.feat[:, T - 1, :], 0.0).then_inc(pads, 1)
            v.memset(src_raw[:, whole * P:], 0).then_inc(pads, 1)
            v.memset(dst_raw[:, whole * P:], PAD_DST).then_inc(pads, 1)
            v.memset(raw[2][:, whole * P:], 0.0).then_inc(pads, 1)
            step = Steps(v, dve)
            v.wait_ge(e_in, 9 * 16)
            v.tensor_copy(src_f, src_raw).then_inc(edge_f, 1)
            step(v.tensor_copy(dst_f, dst_raw))
            step.then(v.tensor_reduce(cmin, dst_f.rearrange("p (b e) -> p b e", b=EB), AX.X, ALU.min))
            step(v.scalar_tensor_tensor(tmp, dst_f, float(NP), dst_f, ALU.is_lt, ALU.mult))
            v.tensor_reduce(cmax, tmp.rearrange("p (b e) -> p b e", b=EB), AX.X, ALU.max).then_inc(edge_f, 1)
            for c in range(T // XT):
                v.wait_ge(x_in[c], 16 if c < T // XT - 1 else 32)
                moments(v, m, dve, m.feat, c * XT, (c + 1) * XT)
            statistics(v, m, step)
            assert step.n == DVE_VAR
            v.wait_ge(sq, 1)
            inverse_root(v, m, step)
            step(v.scalar_tensor_tensor(m.shift, m.mean, -1.0, m.rstd, ALU.mult, ALU.mult))
            assert step.n == DVE_ROOT
            for c in range(0, T // XT, 2):
                with v.Fori(c * XT, (c + 1) * XT) as t:
                    tile = m.feat[:, bass.ds(t, 1), :].rearrange("p o d -> p (o d)")
                    v.tensor_scalar(tile, tile, m.mean[:, bass.ds(t, 1)], m.rstd[:, bass.ds(t, 1)],
                                    ALU.subtract, ALU.mult).then_inc(feat_v, 1)
            v.wait_ge(w_t, 2)
            for k in range(2):
                step.then(v.tensor_reduce(gf[:, 32 * k:32 * k + 32],
                                          m.psum[0:EB, 3, k * P:(k + 1) * P].rearrange("b (g c) -> b g c", c=GC),
                                          AX.X, (ALU.min, ALU.max)[k]))
            step.wait()
            step(v.tensor_copy(gi, gf))
            step(v.tensor_scalar(gi, gi, 7, None, ALU.arith_shift_right))
            step(v.tensor_scalar(gi, gi, T - 1, None, ALU.min))
            step(v.tensor_tensor(gi[:, 32:64], gi[:, 32:64], gi[:, 0:32], ALU.max))
            step(v.tensor_tensor(gi[:, 32:64], gi[:, 32:64], gi[:, 0:32], ALU.subtract))
            v.tensor_scalar(gb, gi[:, 0:32], float(P), None, ALU.mult).then_inc(rng_ready, 1)
            v.wait_ge(chunk_c, 3 * EB)
            v.wait_ge(rng_in, 32)
            step(v.tensor_tensor(m.edst.rearrange("p (g c) -> p g c", c=GC),
                                 m.edst.rearrange("p (g c) -> p g c", c=GC),
                                 m.t0b.unsqueeze(2).to_broadcast([P, GP, GC]), ALU.subtract))




BURSTS = [("rows", (1, 2, 3, 4)), ("rows", (5, 6))] + [("rows", (k,)) for k in range(7, LOG_L + 1)]
for _k in range(LOG_L + 1, LOG_L + 8):
    BURSTS += [("across", _k), ("within", _k)]
PARTS = [2] * len(BURSTS)


def gather_and_sort(nc, ctx, m, a):
    def sem(name):
        return ctx.enter_context(nc.semaphore(name))

    idx_ready, weighted, hot_ready, sums_ready = sem("idx_ready"), sem("weighted"), sem("hot_ready"), sem("sums_ready")
    group_done, hot_x, sums_x = sem("group_done"), sem("hot_x"), sem("sums_x")
    row_in = m.gathered = [sem(f"gathered{k}") for k in range(SLOTS)]
    sorting, turned, turned_c, e2_in, start_sem = (sem("sorting"), sem("turned"), sem("turned_c"), sem("e2_in"),
                                                   sem("b_setup"))
    key_out, prev_in, first_t, bias_in = sem("key_out"), sem("prev_in"), sem("first_t"), sem("bias_in")
    f_c, f_t, f_tc, f_l, f_z = sem("f_c"), sem("f_t"), sem("f_tc"), sem("f_l"), sem("f_z")
    fin, ft = m.work[:, 1536:1792], m.work[:, 1792:2048]
    bias = m.work[:, 2048:2304]
    subs = m.work[:, 2304:2304 + L // SUB]
    xstep = sem("xstep")
    iters = NG // BODY
    assert iters == T

    def parts():
        at = 1
        for n in PARTS:
            yield at, at + n
            at += n
        yield at, iters

    with nc.Block() as block:
        @block.gpsimd
        def _(pool):
            def body(it, first):
                for k in range(SLOTS):
                    if k % 16 == 0:
                        pool.wait_ge(idx_ready, it * 2 + k // 16 + 1)
                    if not first:
                        pool.wait_ge(weighted, used)
                        pool.reg_add(used, used, 1)
                    pool.indirect_dma_start(m.rows[:, k, :], None, a["feat"],
                                            bass.IndirectOffsetOnAxis(ap=m.idx[:, k // 16, k % 16:k % 16 + 1], axis=0))\
                        .then_inc(row_in[k], 16)
            used = pool.alloc_register("used")
            pool.reg_mov(used, 1)
            body(0, True)
            with pool.Fori(1, iters) as it:
                body(it, False)

        @block.scalar
        def _(act):
            for h in range(2):
                act.activation(m.idx[:, h, :], m.esrc[:, 16 * h:16 * h + 16], ACT.Copy).then_inc(idx_ready, 1)
            act.wait_ge(start_sem, 2)

            def body(it, first):
                act.activation(fin, m.feat[:, bass.ds(it, 1), :].rearrange("p o d -> p (o d)"), ACT.Copy).then_inc(f_c, 1)
                for k in range(SLOTS):
                    g = k // GC
                    if k == 4 * GC:
                        act.wait_ge(f_t, it + 1)
                        if not first:
                            act.wait_ge(f_l, it)
                        act.activation(ft, m.psum[:, 6, 0:D], ACT.Copy).then_inc(f_tc, 1)
                    if k % GC == 0 and not (first and g < 2):
                        act.wait_ge(group_done, it * BODY + (g - 1))
                    act.wait_ge(row_in[k], it * 16 + 16)
                    act.activation(m.wrows[:, g % 2, k % GC, 0:D], m.rows[:, k, :], ACT.Copy,
                                   scale=m.ewt[:, bass.ds(it * SLOTS + k, 1)]).then_inc(weighted, 1)
                    if k % 16 == 15:
                        act.activation(m.idx[:, k // 16, :], m.esrc[:, bass.ds(it * SLOTS + (SLOTS + k - 15), 16)],
                                       ACT.Copy).then_inc(idx_ready, 1)
            body(0, True)
            turn = 0
            for (lo, hi), (kind, _) in zip(parts(), BURSTS + [("end", 0)]):
                with act.Fori(lo, hi) as it:
                    body(it, False)
                if kind == "across":
                    for _ in range(2):
                        act.wait_ge(turned, turn + 1)
                        cur = TURNS[turn][0]
                        act.activation(m.key[1 - cur], m.psum[:, 4:6, :].rearrange("p b n -> p (b n)"), ACT.Copy)\
                           .then_inc(turned_c, 1)
                        turn += 1

        @block.tensor
        def _(pe):
            extra = pe.alloc_register("extra_pe")
            pe.reg_mov(extra, 0)

            def sums(out, hot, buf):
                for c in range(GC):
                    last = pe.matmul(out, m.hot[:, hot, c, :], m.wrows[:, buf, c, :], start=(c == 0), stop=(c == GC - 1))
                return last

            def body(it, first):
                for g in range(BODY):
                    if g == 2:
                        pe.wait_ge(f_c, it + 1)
                        if not first:
                            pe.wait_ge(f_tc, it)
                        for k in range(2):
                            last = pe.transpose(m.psum[:, 6, k * P:(k + 1) * P], fin[:, k * P:(k + 1) * P], m.ident[:, :])
                        last.then_inc(f_t, 1)
                    if g == 6:
                        pe.wait_ge(f_tc, it + 1)
                        if not first:
                            pe.wait_ge(f_z, it)
                        for k in range(2):
                            last = pe.matmul(m.psum[:, 7, 0:D], ft[:, k * P:(k + 1) * P], m.wgnn[:, k, :],
                                             start=(k == 0), stop=(k == 1))
                        last.then_inc(f_l, 1)
                    pe.wait_ge(weighted, it * SLOTS + (g + 1) * GC)
                    pe.wait_ge(hot_ready, it * BODY + (g + 1))
                    if not (first and g < 2):
                        pe.wait_ge(group_done, it * BODY + (g - 1))
                    sums(m.psum[:, g % 2, 0:AW], g % 2, g % 2).then_inc(sums_ready, 1)
                    more = pe.value_load(m.regs[0:1, 1, bass.ds(it * BODY + g, 1)], min_val=0, max_val=T - 1)
                    with pe.If(more > 0):
                        with pe.Fori(0, more):
                            pe.reg_add(extra, extra, 1)
                            pe.wait_ge(hot_x, pe.snap(extra))
                            sums(m.psum[:, 2, 0:AW], 2, g % 2).then_inc(sums_x, 1)
            body(0, True)
            turn = 0
            for (lo, hi), (kind, _) in zip(parts(), BURSTS + [("end", 0)]):
                with pe.Fori(lo, hi) as it:
                    body(it, False)
                if kind == "across":
                    for _ in range(2):
                        cur, n = TURNS[turn]
                        pe.wait_ge(sorting, n)
                        if turn:
                            pe.wait_ge(turned_c, turn)
                        for b in range(L // P):
                            last = pe.transpose(m.psum[:, 4 + b // 4, (b % 4) * P:(b % 4 + 1) * P],
                                                m.key[cur][:, b * P:(b + 1) * P], m.ident[:, :])
                        last.then_inc(turned, 1)
                        turn += 1
            pe.wait_ge(first_t, 1)
            pe.transpose(m.psum[:, 3, 0:P], m.hot[:, 2, 0, :], m.ident[:, :]).then_inc(turned, 1)

        @block.sync
        def _(sp):
            for k, dst in enumerate((m.skey[:, :].bitcast(I32), m.ssrc[:, :])):
                sp.dma_start(dst, a["L0_ffn_edge_index"][k, :].rearrange("(p l) -> p l", l=L)).then_inc(e2_in, 16)
            sp.dma_start(bias, a["L0_gnn_b"].partition_broadcast(P)).then_inc(bias_in, 16)
            cur, n = TURNS[-1]
            sp.wait_ge(sorting, n)
            keys = a["keys"].rearrange("(r l) -> r l", l=L)
            sp.dma_start(keys, m.key[cur]).then_inc(key_out, 16)
            sp.wait_ge(key_out, 16)
            sp.dma_start(m.prev[1:P, 0:1], keys[0:P - 1, L - 1:L],
                         allow_slow_non_contiguous=True).then_inc(prev_in, 16)
            sp.wait_ge(first_t, 2)
            sp.dma_start(a["subs"], subs).then_inc(key_out, 16)
            sp.wait_ge(key_out, 32)

        @block.vector
        def _(v):
            step = Steps(v, sorting)
            extra, xs = v.alloc_register("extra_dve"), v.alloc_register("xs_dve")
            v.reg_mov(extra, 0)
            v.reg_mov(xs, 1)
            further = v.alloc_register("further")
            v.memset(m.acc_flat, 0.0).then_inc(start_sem, 1)
            v.memset(m.wrows[:, :, :, D:AW], 1.0).then_inc(start_sem, 1)
            v.wait_ge(start_sem, 2)

            def hot(g, buf, iota):
                return v.tensor_tensor(m.hot[:, buf, :, :], iota.unsqueeze(1).to_broadcast([P, GC, P]),
                                       m.edst[:, bass.ds(g * GC, GC)].unsqueeze(2).to_broadcast([P, GC, P]),
                                       ALU.is_equal)

            def add(tile, bank):
                out = m.acc[:, bass.ds(tile, 1), :].rearrange("p o d -> p (o d)")
                return v.tensor_tensor(out, out, m.psum[:, bank, 0:AW], ALU.add)

            v.wait_ge(bias_in, 16)
            hot(0, 0, m.iota[:, :]).then_inc(hot_ready, 1)

            def body(it, first):
                for g in range(BODY):
                    if g == 7:
                        v.wait_ge(f_l, it + 1)
                        v.tensor_tensor(m.feat[:, bass.ds(it, 1), :].rearrange("p o d -> p (o d)"), m.psum[:, 7, 0:D],
                                        bias, ALU.add).then_inc(f_z, 1)
                    hot(it * BODY + (g + 1), (g + 1) % 2, m.iota[:, :]).then_inc(hot_ready, 1)
                    v.wait_ge(sums_ready, it * BODY + (g + 1))
                    if not (first and g == 0):
                        v.wait_ge(group_done, it * BODY + g)
                    tile = v.value_load(m.regs[0:1, 0, bass.ds(it * BODY + g, 1)], min_val=0, max_val=T - 1)
                    more = v.value_load(m.regs[0:1, 1, bass.ds(it * BODY + g, 1)], min_val=0, max_val=T - 1)
                    with v.If(more > 0):
                        v.reg_mov(further, tile)
                        v.tensor_scalar(m.iota_x[:, :], m.iota[:, :], float(P), None, ALU.add).then_inc(xstep, 1)
                        v.wait_ge(xstep, v.snap(xs))
                        v.reg_add(xs, xs, 1)
                        with v.Fori(0, more):
                            hot(it * BODY + g, 2, m.iota_x[:, :]).then_inc(hot_x, 1)
                            v.reg_add(extra, extra, 1)
                            v.wait_ge(sums_x, v.snap(extra))
                            v.reg_add(further, further, 1)
                            add(v.snap(further, min_val=0, max_val=T - 1), 2).then_inc(xstep, 1)
                            v.tensor_scalar(m.iota_x[:, :], m.iota_x[:, :], float(P), None, ALU.add)\
                             .then_inc(xstep, 1)
                            v.reg_add(xs, xs, 1)
                            v.wait_ge(xstep, v.snap(xs))
                            v.reg_add(xs, xs, 1)
                    add(tile, g % 2).then_inc(group_done, 1)

            cur = 0

            def merge(src, dist, mirror=False):
                nonlocal cur
                s, d = (k.rearrange("p (n two h) -> p n two h", two=2, h=dist) for k in (src, m.key[1 - cur]))
                turn = slice(None, None, -1) if mirror else slice(None)
                step.then(v.tensor_tensor(d[:, :, 0, :], s[:, :, 0, :], s[:, :, 1, turn], ALU.min))
                step(v.tensor_tensor(d[:, :, 1, :], s[:, :, 1, :], s[:, :, 0, turn], ALU.max))
                cur = 1 - cur

            def sign(k):
                nonlocal cur
                step(v.tensor_scalar(m.key[1 - cur], m.key[cur], m.signs[:, k:k + 1], None, ALU.mult))
                cur = 1 - cur

            def turn():
                nonlocal cur, turns
                assert TURNS[turns] == (cur, step.n)
                turns += 1
                v.wait_ge(turned_c, turns)
                cur = 1 - cur

            src, key_i = m.skey[:, :].bitcast(I32), m.key[0].bitcast(I32)
            v.wait_ge(e2_in, 32)
            step.then(v.tensor_scalar(src, src, N - 1, None, ALU.min))
            step(v.tensor_scalar(m.ssrc[:, :], m.ssrc[:, :], N, None, ALU.min))
            step(v.tensor_scalar(m.ssrc[:, :], m.ssrc[:, :], SHIFT, KEY_BASE, ALU.logical_shift_left, ALU.bitwise_or))
            step(v.tensor_tensor(key_i, m.ssrc[:, :], src, ALU.bitwise_or))
            sign(0)
            turns = 0
            body(0, True)
            for (lo, hi), (kind, what) in zip(parts(), BURSTS + [("end", 0)]):
                with v.Fori(lo, hi) as it:
                    body(it, False)
                if kind == "rows":
                    for k in what:
                        merge(m.key[cur], 1 << (k - 1), mirror=True)
                        for j in range(k - 2, -1, -1):
                            merge(m.key[cur], 1 << j)
                if kind == "across":
                    sign(what - LOG_L)
                    turn()
                    for j in range(what - LOG_L - 1, -1, -1):
                        merge(m.key[cur], 1 << j)
                    turn()
                if kind == "within":
                    for j in range(LOG_L - 1, -1, -1):
                        merge(m.key[cur], 1 << j)
            assert TURNS[turns] == (cur, step.n)
            v.wait_ge(group_done, NG)

            key, run = m.key[cur], m.key[1 - cur].bitcast(I32)
            prev = m.prev.bitcast(I32)
            v.wait_ge(prev_in, 16)
            step.then(v.tensor_scalar(m.ssrc[:, :], key.bitcast(I32), (1 << SHIFT) - 1, None, ALU.bitwise_and))
            step.then(v.tensor_scalar(run, key.bitcast(I32), SHIFT, None, ALU.logical_shift_right))
            step.then(v.memset(m.prev[0:1, 0:1], 0.0))
            step(v.tensor_copy(m.hot[:, 2, 0, :], key[:, 0:1].to_broadcast([P, P])))
            v.memset(m.prev[:, 2:3], 0.0).then_inc(first_t, 1)
            v.tensor_copy(subs, key.rearrange("p (s k) -> p s k", k=SUB)[:, :, 0]).then_inc(first_t, 1)
            step(v.tensor_scalar(prev[:, 1:2], prev[:, 0:1], SHIFT, None, ALU.logical_shift_right))
            step.then(v.tensor_tensor(m.skey[:, 1:L], run[:, 1:L], run[:, 0:L - 1], ALU.is_equal))
            step(v.tensor_tensor(m.skey[:, 0:1], run[:, 0:1], prev[:, 1:2], ALU.is_equal))
            below = m.mid[:, 0:ST * P].rearrange("p (t r) -> p t r", t=ST)
            v.wait_ge(turned, len(TURNS))
            step(v.tensor_tensor(below, m.psum[:, 3, 0:P].unsqueeze(1).to_broadcast([P, ST, P]),
                                 m.nodekey[:, :].unsqueeze(2).to_broadcast([P, ST, P]), ALU.is_lt))
            step(v.tensor_reduce(m.row, below, AX.X, ALU.add))
            step(v.tensor_scalar(m.row, m.row, -1.0, 0.0, ALU.add, ALU.max))


def turn_plan():
    cur, n, out = 1, 5, []
    for k in range(1, LOG_L + 1):
        cur, n = (cur + k) % 2, n + 2 * k
    for k in range(1, 8):
        cur, n = 1 - cur, n + 1
        out.append((cur, n))
        cur, n = (cur + 1 + k) % 2, n + 2 * k
        out.append((cur, n))
        cur, n = (cur + 1 + LOG_L) % 2, n + 2 * LOG_L
    return out + [(cur, n)]


TURNS = turn_plan()
BEYOND = 1 << 20


def first_layer(nc, ctx, m, a):
    def sem(name):
        return ctx.enter_context(nc.semaphore(name))

    x_in, c_in, f0_i, f0_in = sem("c_x_in"), sem("c_const"), sem("f0_i"), sem("f0_in")
    dve, sq, pad = sem("c_dve"), sem("c_sqrt"), sem("c_pad")
    mean_c, turned, turned_c, lin = sem("mean_c"), sem("c_turned"), sem("c_turned_c"), sem("lin")
    biased, normed, turned2, turned2_c, kept2, proj, proj_read = (
        sem("biased"), sem("normed"), sem("turned2"), sem("turned2_c"), sem("kept2"), sem("proj"), sem("proj_read"))
    stored, w_ready, seek_idx, seek_in = sem("c_stored"), sem("w_ready"), sem("seek_idx"), sem("seek_in")
    xt = m.work[:, 0:2 * D].rearrange("p (b d) -> p b d", b=2)
    f0 = m.work[:, 512:768]
    wext = m.work[:, 768:816].rearrange("p (k c) -> p k c", k=2)
    att = m.work[:, 816:848]
    prod = m.work[:, 848:912].rearrange("p (s k c) -> p s k c", s=2, k=2)
    z = m.work[:, 1024:1024 + RING * D].rearrange("p (b d) -> p b d", b=RING)
    zin = m.edge[:, 2048:2048 + RING * D].rearrange("p (b d) -> p b d", b=RING)
    proj_sb = m.edge[:, 0:T * WX].rearrange("p (t c) -> p t c", t=T)
    x = m.mid[:, 0:T * D].rearrange("p (t d) -> p t d", t=T)
    x2 = m.acc[:, :, 0:D]
    xnt = m.mid[:, :].rearrange("p (k n) -> p k n", k=2)

    def one(ap, t):
        return ap[:, bass.ds(t, 1), 0:D].rearrange("p o d -> p (o d)")

    def since(eng, done, t, n):
        if not isinstance(t, int) or t - n >= 0:
            eng.wait_ge(done, t - n + 1)

    def pipeline(eng, stage1, stage2, lag):
        def step(t, b, last=T):
            if not isinstance(t, int) or t + lag < last:
                stage1(t + lag, (b + lag) % RING)
            stage2(t, b)
        for t in range(lag):
            stage1(t, t)
        for t in range(RING):
            step(t, t)
        with eng.Fori(1, (T - lag) // RING) as i:
            for b in range(RING):
                step(i * RING + b, b)
        for t in range((T - lag) // RING * RING, T):
            step(t, t % RING)

    with nc.Block() as block:
        @block.sync
        def _(sp):
            sp.dma_start(m.idx[:, 0, 0:1], a["src"][0:1].partition_broadcast(P)).then_inc(f0_i, 16)
            sp.dma_start(x[:, 0:T - 1, :], a["x"][0:(T - 1) * P, :].rearrange("(t p) d -> p t d", p=P)).then_inc(x_in, 16)
            sp.wait_ge(pad, 1)
            sp.dma_start(x[0:N - (T - 1) * P, T - 1, :], a["x"][(T - 1) * P:N, :]).then_inc(x_in, 16)
            sp.wait_ge(dve, C_X2)
            sp.dma_start(a["x2"].rearrange("(t p) d -> p t d", p=P), x2).then_inc(stored, 16)
            sp.wait_ge(proj_read, T)
            sp.dma_start(a["table"].rearrange("(t p) c -> p t c", p=P), proj_sb).then_inc(stored, 16)
            sp.wait_ge(stored, 32)

        @block.gpsimd
        def _(pool):
            pool.wait_ge(f0_i, 16)
            pool.indirect_dma_start(f0, None, a["feat"], bass.IndirectOffsetOnAxis(ap=m.idx[:, 0, 0:1], axis=0))\
                .then_inc(f0_in, 16)
            for k, table in enumerate((a["subs"], a["keys"].rearrange("(r s) -> r s", s=SUB))):
                pool.wait_ge(seek_idx, k + 1)
                for t in range(ST):
                    pool.indirect_dma_start(m.seek[:, t, :], None, table,
                                            bass.IndirectOffsetOnAxis(ap=m.row_i[:, t:t + 1], axis=0)).then_inc(seek_in, 16)
            pool.wait_ge(seek_in, 2 * ST * 16)

        @block.scalar
        def _(act):
            act.dma_start(wext[:, :, 0:HE], a["L0_ffn_W_gat"].rearrange("(k p) c -> p k c", p=P)).then_inc(c_in, 16)
            for k, name in enumerate(("L0_ffn_att_src", "L0_ffn_att_dst")):
                act.dma_start(att[:, HE * k:HE * k + HE], a[name].rearrange("h e -> (h e)").partition_broadcast(P))\
                   .then_inc(c_in, 16)

            def nothing(t, b):
                pass

            def copy(t, b):
                act.wait_ge(turned, t + 1)
                since(act, lin, t, 2)
                act.activation(xt[:, b % 2, :], m.psum[:, b % 2, 0:D], ACT.Copy).then_inc(turned_c, 1)

            pipeline(act, nothing, copy, 0)
            act.wait_ge(dve, C_VAR)
            act.activation(m.rstd, m.var, ACT.Sqrt).then_inc(sq, 1)

            def copies(t, b):
                act.wait_ge(turned2, t + 1)
                since(act, proj, t, 2)
                act.activation(xt[:, b % 2, :], m.psum[:, 4 + b % 2, 0:D], ACT.Copy).then_inc(turned2_c, 1)
                act.activation(xnt[:, :, bass.ds(t * P, P)], m.psum[:, 4 + b % 2, 0:D].rearrange("p (k n) -> p k n", k=2),
                               ACT.Copy).then_inc(kept2, 1)

            pipeline(act, nothing, copies, 0)

        @block.tensor
        def _(pe):
            def turn(t, b):
                pe.wait_ge(mean_c, t + 1)
                since(pe, turned_c, t, 2)
                for k in range(2):
                    last = pe.transpose(m.psum[:, b % 2, k * P:(k + 1) * P], zin[:, b, k * P:(k + 1) * P], m.ident[:, :])
                last.then_inc(turned, 1)

            def linear(t, b):
                pe.wait_ge(turned_c, t + 1)
                since(pe, biased, t, 2)
                for k in range(2):
                    last = pe.matmul(m.psum[:, 2 + b % 2, 0:D], xt[:, b % 2, k * P:(k + 1) * P], m.wgnn[:, 2 + k, :],
                                     start=(k == 0), stop=(k == 1))
                last.then_inc(lin, 1)

            pipeline(pe, turn, linear, 1)
            pe.wait_ge(w_ready, 1)

            def turn2(t, b):
                pe.wait_ge(normed, t + 1)
                since(pe, kept2, t, 2)
                for k in range(2):
                    last = pe.transpose(m.psum[:, 4 + b % 2, k * P:(k + 1) * P], zin[:, b, k * P:(k + 1) * P],
                                        m.ident[:, :])
                last.then_inc(turned2, 1)

            def project(t, b):
                pe.wait_ge(turned2_c, t + 1)
                since(pe, proj_read, t, 2)
                for k in range(2):
                    last = pe.matmul(m.psum[:, 6 + b % 2, 0:WX], xt[:, b % 2, k * P:(k + 1) * P], wext[:, k, :],
                                     start=(k == 0), stop=(k == 1))
                last.then_inc(proj, 1)

            pipeline(pe, turn2, project, 1)

        @block.vector
        def _(v):
            step = Steps(v, dve)
            v.memset(x[:, T - 1, :], 0.0).then_inc(pad, 1)
            v.tensor_copy(m.row_i, m.row).then_inc(seek_idx, 1)
            v.wait_ge(c_in, 48)
            for s in range(2):
                step.then(v.tensor_tensor(prod[:, s, :, :], wext[:, :, 0:HE],
                                          att[:, HE * s:HE * s + HE].unsqueeze(1).to_broadcast([P, 2, HE]), ALU.mult))
            step.wait()
            for s in range(2):
                for k in range(2):
                    step.then(v.tensor_reduce(wext[:, k, HE + H * s:HE + H * s + H],
                                              prod[:, s, k, :].rearrange("p (h e) -> p h e", e=X), AX.X, ALU.add))
            step.wait()
            step(v.tensor_scalar(m.tmp_s, m.acc[:, :, D], 1.0, None, ALU.max))
            step(v.reciprocal(m.cnt[:, 0:T], m.tmp_s))
            v.memset(m.prev[:, 3:4], 0.0).then_inc(w_ready, 1)
            v.wait_ge(f0_in, 16)
            v.wait_ge(x_in, 32)

            def mean(t, b):
                since(v, turned, t, RING)
                v.scalar_tensor_tensor(zin[:, b, :], one(x2, t), m.cnt[:, bass.ds(t, 1)], f0,
                                       ALU.mult, ALU.mult).then_inc(mean_c, 1)

            def residual(t, b):
                v.wait_ge(lin, t + 1)
                since(v, dve_x2, t, RING)
                v.tensor_tensor(z[:, b, :], m.psum[:, 2 + b % 2, 0:D], one(m.feat, t), ALU.add).then_inc(biased, 1)
                if not isinstance(t, int) or t >= 1:
                    activate(t - 1, (b - 1) % RING)

            def activate(t, b):
                v.wait_ge(biased, t + 1)
                v.scalar_tensor_tensor(one(x2, t), z[:, b, :], 0.0, one(x, t), ALU.max, ALU.add).then_inc(dve_x2, 1)

            dve_x2 = sem("x2_tiles")
            pipeline(v, mean, residual, 2)
            activate(T - 1, (T - 1) % RING)
            v.wait_ge(dve_x2, T)
            step(v.memset(m.prev[:, 2:3], 0.0))
            assert step.n == C_X2
            moments(v, m, dve, x2, 0, T)
            statistics(v, m, step)
            assert step.n == C_VAR
            v.wait_ge(seek_in, ST * 16)
            low = m.nodekey[:, :].unsqueeze(2).to_broadcast([P, ST, SUB])
            v.wait_ge(sq, 1)
            inverse_root(v, m, step)
            v.memset(xnt[:, :, NP:ST * P], 0.0).then_inc(pad, 1)
            step(v.tensor_tensor(m.seek, m.seek, low, ALU.is_lt))
            step(v.tensor_reduce(m.tmp_s2, m.seek, AX.X, ALU.add))
            step(v.tensor_scalar(m.tmp_s2, m.tmp_s2, -1.0, 0.0, ALU.add, ALU.max))
            step(v.scalar_tensor_tensor(m.row, m.row, float(L // SUB), m.tmp_s2, ALU.mult, ALU.add))
            v.tensor_copy(m.row_i, m.row).then_inc(seek_idx, 1)

            def normalise(t, b):
                since(v, turned2, t, RING)
                v.tensor_scalar(zin[:, b, :], one(x2, t), m.mean[:, bass.ds(t, 1)], m.rstd[:, bass.ds(t, 1)],
                                ALU.subtract, ALU.mult).then_inc(normed, 1)

            def keep(t, b):
                v.wait_ge(proj, t + 1)
                v.tensor_copy(proj_sb[:, bass.ds(t, 1), :].rearrange("p o c -> p (o c)"), m.psum[:, 6 + b % 2, 0:WX])\
                 .then_inc(proj_read, 1)

            pipeline(v, normalise, keep, 2)
            v.wait_ge(proj_read, T)
            step(v.tensor_copy(m.adst, proj_sb[:, :, TW:WX]))
            v.wait_ge(seek_in, 2 * ST * 16)
            step(v.tensor_tensor(m.seek, m.seek, low, ALU.is_lt))
            step(v.tensor_reduce(m.tmp_s2, m.seek, AX.X, ALU.add))
            step(v.scalar_tensor_tensor(m.start, m.row, float(SUB), m.tmp_s2, ALU.mult, ALU.add))


C_X2 = 9
C_VAR = C_X2 + STATISTICS


def gather_and_experts(nc, ctx, m, a):
    def sem(name):
        return ctx.enter_context(nc.semaphore(name))

    w_in, idx_ready, ones, copied = sem("d_w_in"), sem("d_idx_ready"), sem("d_ones"), sem("copied")
    slot_in = m.gathered[0:GB]
    before = NG // BODY * 16
    up, gelu, down, y_c = sem("up"), sem("gelu"), sem("down"), sem("y_c")
    y_out = [sem(f"y_out{k}") for k in range(2)]
    zeroed, dve, start_t, turned, start_out, end_in, value_idx, value_out, value_in, cols = (
        sem("zeroed"), sem("d_dve"), sem("start_t"), sem("d_turned"), sem("start_out"), sem("end_in"), sem("value_idx"),
        sem("value_out"), sem("value_in"), sem("d_cols"))
    half = GB // 2
    w1 = m.big[:, L * TW:L * TW + X * 2 * FF].rearrange("p (e k f) -> p e k f", e=X, k=2)
    stage = m.big[:, L * TW + X * 2 * FF:L * TW + X * 2 * FF + GB * WX].rearrange("p (s c) -> p s c", s=GB)
    w2 = m.edge[:, 0:X * FF // P * D].rearrange("p (e f d) -> p e f d", e=X, f=FF // P)
    turns = m.edge[:, X * FF // P * D:X * FF // P * D + 3 * P]
    b1 = m.small[:, 64 * 17:64 * 17 + X * FF // P]
    hid = m.work[:, 0:2048].rearrange("p (b f n) -> p b f n", b=2, f=FF // P)
    y = m.work[:, 2048:3072].rearrange("p (b t d) -> p b t d", b=2, t=NB)
    zero = m.wgnn[:, :, :].rearrange("p k d -> p (k d)")
    xnt = m.mid[:, :].rearrange("p (k n) -> p k n", k=2)
    steps = ST // NB
    W = NB * P
    its = L // GB
    scatter_at, spread_at = its // 4, its - 8

    with nc.Block() as block:
        @block.gpsimd
        def _(pool):
            staged = pool.alloc_register("staged")
            pool.reg_mov(staged, 1)

            def gathers(lo, hi):
                with pool.Fori(lo, hi):
                    for k in range(GB):
                        if k % half == 0:
                            pool.wait_ge(idx_ready, staged)
                            pool.reg_add(staged, staged, 1)
                        pool.indirect_dma_start(
                            stage[:, k, :], None, a["table"],
                            bass.IndirectOffsetOnAxis(ap=m.idx[:, k // half, k % half:k % half + 1], axis=0))\
                            .then_inc(slot_in[k], 16)

            gathers(0, scatter_at)
            pool.wait_ge(value_idx, 1)
            pool.wait_ge(zeroed, 4 * 16)
            for t in range(T):
                pool.indirect_dma_start(a["values"], bass.IndirectOffsetOnAxis(ap=m.start_i[:, t:t + 1], axis=0),
                                        m.adst[:, t, :], None, bounds_check=E2 - 1, oob_is_err=False)\
                    .then_inc(value_out, 16)
            gathers(scatter_at, its)

        @block.vector
        def _(v):
            step = Steps(v, dve)
            v.memset(zero, 0.0).then_inc(ones, 1)
            v.memset(m.iota_x[:, :], 1.0).then_inc(ones, 1)
            for h in range(2):
                v.tensor_copy(m.idx[:, h, 0:half], m.ssrc[:, h * half:(h + 1) * half]).then_inc(idx_ready, 1)
            v.wait_ge(turned, 1)
            v.tensor_copy(turns[0:ST, 0:P], m.psum[0:ST, 6, 0:P]).then_inc(start_t, 1)

            def take(it, h, last=False):
                for k in range(h * half, (h + 1) * half):
                    v.wait_ge(slot_in[k], it * 16 + (before + 16))
                v.tensor_copy(m.big[:, bass.ds(it * (GB * TW) + h * half * TW, half * TW)].rearrange("p (s c) -> p s c", c=TW),
                              stage[:, h * half:(h + 1) * half, 0:TW]).then_inc(copied, 1)
                v.wait_ge(copied, it * 2 + h + 1)
                if not last:
                    v.tensor_copy(m.idx[:, h, 0:half], m.ssrc[:, bass.ds(it * GB + GB + h * half, half)])\
                     .then_inc(idx_ready, 1)

            with v.Fori(0, 2) as it:
                take(it, 0)
                take(it, 1)
            v.wait_ge(turned, 2)
            step(v.tensor_copy(m.end, m.psum[:, 6, P:P + T]))
            step(v.tensor_tensor(m.some, m.end, m.start[:, 0:T], ALU.is_gt))
            step(v.scalar_tensor_tensor(m.tmp_s, m.start[:, 0:T], float(-BEYOND), m.some, ALU.add, ALU.mult))
            step.then(v.tensor_scalar(m.start_i, m.tmp_s, float(BEYOND), None, ALU.add))
            step(v.tensor_scalar(m.end_i, m.end, -1.0, 0.0, ALU.add, ALU.max))
            v.memset(m.prev[:, 0:1], 0.0).then_inc(value_idx, 1)
            with v.Fori(2, spread_at) as it:
                take(it, 0)
                take(it, 1)
            pre, val, back = m.pre, m.val, m.back
            v.wait_ge(value_in, 16)
            it = spread_at
            step(v.tensor_tensor_scan(pre, m.skey[:, :], m.skey[:, :], 1.0, ALU.mult, ALU.min))
            for h in range(H):
                step.then(v.tensor_tensor_scan(val[:, :, h], m.skey[:, :], val[:, :, h], 0.0, ALU.mult, ALU.add))
                if h % 2:
                    take(it, 0)
                    take(it, 1)
                    it += 1
            step.wait()
            step.then(v.tensor_copy(m.colp[:, 0:H], val[:, L - 1, :]))
            step(v.tensor_copy(m.flag[:, 0:H], pre[:, L - 1:L].to_broadcast([P, H])))
            v.memset(m.prev[:, 0:1], 0.0).then_inc(cols, 1)
            take(it, 0)
            v.wait_ge(turned, 3)
            step.then(v.tensor_copy(m.line[0:H, :], m.psum[0:H, 6, P:2 * P]))
            step(v.memset(m.carry[0:H, 0:1], 0.0))
            step(v.tensor_tensor_scan(m.carry[0:H, 1:P + 1], m.line[0:H, :], m.psum[0:H, 6, 0:P], 0.0, ALU.mult, ALU.add))
            v.memset(m.prev[:, 0:1], 0.0).then_inc(cols, 1)
            take(it, 1)
            v.wait_ge(turned, 4)
            step(v.tensor_copy(back[:, 0:H], m.psum[:, 7, 0:H]))
            it += 1
            take(it, 0)
            take(it, 1)
            for h in range(H):
                step.then(v.scalar_tensor_tensor(val[:, :, h], pre, back[:, h:h + 1], val[:, :, h], ALU.mult, ALU.add))
            for n in range(it + 1, its):
                take(n, 0, n == its - 1)
                take(n, 1, n == its - 1)

        def experts(eng, stage1, stage2):
            stage1(0, 0, True)
            
            def body(blk, first, last):
                for e in range(X):
                    if not (last and e == X - 1):
                        stage1(blk * X + (e + 1), (e + 1) % X, first and e == 0)
                    stage2(blk * X + e, e, first and e < 2)
            body(0, True, False)
            with eng.Fori(1, steps - 1) as blk:
                body(blk, False, False)
            body(steps - 1, False, True)

        @block.tensor
        def _(pe):
            pe.transpose(m.psum[0:ST, 6, 0:P], m.start, m.ident[:, :]).then_inc(turned, 1)
            pe.wait_ge(end_in, 16)
            pe.transpose(m.psum[:, 6, P:P + T], turns[0:T, P:2 * P], m.ident[0:T, 0:T]).then_inc(turned, 1)
            pe.wait_ge(w_in, 16 * 4)
            pe.wait_ge(ones, 2)

            def hidden(s, e, first):
                if not first:
                    pe.wait_ge(gelu, (s - 1) * (FF // P))
                for f in range(FF // P):
                    for k in range(2):
                        last = pe.matmul(m.psum[:, 2 * (e % 2) + f // 2, (f % 2) * W:(f % 2) * W + W],
                                         w1[:, e, k, f * P:(f + 1) * P], xnt[:, k, bass.ds(node(s, e), W)],
                                         start=(k == 0), stop=(k == 1))
                last.then_inc(up, 1)

            def node(s, e):
                return (s - e) * (W // X)

            def out(s, e, first):
                pe.wait_ge(gelu, s * 4 + 4)
                if not first:
                    pe.wait_ge(y_c, s - 1)
                for t in range(NB):
                    o = m.psum[:, 4 + e % 2, t * D:(t + 1) * D]
                    pe.matmul(o, m.iota_x[0:1, :], m.b2[0:1, e * D:(e + 1) * D], start=True, stop=False)
                    for f in range(FF // P):
                        last = pe.matmul(o, hid[:, e % 2, f, t * P:(t + 1) * P], w2[:, e, f, :], start=False,
                                         stop=(f == FF // P - 1))
                last.then_inc(down, 1)

            experts(pe, hidden, out)
            pe.wait_ge(cols, 1)
            pe.transpose(m.psum[0:H, 6, 0:P], m.colp[:, 0:H], m.ident[:, :])
            pe.transpose(m.psum[0:H, 6, P:2 * P], m.flag[:, 0:H], m.ident[:, :]).then_inc(turned, 1)
            pe.wait_ge(cols, 2)
            pe.transpose(m.psum[:, 7, 0:H], m.carry[0:H, 0:P], m.ident[0:H, 0:H]).then_inc(turned, 1)

        @block.scalar
        def _(act):
            act.wait_ge(w_in, 16 * 4)

            def gelus(s, e, first):
                act.wait_ge(up, s + 1)
                if not first:
                    act.wait_ge(down, s - 1)
                for f in range(FF // P):
                    act.activation(hid[:, e % 2, f, :], m.psum[:, 2 * (e % 2) + f // 2, (f % 2) * W:(f % 2) * W + W],
                                   ACT.Gelu, bias=b1[:, e * 4 + f:e * 4 + f + 1]).then_inc(gelu, 1)

            def keep(s, e, first):
                act.wait_ge(down, s + 1)
                if not first:
                    act.wait_ge(y_out[e % 2], past(s, e))
                act.activation(y[:, e % 2, :, :].rearrange("p t d -> p (t d)"), m.psum[:, 4 + e % 2, :], ACT.Copy)\
                   .then_inc(y_c, 1)

            def past(s, e):
                return (s - e % 2) * 8

            experts(act, gelus, keep)

        @block.sync
        def _(sp):
            sp.wait_ge(ones, 1)
            for i in range(4):
                sp.dma_start(a["values"].rearrange("(p l) c -> p (l c)", p=P)[:, i * 1024:(i + 1) * 1024], zero)\
                  .then_inc(zeroed, 16)
            sp.wait_ge(start_t, 1)
            sp.dma_start(a["starts"].rearrange("(t p) -> t p", p=P), turns[0:ST, 0:P]).then_inc(start_out, 16)
            sp.wait_ge(start_out, 16)
            sp.dma_start(turns[0:T, P:2 * P], a["starts"][1:NP + 1].rearrange("(t p) -> t p", p=P)).then_inc(end_in, 16)
            sp.dma_start(w1, a["L0_ffn_W1"].rearrange("e (k p) f -> p e k f", p=P)).then_inc(w_in, 16)
            sp.dma_start(w2, a["L0_ffn_W2"].rearrange("e (f p) d -> p e f d", p=P)).then_inc(w_in, 16)
            sp.dma_start(b1, a["L0_ffn_b1"].rearrange("e (f p) -> p (e f)", p=P),
                         allow_slow_non_contiguous=True).then_inc(w_in, 16)
            sp.dma_start(m.b2[:, :], a["L0_ffn_b2"].rearrange("(o e) d -> o (e d)", o=1)).then_inc(w_in, 16)
            ys = a["y"].rearrange("(t p) e d -> p t e d", p=P)
            with sp.Fori(0, steps) as blk:
                for e in range(X):
                    sp.wait_ge(y_c, blk * X + (e + 1))
                    sp.dma_start(ys[:, bass.ds(blk * NB, NB), e, :], y[:, e % 2, :, :]).then_inc(y_out[e % 2], 16)
            for k in range(2):
                sp.wait_ge(y_out[k], steps * X // 2 * 16)
            sp.wait_ge(value_out, 16 * T)
            sp.dma_start(m.val, a["values"].rearrange("(p l) c -> p l c", p=P)).then_inc(value_in, 16)


def attention(nc, ctx, m, a):
    def sem(name):
        return ctx.enter_context(nc.semaphore(name))

    dve, turned, cols, act_done, shifted = sem("e_dve"), sem("e_turned"), sem("e_cols"), sem("e_act"), sem("shifted")
    peak_ready, peak_out, peak_end_in, peak_patch, peak_patched, peak_in = (
        sem("peak_ready"), sem("peak_out"), sem("peak_end_in"), sem("peak_patch"), sem("peak_patched"), sem("peak_in"))
    sum_ready, sum_out, sum_end_in, sum_patch, sum_patched, sum_in = (
        sem("sum_ready"), sem("sum_out"), sem("sum_end_in"), sem("sum_patch"), sem("sum_patched"), sem("sum_in"))
    own_in, fin_done = sem("own_in"), sem("fin_done")
    fin_in, fin_out = [sem(f"fin_in{k}") for k in range(FB)], [sem(f"fin_out{k}") for k in range(FB)]
    g = m.big[:, 0:L * TW].rearrange("p (l c) -> p l c", c=TW)
    e, peak, same, pre, bar = m.val, m.peak, m.skey[:, :], m.pre, m.bar
    own = m.edge[:, 0:T * WX].rearrange("p (t c) -> p t c", t=T)
    own_h, own_src, own_dst = own[:, :, 0:HE], own[:, :, HE:TW], own[:, :, TW:WX]
    node = m.big[:, L * TW:]

    def by_node(at, n):
        return node[:, at:at + T * n].rearrange("p (t c) -> p t c", t=T)

    top, w_edges, w_own, sums = by_node(0, H), by_node(196, H), by_node(392, H), by_node(588, TW)
    weights = node[:, 196:588]
    own_part, agg, sq = by_node(1568, TW), by_node(2548, HE), by_node(3332, HE)
    w = m.work
    es, score, rank, gate, cmp = (w[:, k * 196:(k + 1) * 196].rearrange("p (t c) -> p t c", t=T) for k in range(5))
    inv = w[:, 980:1176].rearrange("p (t c) -> p t c", t=T)
    par = w[:, 1200:1248].rearrange("p (s c) -> p s c", s=3)
    line, carry, prev, carry2 = m.line, m.carry, m.line2, m.carry2
    ratio = w[:, 1300:1300 + 2 * P]
    colp, flag, back, back2 = m.colp, m.flag, m.back, m.back2
    end_row = w[:, 1600:1604]
    end_g, end_s = w[:, 1604:1605].bitcast(I32), w[:, 1605:1606].bitcast(I32)
    end_peak, new_peak = w[:, 1610:1614], w[:, 1614:1618]
    w_end = w[:, 1620:1628]
    end_sum, new_sum, part = w[:, 1632:1652], w[:, 1652:1672], w[:, 1672:1692]
    marks = w[:, 1700:1732]
    slot = m.big[:, 0:FB * FG * X * D].rearrange("p (b t e d) -> p b t e d", b=FB, t=FG, e=X)
    xs = m.big[:, FB * FG * X * D:FB * FG * (X + 1) * D].rearrange("p (b t d) -> p b t d", b=FB, t=FG)
    ob = m.mid[:, 0:FB * FG * D].rearrange("p (b t d) -> p b t d", b=FB, t=FG)
    groups = (T - 1) // FG

    def spread(ap, n):
        return ap.unsqueeze(2).to_broadcast([P, T, n])

    with nc.Block() as block:
        @block.sync
        def _(sp):
            sp.dma_start(own, a["table"].rearrange("(t p) c -> p t c", p=P)).then_inc(own_in, 16)
            for k, name in enumerate(("L0_ffn_b_gat", "L0_ffn_ln_gamma", "L0_ffn_ln_beta")):
                sp.dma_start(par[:, k, :], a[name].partition_broadcast(P)).then_inc(own_in, 16)
            sp.wait_ge(peak_ready, 1)
            sp.dma_start(a["peaks"].rearrange("(p l) c -> p l c", p=P), peak).then_inc(peak_out, 16)
            sp.wait_ge(sum_ready, 1)
            sp.dma_start(a["sums"].rearrange("(p l) c -> p l c", p=P), g).then_inc(sum_out, 16)
            sp.wait_ge(sum_out, 16)
            ys = a["y"].rearrange("(t p) e d -> p t e d", p=P)
            x2 = a["x2"].rearrange("(t p) d -> p t d", p=P)

            def load(at, b, n=FG):
                sp.dma_start(slot[:, b, 0:n, :, :], ys[:, bass.ds(at, n), :, :]).then_inc(fin_in[b], 16)
                sp.dma_start(xs[:, b, 0:n, :], x2[:, bass.ds(at, n), :]).then_inc(fin_in[b], 16)

            for b in range(FB):
                load(b * FG, b)
            with sp.Fori(0, groups // FB - 1) as i:
                for b in range(FB):
                    sp.wait_ge(fin_done, i * (FB * FG) + (b + 1) * FG)
                    load(i * (FB * FG) + (b + FB) * FG, b)
            sp.wait_ge(fin_done, (groups - FB + 1) * FG)
            load(T - 1, 0, 1)

        @block.gpsimd
        def _(pool):
            def gather(out, table, idx, done):
                pool.indirect_dma_start(out, None, table, bass.IndirectOffsetOnAxis(ap=idx, axis=0)).then_inc(done, 16)

            def patch(table, idx, value, done):
                pool.indirect_dma_start(table, bass.IndirectOffsetOnAxis(ap=idx, axis=0), value, None,
                                        bounds_check=E2 - 1, oob_is_err=False).then_inc(done, 16)

            for k, (table, out, ends, new, stored, ends_in, ready, patched, done) in enumerate((
                    (a["peaks"], top, end_peak, new_peak, peak_out, peak_end_in, peak_patch, peak_patched, peak_in),
                    (a["sums"], sums, end_sum, new_sum, sum_out, sum_end_in, sum_patch, sum_patched, sum_in))):
                pool.wait_ge(stored, 16)
                gather(ends, table, end_g, ends_in)
                pool.wait_ge(ready, 1)
                patch(table, end_s, new, patched)
                pool.wait_ge(patched, 16)
                for t in range(T):
                    gather(out[:, t, :], table, m.end_i[:, t:t + 1], done)

        @block.tensor
        def _(pe):
            pe.wait_ge(cols, 1)
            pe.transpose(m.psum[0:TW, 0, 0:P], colp, m.ident[:, :])
            pe.transpose(m.psum[0:TW, 0, P:2 * P], flag, m.ident[:, :]).then_inc(turned, 1)
            pe.wait_ge(cols, 2)
            pe.transpose(m.psum[:, 1, 0:TW], carry[0:TW, 0:P], m.ident[0:TW, 0:TW]).then_inc(turned, 1)
            pe.wait_ge(cols, 3)
            pe.transpose(m.psum[0:TW, 2, 0:P], colp, m.ident[:, :]).then_inc(turned, 1)
            pe.wait_ge(cols, 4)
            pe.transpose(m.psum[:, 3, 0:TW], carry2[0:TW, 0:P], m.ident[0:TW, 0:TW]).then_inc(turned, 1)

        @block.scalar
        def _(act):
            def exp(n, out, x):
                act.wait_ge(shifted, n)
                act.activation(out, x, ACT.Exp).then_inc(act_done, 1)

            hl = L // 2
            exp(1, g[:, 0:hl, HE:TW], e[:, 0:hl, :])
            exp(2, g[:, hl:L, HE:TW], e[:, hl:L, :])
            exp(3, ratio[0:TW, :], ratio[0:TW, :])
            exp(4, w_end, w_end)
            exp(5, weights, weights)
            act.wait_ge(shifted, 6)
            act.activation(m.rstd, m.var, ACT.Sqrt).then_inc(act_done, 1)
            exp(7, gate, gate)
            tile = a["out"][0:(T - 1) * P, :].rearrange("(t p) d -> p t d", p=P)
            with act.Fori(0, groups // FB) as i:
                for b in range(FB):
                    act.wait_ge(fin_done, i * (FB * FG) + (b + 1) * FG)
                    act.dma_start(tile[:, bass.ds(i * (FB * FG) + b * FG, FG), :], ob[:, b, :, :]).then_inc(fin_out[b], 16)
            act.wait_ge(fin_done, T)
            act.dma_start(a["out"][(T - 1) * P:N, :], ob[0:N - (T - 1) * P, 0, 0, :]).then_inc(fin_out[0], 16)
            for b in range(FB):
                act.wait_ge(fin_out[b], (groups // FB + (b == 0)) * 16)

        @block.vector
        def _(v):
            step = Steps(v, dve)
            hl = L // 2

            signals = iter(range(32))

            def signal(s):
                n = next(signals)
                step.wait()
                v.memset(marks[:, n:n + 1], 0.0).then_inc(s, 1)

            def leaky(out, z):
                return v.scalar_tensor_tensor(out, z, 0.2, z, ALU.mult, ALU.max)

            step(v.tensor_reduce(end_row[:, 0:1], pre, AX.X, ALU.add))
            step(v.tensor_tensor(end_row[:, 0:1], end_row[:, 0:1], m.signs[:, 8:9], ALU.add))
            step.then(v.tensor_scalar(end_g, end_row[:, 0:1], 0.0, None, ALU.max))
            step(v.scalar_tensor_tensor(end_row[:, 1:2], end_row[:, 0:1], float(-BEYOND), same[:, 0:1], ALU.add, ALU.mult))
            step(v.tensor_scalar(end_s, end_row[:, 1:2], float(BEYOND), None, ALU.add))
            step.then(v.tensor_scalar(bar, same, -1.0, -NEG, ALU.add, ALU.mult))
            step(v.tensor_tensor(e, g[:, :, HE:TW], e, ALU.add))
            step(leaky(e, e))
            for h in range(H):
                step.then(v.tensor_tensor_scan(peak[:, :, h], bar, e[:, :, h], NEG, ALU.add, ALU.max))
            step.wait()
            for h in range(H):
                inner = peak[:, 0:L - 1, h][:, ::-1]
                step.then(v.tensor_tensor_scan(inner, bar[:, 1:L][:, ::-1], inner, peak[:, L - 1:L, h],
                                               ALU.add, ALU.max))
            signal(peak_ready)
            for n, (lo, hi) in enumerate(((0, hl), (hl, L))):
                step(v.tensor_tensor(e[:, lo:hi, :], e[:, lo:hi, :], peak[:, lo:hi, :], ALU.subtract))
                signal(shifted)
            step.then(v.tensor_copy(colp[:, 0:HE].rearrange("p (h e) -> p h e", e=X),
                                    peak[:, L - 1, :].unsqueeze(2).to_broadcast([P, H, X])))
            step.then(v.tensor_copy(colp[:, HE:TW], peak[:, L - 1, :]))
            step.then(v.tensor_copy(flag, pre[:, L - 1:L].to_broadcast([P, TW])))
            signal(cols)
            def scale(lo, hi):
                msg = g[:, lo:hi, 0:HE].rearrange("p l (h e) -> p l h e", e=X)
                step.then(v.tensor_tensor(msg, msg, g[:, lo:hi, HE:TW].unsqueeze(3).to_broadcast([P, hi - lo, H, X]),
                                          ALU.mult))

            v.wait_ge(act_done, 1)
            scale(0, hl)
            v.wait_ge(turned, 1)
            last, kept = m.psum[0:TW, 0, 0:P], m.psum[0:TW, 0, P:2 * P]
            c, r = carry[0:TW, :], ratio[0:TW, :]
            step.then(v.tensor_scalar(line[0:TW, :], kept, -1.0, -NEG, ALU.add, ALU.mult))
            step(v.memset(c[:, 0:1], NEG))
            step(v.tensor_tensor_scan(c[:, 1:P + 1], line[0:TW, :], last, NEG, ALU.add, ALU.max))
            signal(cols)
            step.then(v.tensor_tensor(prev[0:TW, :], c[:, 0:P], line[0:TW, :], ALU.add))
            step(v.tensor_tensor(r[:, P:2 * P], last, c[:, 1:P + 1], ALU.subtract))
            step(v.tensor_tensor(r[:, 0:P], prev[0:TW, :], c[:, 1:P + 1], ALU.subtract))
            signal(shifted)
            v.wait_ge(act_done, 2)
            scale(hl, L)
            v.wait_ge(turned, 2)
            step(v.tensor_copy(back, m.psum[:, 1, 0:TW]))
            v.wait_ge(peak_end_in, 16)
            step(v.tensor_tensor(new_peak, end_peak, back[:, HE:TW], ALU.max))
            signal(peak_patch)
            step.then(v.tensor_tensor(w_end[:, 0:H], end_peak, new_peak, ALU.subtract))
            step.then(v.tensor_tensor(w_end[:, H:2 * H], back[:, HE:TW], new_peak, ALU.subtract))
            signal(shifted)
            for k in range(TW):
                step.then(v.tensor_tensor_scan(g[:, :, k], same, g[:, :, k], 0.0, ALU.mult, ALU.add))
            step.wait()
            step.then(v.tensor_copy(colp, g[:, L - 1, :]))
            signal(sum_ready)
            signal(cols)
            v.wait_ge(act_done, 3)
            v.wait_ge(turned, 3)
            step.then(v.memset(carry2[0:TW, 0:1], 0.0))
            step(v.tensor_tensor(prev[0:TW, :], m.psum[0:TW, 2, 0:P], r[:, P:2 * P], ALU.mult))
            step(v.tensor_tensor_scan(carry2[0:TW, 1:P + 1], r[:, 0:P], prev[0:TW, :], 0.0, ALU.mult, ALU.add))
            signal(cols)
            v.wait_ge(turned, 4)
            v.wait_ge(act_done, 4)
            step(v.tensor_copy(back2, m.psum[:, 3, 0:TW]))

            def by_column(out, x, weight):
                step.then(v.tensor_tensor(out[:, 0:HE].rearrange("p (h e) -> p h e", e=X),
                                          x[:, 0:HE].rearrange("p (h e) -> p h e", e=X),
                                          weight.unsqueeze(2).to_broadcast([P, H, X]), ALU.mult))
                step.then(v.tensor_tensor(out[:, HE:TW], x[:, HE:TW], weight, ALU.mult))

            by_column(part, back2, w_end[:, H:2 * H])
            v.wait_ge(sum_end_in, 16)
            by_column(new_sum, end_sum, w_end[:, 0:H])
            step.wait()
            step(v.tensor_tensor(new_sum, new_sum, part, ALU.add))
            signal(sum_patch)
            v.wait_ge(own_in, 64)
            step(v.tensor_tensor(es, own_src, own_dst, ALU.add))
            step(leaky(es, es))
            v.wait_ge(peak_in, 16 * T)
            step(v.tensor_tensor(top, top, spread(m.some, H), ALU.mult))
            step(v.tensor_scalar(m.tmp_s, m.some, -1.0, -NEG, ALU.add, ALU.mult))
            step(v.tensor_tensor(top, top, spread(m.tmp_s, H), ALU.add))
            step(v.tensor_tensor(cmp, top, es, ALU.max))
            step.then(v.tensor_tensor(w_edges, top, cmp, ALU.subtract))
            step.then(v.tensor_tensor(w_own, es, cmp, ALU.subtract))
            signal(shifted)
            v.wait_ge(act_done, 5)

            def heads(ap):
                return ap.rearrange("p t (h e) -> p t h e", e=X)

            def each(ap):
                return ap.unsqueeze(3).to_broadcast([P, T, H, X])

            step.then(v.tensor_tensor(heads(own_part[:, :, 0:HE]), heads(own_h), each(w_own), ALU.mult))
            step(v.tensor_scalar(own_part[:, :, HE:TW], w_own, 1e-16, None, ALU.add))
            v.wait_ge(sum_in, 16 * T)
            step.then(v.tensor_tensor(heads(agg), heads(sums[:, :, 0:HE]), each(w_edges), ALU.mult))
            step(v.tensor_tensor(inv, sums[:, :, HE:TW], w_edges, ALU.mult))
            step.then(v.tensor_tensor(agg, agg, own_part[:, :, 0:HE], ALU.add))
            step(v.tensor_tensor(inv, inv, own_part[:, :, HE:TW], ALU.add))
            step(v.reciprocal(inv, inv))
            step(v.tensor_tensor(heads(agg), heads(agg), each(inv), ALU.mult))

            def param(k):
                return par[:, k, :].unsqueeze(1).to_broadcast([P, T, HE])

            step(v.tensor_tensor(agg, agg, param(0), ALU.add))
            step(v.tensor_reduce(m.mean, agg, AX.X, ALU.add))
            step(v.tensor_scalar(m.mean, m.mean, 1.0 / HE, None, ALU.mult))
            step(v.tensor_tensor(agg, agg, spread(m.mean, HE), ALU.subtract))
            step(v.tensor_tensor(sq, agg, agg, ALU.mult))
            step(v.tensor_reduce(m.var, sq, AX.X, ALU.add))
            step(v.tensor_scalar(m.var, m.var, 1.0 / HE, EPS, ALU.mult, ALU.add))
            signal(shifted)
            v.wait_ge(act_done, 6)
            inverse_root(v, m, step)
            step(v.tensor_tensor(agg, agg, spread(m.rstd, HE), ALU.mult))
            step(v.tensor_tensor(agg, agg, param(1), ALU.mult))
            step(v.tensor_tensor(agg, agg, param(2), ALU.add))
            step(v.tensor_reduce(score, agg.rearrange("p t (h e) -> p t e h", e=X), AX.X, ALU.add))
            step(v.tensor_scalar(score, score, 1.0 / H, None, ALU.mult))
            step(v.tensor_reduce(m.mean, score, AX.X, ALU.max))
            step(v.tensor_tensor(gate, score, spread(m.mean, X), ALU.subtract))
            signal(shifted)
            step(v.memset(rank, 0.0))
            pairs = [(lo, hi) for hi in range(1, X) for lo in range(hi)]
            wins = sq.rearrange("p t c -> p c t")
            for k, (lo, hi) in enumerate(pairs):
                step.then(v.tensor_tensor(wins[:, k, :], score[:, :, lo], score[:, :, hi], ALU.is_ge))
            step.wait()
            for k, (lo, hi) in enumerate(pairs):
                step.then(v.tensor_tensor(rank[:, :, hi], rank[:, :, hi], wins[:, k, :], ALU.add))
                step.wait()
                step(v.scalar_tensor_tensor(rank[:, :, lo], wins[:, k, :], -1.0, rank[:, :, lo], ALU.mult, ALU.add))
            for lo in range(X - 1):
                step.then(v.tensor_scalar(rank[:, :, lo], rank[:, :, lo], float(X - 1 - lo), None, ALU.add))
            step.wait()
            v.wait_ge(act_done, 7)
            step(v.scalar_tensor_tensor(gate, rank, 2.0, gate, ALU.is_lt, ALU.mult))
            step(v.tensor_reduce(m.var, gate, AX.X, ALU.add))
            step(v.reciprocal(m.var, m.var))
            step(v.tensor_tensor(gate, gate, spread(m.var, X), ALU.mult))

            def combine(t, b, k, x):
                return v.scalar_tensor_tensor(ob[:, b, k, :], slot[:, b, k, x, :], gate[:, bass.ds(t, 1), x],
                                              (xs if x == 0 else ob)[:, b, k, :], ALU.mult, ALU.add)

            base, per = step.n, (X - 1) * FG
            with v.Fori(0, groups // FB) as i:
                for b in range(FB):
                    v.wait_ge(fin_in[b], i * 32 + 32)
                    v.wait_ge(fin_out[b], i * 16)
                    for x in range(X):
                        if x:
                            v.wait_ge(dve, i * (per * FB) + (base + b * per + x * FG))
                        for k in range(FG):
                            combine(i * (FB * FG) + (b * FG + k), b, k, x).then_inc(dve if x < X - 1 else fin_done, 1)
            step.n += groups * per
            v.wait_ge(fin_in[0], (groups // FB + 1) * 32)
            v.wait_ge(fin_out[0], groups // FB * 16)
            for x in range(X - 1):
                step(combine(T - 1, 0, 0, x))
            combine(T - 1, 0, 0, X - 1).then_inc(fin_done, 1)


def program(nc, a):
    ctx = ExitStack()
    m = Mem()
    with ctx:
        allocate(nc, ctx, m)
        load_and_normalise(nc, ctx, m, a)
        gather_and_sort(nc, ctx, m, a)
        first_layer(nc, ctx, m, a)
        gather_and_experts(nc, ctx, m, a)
        attention(nc, ctx, m, a)


def constants():
    p = np.arange(P)

    def sign(k):
        return np.where((p >> (k - LOG_L)) & 1, -1.0, 1.0)

    last = LOG_L + 7
    signs = [sign(LOG_L)] + [sign(k) * sign(k - 1) for k in range(LOG_L + 1, last)] + [sign(last - 1), p * L - 1.0]
    nodes = np.arange(ST)[None, :] * P + p[:, None]
    return {
        "c_ident": np.eye(P, dtype=np.float32),
        "c_iota": np.ascontiguousarray(np.broadcast_to(p.astype(np.float32), (P, P))),
        "c_signs": np.stack(signs, axis=1).astype(np.float32),
        "c_nodekey": ((nodes << SHIFT) | KEY_BASE).astype(np.int32).view(np.float32),
    }


SCRATCH = {"feat": ((NP, D), F32), "rng_i": ((2, GP), I32), "rng_f": ((GP,), F32), "keys": ((E2,), F32),
           "starts": ((ST * P,), F32), "x2": ((NP, D), F32), "table": ((NP, WX), F32), "values": ((E2, H), F32), "subs": ((P, L // SUB), F32),
           "peaks": ((E2, H), F32), "sums": ((E2, TW), F32), "y": ((ST * P, X, D), F32)}
_INS = ["x", "src", "dst", "edge_weight", "L0_gnn_W", "L0_gnn_b", "L0_ffn_W_gat", "L0_ffn_att_src", "L0_ffn_att_dst",
        "L0_ffn_b_gat", "L0_ffn_ln_gamma", "L0_ffn_ln_beta", "L0_ffn_W1", "L0_ffn_b1", "L0_ffn_W2", "L0_ffn_b2",
        "L0_ffn_edge_index"]


def kernel(**inputs):
    import concourse.bacc as bacc
    from concourse.bass_utils import run_bass_kernel_spmd

    nc = bacc.Bacc("TRN2", target_bir_lowering=False, num_devices=1)
    arrays, a = {}, {}
    for name, value in [(n, inputs[n]) for n in _INS] + list(constants().items()):
        value = np.ascontiguousarray(value)
        arrays[f"in_{name}"] = value
        a[name] = nc.dram_tensor(f"in_{name}", value.shape, mybir.dt.from_np(value.dtype), kind="ExternalInput").ap()
    for name, (shape, dt) in SCRATCH.items():
        a[name] = nc.dram_tensor(f"s_{name}", list(shape), dt, kind="Internal").ap()
    a["out"] = nc.dram_tensor("out_0", [N, D], F32, kind="ExternalOutput").ap()
    program(nc, a)
    return run_bass_kernel_spmd(nc, [arrays], core_ids=[0]).results[0]["out_0"]
```

```python
from contextlib import ExitStack

import numpy as np

import concourse.bass as bass
from concourse import mybir

F32 = mybir.dt.float32
I32 = mybir.dt.int32
ALU = mybir.AluOpType
ACT = mybir.ActivationFunctionType
AX = mybir.AxisListType

P = 128
N = 6250
D = 256
T = -(-N // P)
NP = T * P
E1 = 200000
CH = -(-E1 // P)
GC = 4
BODY = 8
NG = -(-CH // (GC * BODY)) * BODY
EB = -(-CH // P)
CP = EB * P
GP = CP // GC
PAD_DST = 8191
E2 = 131072
L = E2 // P
LOG_L = L.bit_length() - 1
SHIFT = 13
KEY_BASE = 0x38000000
KEY_END = float(np.array((N << SHIFT) | KEY_BASE, np.int32).view(np.float32))
HE = 16
H = 4
X = 4
TW = HE + H
WX = HE + 2 * H
FF = 512
EPS = 1e-5
SLOTS = BODY * GC
ST = T + 1
NB = 2
LEAST = 12
GB = 16
NEG = -1.0e38
NOTHING = -1.0e30
FB = 6
QL = 256
WHOLE = (L - QL) // GB
FG = 4
XT = 7
SUB = 32
RING = 4
AW = D + 1


class Steps:

    def __init__(self, eng, sem, base=0):
        self.eng, self.sem, self.base, self.n = eng, sem, base, 0

    def then(self, ins):
        ins.then_inc(self.sem, 1)
        self.n += 1

    def wait(self):
        self.eng.wait_ge(self.sem, self.base + self.n)

    def __call__(self, ins):
        self.then(ins)
        self.wait()


class Mem:
    pass


def moments(v, m, sem, x, lo, hi):
    with v.Fori(lo, hi) as t:
        v.bn_stats(m.stats[:, bass.ds(t, 1), :].rearrange("p o s -> p (o s)"),
                   x[:, bass.ds(t, 1), 0:D].rearrange("p o d -> p (o d)")).then_inc(sem, 1)


def statistics(v, m, step):
    step.n += T
    step.wait()
    step.then(v.tensor_tensor(m.mean, m.stats[:, :, 1], m.stats[:, :, 4], ALU.add))
    step.then(v.tensor_tensor(m.tmp_s, m.stats[:, :, 1], m.stats[:, :, 4], ALU.subtract))
    step(v.tensor_tensor(m.var, m.stats[:, :, 2], m.stats[:, :, 5], ALU.add))
    step.then(v.tensor_scalar(m.mean, m.mean, 0.5, None, ALU.mult))
    step.then(v.tensor_scalar(m.var, m.var, 1.0 / D, EPS, ALU.mult, ALU.add))
    step(v.scalar_tensor_tensor(m.tmp_s, m.tmp_s, 0.25, m.tmp_s, ALU.mult, ALU.mult))
    step(v.tensor_tensor(m.var, m.var, m.tmp_s, ALU.add))


STATISTICS = T + 7


def inverse_root(v, m, step, lo=0, hi=T):
    r, var, tmp = (k[:, lo:hi] for k in (m.rstd, m.var, m.tmp_s))
    step(v.reciprocal(r, r))
    step(v.tensor_tensor(tmp, r, r, ALU.mult))
    step(v.tensor_tensor(tmp, tmp, var, ALU.mult))
    step(v.tensor_scalar(tmp, tmp, -0.5, 1.5, ALU.mult, ALU.add))
    step(v.tensor_tensor(r, r, tmp, ALU.mult))


INVERSE_ROOT = 5
DVE_VAR = 3 + STATISTICS
DVE_ROOT = DVE_VAR + INVERSE_ROOT + 1


def allocate(nc, ctx, m):
    def sb(name, shape, dt=F32):
        return ctx.enter_context(nc.sbuf_tensor(name, shape, dt))

    m.big = sb("big", [P, T * D + T * AW])
    m.mid = sb("mid", [P, ST * D])
    m.edge = sb("edge", [P, 3 * CP])
    m.skey = sb("skey", [P, L])
    m.ssrc = sb("ssrc", [P, L], I32)
    m.wgnn = sb("wgnn", [P, 4, D])
    m.b2 = sb("b2", [1, X * D])
    m.ident = sb("ident", [P, P])
    m.iota = sb("iota", [P, P])
    m.iota_x = sb("iota_x", [P, P])
    m.signs = sb("signs", [P, 9])
    m.nodekey = sb("nodekey", [P, ST])
    m.small = sb("small", [P, 24 * 64])
    m.regs = sb("regs", [1, 2, GP], I32)
    m.idx = sb("idx", [P, 4, SLOTS // 2], I32)
    m.work = sb("work", [P, 3072])
    m.psum = ctx.enter_context(nc.psum_tensor("ps", [P, 8, 512], F32))

    m.feat = m.big[:, 0:T * D].rearrange("p (t d) -> p t d", t=T)
    m.acc = m.big[:, T * D:].rearrange("p (t d) -> p t d", t=T)
    m.acc_flat = m.big[:, T * D:]
    m.esrc = m.edge[:, 0:CP].bitcast(I32)
    m.edst = m.edge[:, CP:2 * CP]
    m.ewt = m.edge[:, 2 * CP:3 * CP]
    m.key = [m.mid[:, 10496 + k * L:10496 + (k + 1) * L] for k in range(2)]

    def small(k, n=ST):
        return m.small[:, 64 * k:64 * k + n]

    m.mean, m.var, m.rstd, m.tmp_s = small(0, T), small(1, T), small(2, T), small(15, T)
    m.start, m.end, m.some, m.row, m.cnt = small(3), small(4, T), small(5, T), small(8), small(9)
    m.row_i = small(6).bitcast(I32)
    m.start_i, m.end_i = small(6, T).bitcast(I32), small(7, T).bitcast(I32)
    m.stats = m.small[:, 640:640 + 6 * T].rearrange("p (t s) -> p t s", s=6)
    m.prev = m.small[:, 64 * 16:64 * 16 + 4]
    m.length, m.length_i = m.small[:, 64 * 16 + 4:64 * 16 + 8], m.small[:, 64 * 16 + 8:64 * 16 + 10].bitcast(I32)
    m.rows = m.mid[:, 0:SLOTS * D].rearrange("p (s d) -> p s d", s=SLOTS)
    m.wrows = m.mid[:, SLOTS * D:SLOTS * D + 2 * GC * AW].rearrange("p (b c d) -> p b c d", b=2, c=GC)
    m.hot = m.work[:, 0:3 * GC * P].rearrange("p (b c n) -> p b c n", b=3, c=GC)
    m.seek = m.edge[:, 3072:3072 + ST * SUB].rearrange("p (t s) -> p t s", t=ST)
    m.t0b = m.mid[:, 0:GP]
    m.shift, m.tmp_s2 = small(3, T), m.small[:, 64 * 22:64 * 22 + ST]
    m.val = m.mid[:, 0:L * H].rearrange("p (l c) -> p l c", c=H)
    m.peak = m.mid[:, L * H:2 * L * H].rearrange("p (l c) -> p l c", c=H)
    m.pre, m.bar = m.mid[:, 8192:9216], m.mid[:, 9216:10240]
    last = m.mid[:, 10240:]
    m.line, m.carry, m.line2, m.carry2 = last[:, 0:P], last[:, P:2 * P + 1], last[:, 300:300 + P], last[:, 440:441 + P]
    m.colp, m.flag, m.back, m.back2 = (last[:, 600 + 32 * k:600 + 32 * k + TW] for k in range(4))
    m.adst = m.small[:, 64 * 18:64 * 18 + H * T].rearrange("p (t h) -> p t h", t=T)


def load_and_normalise(nc, ctx, m, a):
    def sem(name):
        return ctx.enter_context(nc.semaphore(name))

    x_in = m.loaded = [sem(f"x_in{c}") for c in range(T // XT)]
    e_in, c_in, w_in, feat_v, feat_a = sem("e_in"), sem("c_in"), sem("w_in"), sem("feat_v"), sem("feat_a")
    pads, dve, sq, chunk_t, chunk_c = sem("pads"), sem("a_dve"), sem("a_sqrt"), sem("chunk_t"), sem("chunk_c")
    edge_f, feat_out, rng_ready, rng_out, rng_in = (sem("edge_f"), sem("feat_out"), sem("rng_ready"),
                                                   sem("rng_out"), sem("rng_in"))
    w_t, w_c = sem("w_t"), sem("w_c")
    full, rest = E1 // P, E1 % P
    whole, tail = EB - 1, full - (EB - 1) * P
    raw = [m.mid[:, k * CP:(k + 1) * CP] for k in range(3)]
    src_raw, dst_raw = raw[0].bitcast(I32), raw[1].bitcast(I32)
    src_f, dst_f, tmp = (m.mid[:, k * CP:(k + 1) * CP] for k in (3, 4, 5))
    wraw = m.skey[:, 0:1024].rearrange("p (a k) -> p a k", a=2)
    cmin, cmax = m.small[:, 64 * 20:64 * 20 + EB], m.small[:, 64 * 20 + EB:64 * 20 + 2 * EB]
    gi = m.small[0:EB, 64 * 21:64 * 21 + 64].bitcast(I32)
    gf = m.small[0:EB, 64 * 22:64 * 22 + 64]
    gb = m.small[0:EB, 64 * 23:64 * 23 + 32]

    with nc.Block() as block:
        @block.sync
        def _(sp):
            sp.wait_ge(pads, 4)
            for r, name in ((src_raw, "src"), (dst_raw, "dst"), (raw[2], "edge_weight")):
                v = r.rearrange("p (b e) -> p b e", b=EB)
                s = a[name]
                sp.dma_start(v[:, 0:whole, :], s[0:whole * P * P].rearrange("(b p e) -> p b e", b=whole, p=P))\
                    .then_inc(e_in, 16)
                sp.dma_start(v[0:tail, whole, :], s[whole * P * P:full * P].rearrange("(p e) -> p e", e=P))\
                    .then_inc(e_in, 16)
                sp.dma_start(v[tail:tail + 1, whole, 0:rest], s[full * P:E1].rearrange("(p e) -> p e", p=1))\
                    .then_inc(e_in, 16)
            xt = a["x"][0:(T - 1) * P, :].rearrange("(t p) d -> p t d", p=P)
            for c in range(T // XT):
                hi = min((c + 1) * XT, T - 1)
                sp.dma_start(m.feat[:, c * XT:hi, :], xt[:, c * XT:hi, :]).then_inc(x_in[c], 16)
            sp.dma_start(m.feat[0:N - (T - 1) * P, T - 1, :], a["x"][(T - 1) * P:N, :]).then_inc(x_in[-1], 16)
            sp.wait_ge(rng_ready, 1)
            sp.dma_start(a["rng_i"].rearrange("k (b g) -> b k g", b=EB), gi.rearrange("b (k g) -> b k g", k=2))\
                .then_inc(rng_out, 16)
            sp.dma_start(a["rng_f"].rearrange("(b g) -> b g", b=EB), gb).then_inc(rng_out, 16)
            sp.wait_ge(rng_out, 32)
            sp.dma_start(m.regs[0:1, :, :], a["rng_i"].rearrange("(o k) g -> o k g", o=1)).then_inc(rng_in, 16)
            sp.dma_start(m.t0b, a["rng_f"].partition_broadcast(P)).then_inc(rng_in, 16)
            sp.wait_ge(rng_in, 32)

        @block.gpsimd
        def _(pool):
            fo = a["feat"].rearrange("(t p) d -> p t d", p=P)
            for c in range(T // XT):
                if c % 2 == 0:
                    pool.wait_ge(feat_v, (c // 2 + 1) * XT)
                else:
                    pool.wait_ge(feat_a, (c // 2 + 1) * XT)
                pool.dma_start(fo[:, c * XT:(c + 1) * XT, :], m.feat[:, c * XT:(c + 1) * XT, :]).then_inc(feat_out, 16)
            pool.wait_ge(feat_out, T // XT * 16)

        @block.scalar
        def _(act):
            for dst, name in ((m.ident, "c_ident"), (m.iota, "c_iota"), (m.signs, "c_signs"),
                              (m.nodekey, "c_nodekey")):
                act.dma_start(dst[:, :], a[name]).then_inc(c_in, 16)
            act.dma_start(wraw, a["L0_gnn_W"].rearrange("(a o) k -> o a k", a=2)).then_inc(w_in, 16)
            act.wait_ge(w_t, 1)
            for b in range(2):
                act.activation(m.wgnn[:, 2 * b:2 * b + 2, :].rearrange("p k o -> p (k o)"), m.psum[:, b, :],
                               ACT.Copy).then_inc(w_c, 1)
            for b in range(EB):
                act.wait_ge(chunk_t, b + 1)
                for k, dst in enumerate((m.esrc, m.edst, m.ewt)):
                    act.activation(dst[:, b * P:(b + 1) * P], m.psum[:, 4 + b % 4, k * P:(k + 1) * P], ACT.Copy)\
                       .then_inc(chunk_c, 1)
            act.wait_ge(dve, DVE_VAR)
            act.activation(m.rstd, m.var, ACT.Sqrt).then_inc(sq, 1)
            act.wait_ge(dve, DVE_ROOT)
            for c in range(1, T // XT, 2):
                with act.Fori(c * XT, (c + 1) * XT) as t:
                    tile = m.feat[:, bass.ds(t, 1), :].rearrange("p o d -> p (o d)")
                    act.activation(tile, tile, ACT.Identity, scale=m.rstd[:, bass.ds(t, 1)],
                                   bias=m.shift[:, bass.ds(t, 1)]).then_inc(feat_a, 1)

        @block.tensor
        def _(pe):
            pe.wait_ge(c_in, 64)
            pe.wait_ge(w_in, 16)
            for k in range(4):
                for o in range(2):
                    last = pe.transpose(m.psum[:, k // 2, (k % 2) * D + o * P:(k % 2) * D + (o + 1) * P],
                                        wraw[:, o, k * P:(k + 1) * P], m.ident[:, :])
            last.then_inc(w_t, 1)
            pe.wait_ge(edge_f, 2)
            pe.wait_ge(dve, 3)
            pe.transpose(m.psum[0:EB, 3, 0:P], cmin, m.ident[:, :])
            pe.transpose(m.psum[0:EB, 3, P:2 * P], cmax, m.ident[:, :]).then_inc(w_t, 1)
            pe.wait_ge(e_in, 9 * 16)
            for b in range(EB):
                if b >= 4:
                    pe.wait_ge(chunk_c, (b - 3) * 3)
                for k, s in enumerate((src_f, dst_f, raw[2])):
                    last = pe.transpose(m.psum[:, 4 + b % 4, k * P:(k + 1) * P], s[:, b * P:(b + 1) * P],
                                        m.ident[:, :])
                last.then_inc(chunk_t, 1)

        @block.vector
        def _(v):
            v.memset(m.feat[:, T - 1, :], 0.0).then_inc(pads, 1)
            v.memset(src_raw[:, whole * P:], 0).then_inc(pads, 1)
            v.memset(dst_raw[:, whole * P:], PAD_DST).then_inc(pads, 1)
            v.memset(raw[2][:, whole * P:], 0.0).then_inc(pads, 1)
            step = Steps(v, dve)
            v.wait_ge(e_in, 9 * 16)
            v.tensor_copy(src_f, src_raw).then_inc(edge_f, 1)
            step(v.tensor_copy(dst_f, dst_raw))
            step.then(v.tensor_reduce(cmin, dst_f.rearrange("p (b e) -> p b e", b=EB), AX.X, ALU.min))
            step(v.scalar_tensor_tensor(tmp, dst_f, float(NP), dst_f, ALU.is_lt, ALU.mult))
            v.tensor_reduce(cmax, tmp.rearrange("p (b e) -> p b e", b=EB), AX.X, ALU.max).then_inc(edge_f, 1)
            for c in range(T // XT):
                v.wait_ge(x_in[c], 16 if c < T // XT - 1 else 32)
                moments(v, m, dve, m.feat, c * XT, (c + 1) * XT)
            statistics(v, m, step)
            assert step.n == DVE_VAR
            v.wait_ge(sq, 1)
            inverse_root(v, m, step)
            step(v.scalar_tensor_tensor(m.shift, m.mean, -1.0, m.rstd, ALU.mult, ALU.mult))
            assert step.n == DVE_ROOT
            for c in range(0, T // XT, 2):
                with v.Fori(c * XT, (c + 1) * XT) as t:
                    tile = m.feat[:, bass.ds(t, 1), :].rearrange("p o d -> p (o d)")
                    v.tensor_scalar(tile, tile, m.mean[:, bass.ds(t, 1)], m.rstd[:, bass.ds(t, 1)],
                                    ALU.subtract, ALU.mult).then_inc(feat_v, 1)
            v.wait_ge(w_t, 2)
            for k in range(2):
                step.then(v.tensor_reduce(gf[:, 32 * k:32 * k + 32],
                                          m.psum[0:EB, 3, k * P:(k + 1) * P].rearrange("b (g c) -> b g c", c=GC),
                                          AX.X, (ALU.min, ALU.max)[k]))
            step.wait()
            step(v.tensor_copy(gi, gf))
            step(v.tensor_scalar(gi, gi, 7, None, ALU.arith_shift_right))
            step(v.tensor_scalar(gi, gi, T - 1, None, ALU.min))
            step(v.tensor_tensor(gi[:, 32:64], gi[:, 32:64], gi[:, 0:32], ALU.max))
            step(v.tensor_tensor(gi[:, 32:64], gi[:, 32:64], gi[:, 0:32], ALU.subtract))
            v.tensor_scalar(gb, gi[:, 0:32], float(P), None, ALU.mult).then_inc(rng_ready, 1)
            v.wait_ge(chunk_c, 3 * EB)
            v.wait_ge(rng_in, 32)
            step(v.tensor_tensor(m.edst.rearrange("p (g c) -> p g c", c=GC),
                                 m.edst.rearrange("p (g c) -> p g c", c=GC),
                                 m.t0b.unsqueeze(2).to_broadcast([P, GP, GC]), ALU.subtract))




def sort_plan():
    slots, cur, n = [], 1, 5

    def add(kind, arg, steps):
        nonlocal cur, n
        slots.append((kind, cur, arg, n))
        cur, n = 1 - cur, n + steps

    for k in range(1, LOG_L + 1):
        add("mirror", 1 << (k - 1), 2)
        for j in range(k - 2, -1, -1):
            add("merge", 1 << j, 2)
    for k in range(1, P.bit_length()):
        add("sign", k, 1)
        add("turn", 0, 0)
        for j in range(k - 1, -1, -1):
            add("merge", 1 << j, 2)
        add("turn", 0, 0)
        for j in range(LOG_L - 1, -1, -1):
            add("merge", 1 << j, 2)
    return slots, cur, n


def turns_before(n):
    return sum(kind == "turn" and at < n for kind, _, _, at in PLAN)


PLAN, SORTED, SORT_STEPS = sort_plan()
BELOW = L // P
FINISH = ["first", "count"] + ["below"] * (-(-ST // BELOW))
LATE = ["sources", "same"]
SPECIAL = -(-(len(PLAN) + len(FINISH)) // BODY)
BEYOND = 1 << 20


def gather_and_sort(nc, ctx, m, a):
    def sem(name):
        return ctx.enter_context(nc.semaphore(name))

    idx_ready, weighted, hot_ready, sums_ready = sem("idx_ready"), sem("weighted"), sem("hot_ready"), sem("sums_ready")
    group_done, hot_x, sums_x = sem("group_done"), sem("hot_x"), sem("sums_x")
    row_in = m.gathered = [sem(f"gathered{k}") for k in range(SLOTS)]
    sorting, turned, turned_c, e2_in, start_sem = (sem("sorting"), sem("turned"), sem("turned_c"), sem("e2_in"),
                                                   sem("b_setup"))
    first_keys, first_turned, length_ready, bias_in = sem("first_keys"), sem("first_turned"), sem("length_ready"), sem("bias_in")
    key_out, sub_out, row_out, rows_in = sem("key_out"), sem("sub_out"), sem("row_out"), sem("rows_in")
    f_c, f_t, f_tc, f_l, f_z = sem("f_c"), sem("f_t"), sem("f_tc"), sem("f_l"), sem("f_z")
    fin, ft = m.work[:, 1536:1792], m.work[:, 1792:2048]
    bias = m.work[:, 2048:2304]
    subs = m.work[:, 2304:2304 + L // SUB]
    firsts, ones, valid = m.work[:, 2400:2528], m.work[:, 2528:2656], m.work[:, 2656:2657]
    xstep = sem("xstep")
    iters = NG // BODY
    assert iters == T and iters % 2 == 1

    def slot(it, g):
        if not isinstance(it, int):
            return "", 0, 0, 0
        at = it * BODY + g
        if at < len(PLAN):
            return PLAN[at]
        at -= len(PLAN)
        kinds = FINISH[at:at + 1] or (LATE[g:g + 1] if it == iters - 1 else [])
        return (kinds or [""])[0], 0, 0, 0

    def iterations(eng, body, kinds):
        at = 0
        while at < iters:
            until = at
            while until < SPECIAL and not any(slot(until, g)[0] in kinds for g in range(BODY)):
                until += 1
            if until == SPECIAL:
                until = iters - 1
            if at == 0 or until - at < 2:
                body(at, at == 0)
                at += 1
            else:
                with eng.Fori(at, until) as it:
                    body(it, False)
                at = until

    with nc.Block() as block:
        @block.gpsimd
        def _(pool):
            def body(it, odd, first):
                for k in range(SLOTS):
                    if k % half == 0:
                        q = 2 * odd + k // half
                        stage(it * 2 + (k // half + 1), (q + 1) % 4)
                        pool.wait_ge(idx_ready, it * 2 + (k // half + 1))
                    if not first:
                        pool.wait_ge(weighted, used)
                        pool.reg_add(used, used, 1)
                    pool.indirect_dma_start(m.rows[:, k, :], None, a["feat"],
                                            bass.IndirectOffsetOnAxis(ap=m.idx[:, q, k % half:k % half + 1], axis=0))\
                        .then_inc(row_in[k], 16)

            def stage(n, q):
                pool.tensor_copy(m.idx[:, q, :], m.esrc[:, bass.ds(n * half, half)]).then_inc(idx_ready, 1)

            half = SLOTS // 2
            used = pool.alloc_register("used")
            pool.reg_mov(used, 1)
            stage(0, 0)
            body(0, 0, True)
            with pool.Fori(0, iters // 2) as i:
                for n in range(2):
                    body(i * 2 + (n + 1), 1 - n, False)

        @block.scalar
        def _(act):
            act.wait_ge(start_sem, 2)

            def body(it, first):
                act.activation(fin, m.feat[:, bass.ds(it, 1), :].rearrange("p o d -> p (o d)"), ACT.Copy).then_inc(f_c, 1)
                for k in range(SLOTS):
                    g = k // GC
                    if k == 4 * GC:
                        act.wait_ge(f_t, it + 1)
                        if not first:
                            act.wait_ge(f_l, it)
                        act.activation(ft, m.psum[:, 6, 0:D], ACT.Copy).then_inc(f_tc, 1)
                    if k % GC == 0 and not (first and g < 2):
                        act.wait_ge(group_done, it * BODY + (g - 1))
                    act.wait_ge(row_in[k], it * 16 + 16)
                    act.activation(m.wrows[:, g % 2, k % GC, 0:D], m.rows[:, k, :], ACT.Copy,
                                   scale=m.ewt[:, bass.ds(it * SLOTS + k, 1)]).then_inc(weighted, 1)
                    kind, cur, _, n = slot(it, g)
                    if kind == "turn" and k % GC == GC - 1:
                        act.wait_ge(turned, turns_before(n) + 1)
                        act.activation(m.key[1 - cur], m.psum[:, 4:6, :].rearrange("p b n -> p (b n)"), ACT.Copy)\
                           .then_inc(turned_c, 1)
            iterations(act, body, ("turn",))

        @block.tensor
        def _(pe):
            extra = pe.alloc_register("extra_pe")
            pe.reg_mov(extra, 0)

            def sums(out, hot, buf):
                for c in range(GC):
                    last = pe.matmul(out, m.hot[:, hot, c, :], m.wrows[:, buf, c, :], start=(c == 0), stop=(c == GC - 1))
                return last

            def body(it, first):
                for g in range(BODY):
                    if g == 2:
                        pe.wait_ge(f_c, it + 1)
                        if not first:
                            pe.wait_ge(f_tc, it)
                        for k in range(2):
                            last = pe.transpose(m.psum[:, 6, k * P:(k + 1) * P], fin[:, k * P:(k + 1) * P], m.ident[:, :])
                        last.then_inc(f_t, 1)
                    if g == 6:
                        pe.wait_ge(f_tc, it + 1)
                        if not first:
                            pe.wait_ge(f_z, it)
                        for k in range(2):
                            last = pe.matmul(m.psum[:, 7, 0:D], ft[:, k * P:(k + 1) * P], m.wgnn[:, k, :],
                                             start=(k == 0), stop=(k == 1))
                        last.then_inc(f_l, 1)
                    kind, cur, _, n = slot(it, g)
                    if kind == "turn":
                        pe.wait_ge(sorting, n)
                        if turns_before(n):
                            pe.wait_ge(turned_c, turns_before(n))
                        for b in range(L // P):
                            last = pe.transpose(m.psum[:, 4 + b // 4, (b % 4) * P:(b % 4 + 1) * P],
                                                m.key[cur][:, b * P:(b + 1) * P], m.ident[:, :])
                        last.then_inc(turned, 1)
                    if kind == "count":
                        pe.wait_ge(first_keys, 1)
                        pe.transpose(m.psum[:, 3, 0:P], firsts, m.ident[:, :])
                        pe.matmul(m.psum[:, 3, P:P + 1], ones, valid, start=True, stop=True).then_inc(first_turned, 1)
                    pe.wait_ge(weighted, it * SLOTS + (g + 1) * GC)
                    pe.wait_ge(hot_ready, it * BODY + (g + 1))
                    if not (first and g < 2):
                        pe.wait_ge(group_done, it * BODY + (g - 1))
                    sums(m.psum[:, g % 2, 0:AW], g % 2, g % 2).then_inc(sums_ready, 1)
                    more = pe.value_load(m.regs[0:1, 1, bass.ds(it * BODY + g, 1)], min_val=0, max_val=T - 1)
                    with pe.If(more > 0):
                        with pe.Fori(0, more):
                            pe.reg_add(extra, extra, 1)
                            pe.wait_ge(hot_x, pe.snap(extra))
                            sums(m.psum[:, 2, 0:AW], 2, g % 2).then_inc(sums_x, 1)
            iterations(pe, body, ("turn", "count"))

        @block.sync
        def _(sp):
            for k, dst in enumerate((m.skey[:, :].bitcast(I32), m.ssrc[:, :])):
                sp.dma_start(dst, a["L0_ffn_edge_index"][k, :].rearrange("(p l) -> p l", l=L)).then_inc(e2_in, 16)
            sp.dma_start(bias, a["L0_gnn_b"].partition_broadcast(P)).then_inc(bias_in, 16)
            sp.wait_ge(sorting, SORT_STEPS)
            sp.dma_start(a["keys"].rearrange("(r l) -> r l", l=L), m.key[SORTED]).then_inc(key_out, 16)
            sp.wait_ge(first_keys, 2)
            sp.dma_start(a["subs"], subs).then_inc(sub_out, 16)
            sp.wait_ge(length_ready, 1)
            length = sp.value_load(m.length_i[0:1, 0:1], min_val=GB * LEAST, max_val=L)
            sp.wait_ge(key_out, 16)
            at = sp.alloc_register("at")
            sp.reg_mov(at, 0)
            with sp.Fori(0, P) as r:
                sp.dma_start(a["rows"][bass.ds(r * L, L)], a["keys"][bass.ds(sp.snap(at, min_val=0, max_val=E2 - L), L)])\
                  .then_inc(row_out, 16)
                sp.reg_add(at, at, length)
            sp.wait_ge(row_out, P * 16)
            rows = a["rows"].rearrange("(r l) -> r l", l=L)
            sp.dma_start(m.skey[:, :], rows).then_inc(rows_in, 16)
            sp.dma_start(m.prev[1:P, 0:1], rows[0:P - 1, bass.ds(length - 1, 1)],
                         allow_slow_non_contiguous=True).then_inc(rows_in, 16)
            sp.wait_ge(rows_in, 32)
            sp.wait_ge(sub_out, 16)

        @block.vector
        def _(v):
            step = Steps(v, sorting)
            extra, xs = v.alloc_register("extra_dve"), v.alloc_register("xs_dve")
            v.reg_mov(extra, 0)
            v.reg_mov(xs, 1)
            further = v.alloc_register("further")
            v.memset(m.acc_flat, 0.0).then_inc(start_sem, 1)
            v.memset(m.wrows[:, :, :, D:AW], 1.0).then_inc(start_sem, 1)
            v.wait_ge(start_sem, 2)

            def hot(g, buf, iota):
                return v.tensor_tensor(m.hot[:, buf, :, :], iota.unsqueeze(1).to_broadcast([P, GC, P]),
                                       m.edst[:, bass.ds(g * GC, GC)].unsqueeze(2).to_broadcast([P, GC, P]),
                                       ALU.is_equal)

            def add(tile, bank):
                out = m.acc[:, bass.ds(tile, 1), :].rearrange("p o d -> p (o d)")
                return v.tensor_tensor(out, out, m.psum[:, bank, 0:AW], ALU.add)

            v.wait_ge(bias_in, 16)
            hot(0, 0, m.iota[:, :]).then_inc(hot_ready, 1)

            def body(it, first):
                for g in range(BODY):
                    if g == 7:
                        v.wait_ge(f_l, it + 1)
                        v.tensor_tensor(m.feat[:, bass.ds(it, 1), :].rearrange("p o d -> p (o d)"), m.psum[:, 7, 0:D],
                                        bias, ALU.add).then_inc(f_z, 1)
                    hot(it * BODY + (g + 1), (g + 1) % 2, m.iota[:, :]).then_inc(hot_ready, 1)
                    slot_step(*slot(it, g))
                    v.wait_ge(sums_ready, it * BODY + (g + 1))
                    if not (first and g == 0):
                        v.wait_ge(group_done, it * BODY + g)
                    tile = v.value_load(m.regs[0:1, 0, bass.ds(it * BODY + g, 1)], min_val=0, max_val=T - 1)
                    more = v.value_load(m.regs[0:1, 1, bass.ds(it * BODY + g, 1)], min_val=0, max_val=T - 1)
                    with v.If(more > 0):
                        v.reg_mov(further, tile)
                        v.tensor_scalar(m.iota_x[:, :], m.iota[:, :], float(P), None, ALU.add).then_inc(xstep, 1)
                        v.wait_ge(xstep, v.snap(xs))
                        v.reg_add(xs, xs, 1)
                        with v.Fori(0, more):
                            hot(it * BODY + g, 2, m.iota_x[:, :]).then_inc(hot_x, 1)
                            v.reg_add(extra, extra, 1)
                            v.wait_ge(sums_x, v.snap(extra))
                            v.reg_add(further, further, 1)
                            add(v.snap(further, min_val=0, max_val=T - 1), 2).then_inc(xstep, 1)
                            v.tensor_scalar(m.iota_x[:, :], m.iota_x[:, :], float(P), None, ALU.add)\
                             .then_inc(xstep, 1)
                            v.reg_add(xs, xs, 1)
                            v.wait_ge(xstep, v.snap(xs))
                            v.reg_add(xs, xs, 1)
                    add(tile, g % 2).then_inc(group_done, 1)

            def sort_step(kind, cur, arg, n):
                s, d = m.key[cur], m.key[1 - cur]
                if kind == "sign":
                    step(v.tensor_scalar(d, s, m.signs[:, arg:arg + 1], None, ALU.mult))
                if kind in ("merge", "mirror"):
                    turn = slice(None, None, -1) if kind == "mirror" else slice(None)
                    s, d = (k.rearrange("p (n two h) -> p n two h", two=2, h=arg) for k in (s, d))
                    if turns_before(n + 1) > turns_before(n):
                        v.wait_ge(turned_c, turns_before(n + 1))
                    step.then(v.tensor_tensor(d[:, :, 0, :], s[:, :, 0, :], s[:, :, 1, turn], ALU.min))
                    step(v.tensor_tensor(d[:, :, 1, :], s[:, :, 1, :], s[:, :, 0, turn], ALU.max))

            key, spare = m.key[SORTED], m.key[1 - SORTED]
            searched = 0

            def finish_step(kind):
                nonlocal searched
                if kind == "first":
                    step.then(v.tensor_copy(firsts, key[:, 0:1].to_broadcast([P, P])))
                    step.then(v.memset(ones, 1.0))
                    step.then(v.memset(m.prev[0:1, 0:1], 0.0))
                    step(v.tensor_scalar(m.skey[:, :], key, KEY_END, None, ALU.is_lt))
                    v.tensor_reduce(valid, m.skey[:, :], AX.X, ALU.add).then_inc(first_keys, 1)
                    v.tensor_copy(subs, key.rearrange("p (s k) -> p s k", k=SUB)[:, :, 0]).then_inc(first_keys, 1)
                if kind == "below":
                    if searched == 0:
                        v.wait_ge(first_turned, 1)
                        step(v.tensor_scalar(m.length[:, 0:1], m.psum[:, 3, P:P + 1], float(GB * P - 1), None, ALU.add))
                        step(v.tensor_copy(m.length_i[:, 0:1], m.length[:, 0:1]))
                        step(v.tensor_scalar(m.length_i[:, 1:2], m.length_i[:, 0:1], (GB * P).bit_length() - 1, None,
                                             ALU.logical_shift_right))
                        step(v.tensor_scalar(m.length_i[:, 1:2], m.length_i[:, 1:2], LEAST, None, ALU.max))
                        v.tensor_scalar(m.length_i[:, 0:1], m.length_i[:, 1:2], GB, None, ALU.mult).then_inc(length_ready, 1)
                        v.wait_ge(length_ready, 1)
                        step.then(v.tensor_copy(m.length[:, 0:2], m.length_i[:, 0:2]))
                    lo, hi = searched, min(searched + BELOW, ST)
                    below = spare[:, 0:(hi - lo) * P].rearrange("p (t r) -> p t r", t=hi - lo)
                    step(v.tensor_tensor(below, m.psum[:, 3, 0:P].unsqueeze(1).to_broadcast([P, hi - lo, P]),
                                         m.nodekey[:, lo:hi].unsqueeze(2).to_broadcast([P, hi - lo, P]), ALU.is_lt))
                    step(v.tensor_reduce(m.row[:, lo:hi], below, AX.X, ALU.add))
                    searched = hi
                run = spare.bitcast(I32)
                if kind == "sources":
                    v.wait_ge(rows_in, 32)
                    step.then(v.tensor_scalar(m.ssrc[:, :], m.skey[:, :].bitcast(I32), (1 << SHIFT) - 1, None, ALU.bitwise_and))
                    step.then(v.tensor_scalar(run, m.skey[:, :].bitcast(I32), SHIFT, None, ALU.logical_shift_right))
                    step.then(v.tensor_scalar(prev[:, 1:2], prev[:, 0:1], SHIFT, None, ALU.logical_shift_right))
                if kind == "same":
                    step.wait()
                    step.then(v.tensor_tensor(m.skey[:, 1:L], run[:, 1:L], run[:, 0:L - 1], ALU.is_equal))
                    step(v.tensor_tensor(m.skey[:, 0:1], run[:, 0:1], prev[:, 1:2], ALU.is_equal))
                    step(v.tensor_scalar(m.row, m.row, -1.0, 0.0, ALU.add, ALU.max))

            def slot_step(kind, cur, arg, n):
                if kind in FINISH + LATE:
                    finish_step(kind)
                else:
                    sort_step(kind, cur, arg, n)

            src, key_i = m.skey[:, :].bitcast(I32), m.key[0].bitcast(I32)
            v.wait_ge(e2_in, 32)
            step.then(v.tensor_scalar(src, src, N - 1, None, ALU.min))
            step(v.tensor_scalar(m.ssrc[:, :], m.ssrc[:, :], N, None, ALU.min))
            step(v.tensor_scalar(m.ssrc[:, :], m.ssrc[:, :], SHIFT, KEY_BASE, ALU.logical_shift_left, ALU.bitwise_or))
            step(v.tensor_tensor(key_i, m.ssrc[:, :], src, ALU.bitwise_or))
            step(v.tensor_scalar(m.key[1], m.key[0], m.signs[:, 0:1], None, ALU.mult))
            prev = m.prev.bitcast(I32)
            iterations(v, body, ("sign", "merge", "mirror") + tuple(FINISH + LATE))
            v.wait_ge(group_done, NG)


def first_layer(nc, ctx, m, a):
    def sem(name):
        return ctx.enter_context(nc.semaphore(name))

    x_in, c_in, f0_i, f0_in = sem("c_x_in"), sem("c_const"), sem("f0_i"), sem("f0_in")
    dve, sq, pad = sem("c_dve"), sem("c_sqrt"), sem("c_pad")
    mean_c, turned, turned_c, lin = sem("mean_c"), sem("c_turned"), sem("c_turned_c"), sem("lin")
    biased, normed, turned2, turned2_c, kept2, proj, proj_read = (
        sem("biased"), sem("normed"), sem("turned2"), sem("turned2_c"), sem("kept2"), sem("proj"), sem("proj_read"))
    dve_x2, tile_stats, f0_turned, f0_c = sem("x2_tiles"), sem("c_stats"), sem("f0_turned"), sem("f0_c")
    stored, w_ready, seek_idx, seek_in = sem("c_stored"), sem("w_ready"), sem("seek_idx"), sem("seek_in")
    xt = m.work[:, 0:2 * D].rearrange("p (b d) -> p b d", b=2)
    f0 = m.work[:, 512:768]
    wext = m.work[:, 768:816].rearrange("p (k c) -> p k c", k=2)
    att = m.work[:, 816:848]
    f0t = m.work[:, 920:922]
    prod = m.work[:, 848:912].rearrange("p (s k c) -> p s k c", s=2, k=2)
    z = m.work[:, 1024:1024 + RING * D].rearrange("p (b d) -> p b d", b=RING)
    zin = m.edge[:, 2048:2048 + RING * D].rearrange("p (b d) -> p b d", b=RING)
    proj_sb = m.edge[:, 0:T * WX].rearrange("p (t c) -> p t c", t=T)
    x = m.mid[:, 0:T * D].rearrange("p (t d) -> p t d", t=T)
    x2 = m.acc[:, :, 0:D]
    xnt = m.mid[:, :].rearrange("p (k n) -> p k n", k=2)

    def one(ap, t):
        return ap[:, bass.ds(t, 1), 0:D].rearrange("p o d -> p (o d)")

    def since(eng, done, t, n):
        if not isinstance(t, int) or t - n >= 0:
            eng.wait_ge(done, t - n + 1)

    def pipeline(eng, stage1, stage2, lag, pause=None):
        def step(t, b, last=T):
            if not isinstance(t, int) or t + lag < last:
                stage1(t + lag, (b + lag) % RING)
            stage2(t, b)
        for t in range(lag):
            stage1(t, t)
        for t in range(RING):
            step(t, t)
        loops = (T - lag) // RING
        parts = (1, 3 * loops // 4, loops) if pause else (1, loops)
        for lo, hi in zip(parts, parts[1:]):
            with eng.Fori(lo, hi) as i:
                for b in range(RING):
                    step(i * RING + b, b)
            if pause and hi < loops:
                pause()
        for t in range((T - lag) // RING * RING, T):
            step(t, t % RING)

    with nc.Block() as block:
        @block.sync
        def _(sp):
            sp.dma_start(m.idx[:, 0, 0:1], a["src"][0:1].partition_broadcast(P)).then_inc(f0_i, 16)
            sp.dma_start(x[:, 0:T - 1, :], a["x"][0:(T - 1) * P, :].rearrange("(t p) d -> p t d", p=P)).then_inc(x_in, 16)
            sp.wait_ge(pad, 1)
            sp.dma_start(x[0:N - (T - 1) * P, T - 1, :], a["x"][(T - 1) * P:N, :]).then_inc(x_in, 16)
            sp.wait_ge(dve_x2, T)
            sp.dma_start(a["x2"].rearrange("(t p) d -> p t d", p=P), x2).then_inc(stored, 16)
            table = a["table"].rearrange("(t p) c -> p t c", p=P)
            for lo in range(0, T, XT):
                sp.wait_ge(proj_read, lo + XT)
                sp.dma_start(table[:, lo:lo + XT, :], proj_sb[:, lo:lo + XT, :]).then_inc(stored, 16)
            sp.wait_ge(stored, 16 + T // XT * 16)

        @block.gpsimd
        def _(pool):
            pool.wait_ge(f0_i, 16)
            pool.indirect_dma_start(f0, None, a["feat"], bass.IndirectOffsetOnAxis(ap=m.idx[:, 0, 0:1], axis=0))\
                .then_inc(f0_in, 16)
            for k, table in enumerate((a["subs"], a["keys"].rearrange("(r s) -> r s", s=SUB))):
                pool.wait_ge(seek_idx, k + 1)
                for t in range(ST):
                    pool.indirect_dma_start(m.seek[:, t, :], None, table,
                                            bass.IndirectOffsetOnAxis(ap=m.row_i[:, t:t + 1], axis=0)).then_inc(seek_in, 16)
            pool.wait_ge(seek_in, 2 * ST * 16)

        @block.scalar
        def _(act):
            act.dma_start(wext[:, :, 0:HE], a["L0_ffn_W_gat"].rearrange("(k p) c -> p k c", p=P)).then_inc(c_in, 16)
            for k, name in enumerate(("L0_ffn_att_src", "L0_ffn_att_dst")):
                act.dma_start(att[:, HE * k:HE * k + HE], a[name].rearrange("h e -> (h e)").partition_broadcast(P))\
                   .then_inc(c_in, 16)

            def nothing(t, b):
                pass

            def bring(t, b):
                since(act, turned, t, RING)
                act.activation(zin[:, b, :], one(x2, t), ACT.Copy).then_inc(mean_c, 1)

            def copy(t, b):
                act.wait_ge(turned, t + 1)
                since(act, lin, t, 2)
                for k in range(2):
                    act.activation(xt[:, b % 2, k * P:(k + 1) * P], m.psum[:, b % 2, k * P:(k + 1) * P], ACT.Copy,
                                   scale=f0t[:, k:k + 1]).then_inc(turned_c, 1)

            act.wait_ge(f0_turned, 1)
            act.activation(f0t, m.psum[:, 4, 0:2 * P:P], ACT.Copy).then_inc(f0_c, 1)
            act.wait_ge(f0_c, 1)
            pipeline(act, bring, copy, 2)
            act.wait_ge(dve, C_VAR)
            act.activation(m.rstd, m.var, ACT.Sqrt).then_inc(sq, 1)

            def copies(t, b):
                act.wait_ge(turned2, t + 1)
                since(act, proj, t, 2)
                act.activation(xt[:, b % 2, :], m.psum[:, 4 + b % 2, 0:D], ACT.Copy).then_inc(turned2_c, 1)
                act.activation(xnt[:, :, bass.ds(t * P, P)], m.psum[:, 4 + b % 2, 0:D].rearrange("p (k n) -> p k n", k=2),
                               ACT.Copy).then_inc(kept2, 1)

            pipeline(act, nothing, copies, 0)

        @block.tensor
        def _(pe):
            def turn(t, b):
                pe.wait_ge(mean_c, t + 1)
                if not isinstance(t, int) or t >= 2:
                    pe.wait_ge(turned_c, (t - 1) * 2)
                for k in range(2):
                    last = pe.transpose(m.psum[:, b % 2, k * P:(k + 1) * P], zin[:, b, k * P:(k + 1) * P], m.ident[:, :])
                last.then_inc(turned, 1)

            def linear(t, b):
                pe.wait_ge(turned_c, t * 2 + 2)
                since(pe, biased, t, 2)
                for k in range(2):
                    last = pe.matmul(m.psum[:, 2 + b % 2, 0:D], xt[:, b % 2, k * P:(k + 1) * P], m.wgnn[:, 2 + k, :],
                                     start=(k == 0), stop=(k == 1))
                last.then_inc(lin, 1)

            pe.wait_ge(f0_in, 16)
            for k in range(2):
                last = pe.transpose(m.psum[:, 4, k * P:(k + 1) * P], f0[:, k * P:(k + 1) * P], m.ident[:, :])
            last.then_inc(f0_turned, 1)
            pipeline(pe, turn, linear, 1)
            pe.wait_ge(w_ready, 1)

            def turn2(t, b):
                pe.wait_ge(normed, t + 1)
                since(pe, kept2, t, 2)
                for k in range(2):
                    last = pe.transpose(m.psum[:, 4 + b % 2, k * P:(k + 1) * P], zin[:, b, k * P:(k + 1) * P],
                                        m.ident[:, :])
                last.then_inc(turned2, 1)

            def project(t, b):
                pe.wait_ge(turned2_c, t + 1)
                since(pe, proj_read, t, 2)
                for k in range(2):
                    last = pe.matmul(m.psum[:, 6 + b % 2, 0:WX], xt[:, b % 2, k * P:(k + 1) * P], wext[:, k, :],
                                     start=(k == 0), stop=(k == 1))
                last.then_inc(proj, 1)

            pipeline(pe, turn2, project, 1)

        @block.vector
        def _(v):
            step = Steps(v, dve)
            v.memset(x[:, T - 1, :], 0.0).then_inc(pad, 1)
            v.tensor_copy(m.row_i, m.row).then_inc(seek_idx, 1)
            v.wait_ge(c_in, 48)
            for s in range(2):
                step.then(v.tensor_tensor(prod[:, s, :, :], wext[:, :, 0:HE],
                                          att[:, HE * s:HE * s + HE].unsqueeze(1).to_broadcast([P, 2, HE]), ALU.mult))
            step.wait()
            for s in range(2):
                for k in range(2):
                    step.then(v.tensor_reduce(wext[:, k, HE + H * s:HE + H * s + H],
                                              prod[:, s, k, :].rearrange("p (h e) -> p h e", e=X), AX.X, ALU.add))
            step.wait()
            step(v.tensor_scalar(m.tmp_s, m.acc[:, :, D], 1.0, None, ALU.max))
            step(v.reciprocal(m.cnt[:, 0:T], m.tmp_s))
            v.memset(m.prev[:, 3:4], 0.0).then_inc(w_ready, 1)
            v.wait_ge(x_in, 32)

            def residual(t, b):
                v.wait_ge(lin, t + 1)
                since(v, dve_x2, t, RING)
                v.scalar_tensor_tensor(z[:, b, :], m.psum[:, 2 + b % 2, 0:D], m.cnt[:, bass.ds(t, 1)], one(m.feat, t),
                                       ALU.mult, ALU.add).then_inc(biased, 1)
                if not isinstance(t, int) or t >= 1:
                    activate(t - 1, (b - 1) % RING)
                if not isinstance(t, int) or t >= 2:
                    moments_of(t - 2)

            def activate(t, b):
                v.wait_ge(biased, t + 1)
                v.scalar_tensor_tensor(one(x2, t), z[:, b, :], 0.0, one(x, t), ALU.max, ALU.add).then_inc(dve_x2, 1)

            def moments_of(t):
                v.wait_ge(dve_x2, t + 1)
                v.bn_stats(m.stats[:, bass.ds(t, 1), :].rearrange("p o s -> p (o s)"), one(x2, t)).then_inc(tile_stats, 1)

            def nothing(t, b):
                pass

            low = m.nodekey[:, :].unsqueeze(2).to_broadcast([P, ST, SUB])

            def seek_key():
                v.wait_ge(seek_in, ST * 16)
                step(v.tensor_tensor(m.seek, m.seek, low, ALU.is_lt))
                step(v.tensor_reduce(m.tmp_s2, m.seek, AX.X, ALU.add))
                step(v.tensor_scalar(m.tmp_s2, m.tmp_s2, -1.0, 0.0, ALU.add, ALU.max))
                step(v.scalar_tensor_tensor(m.row, m.row, float(L // SUB), m.tmp_s2, ALU.mult, ALU.add))
                v.tensor_copy(m.row_i, m.row).then_inc(seek_idx, 1)

            pipeline(v, nothing, residual, 0, seek_key)
            activate(T - 1, (T - 1) % RING)
            moments_of(T - 2)
            moments_of(T - 1)
            v.wait_ge(tile_stats, T)
            step.n -= T
            statistics(v, m, step)
            assert step.n == C_VAR
            v.wait_ge(sq, 1)
            inverse_root(v, m, step)
            v.memset(xnt[:, :, NP:ST * P], 0.0).then_inc(pad, 1)

            def normalise(t, b):
                since(v, turned2, t, RING)
                v.tensor_scalar(zin[:, b, :], one(x2, t), m.mean[:, bass.ds(t, 1)], m.rstd[:, bass.ds(t, 1)],
                                ALU.subtract, ALU.mult).then_inc(normed, 1)

            def keep(t, b):
                v.wait_ge(proj, t + 1)
                v.tensor_copy(proj_sb[:, bass.ds(t, 1), :].rearrange("p o c -> p (o c)"), m.psum[:, 6 + b % 2, 0:WX])\
                 .then_inc(proj_read, 1)

            pipeline(v, normalise, keep, 2)
            v.wait_ge(proj_read, T)
            step(v.tensor_copy(m.adst, proj_sb[:, :, TW:WX]))
            v.wait_ge(seek_in, 2 * ST * 16)
            step(v.tensor_tensor(m.seek, m.seek, low, ALU.is_lt))
            step(v.tensor_reduce(m.tmp_s2, m.seek, AX.X, ALU.add))
            step(v.scalar_tensor_tensor(m.start, m.row, float(SUB), m.tmp_s2, ALU.mult, ALU.add))


C_VAR = 8 + 4 + STATISTICS - T


def gather_and_experts(nc, ctx, m, a):
    def sem(name):
        return ctx.enter_context(nc.semaphore(name))

    w_in, idx_ready, ones, copied = sem("d_w_in"), sem("d_idx_ready"), sem("d_ones"), sem("copied")
    slot_in = m.gathered[0:GB]
    before = NG // BODY * 16
    up, gelu, down, y_c = sem("up"), sem("gelu"), sem("down"), sem("y_c")
    y_out = [sem(f"y_out{k}") for k in range(2)]
    zeroed, dve, start_t, turned, start_out, end_in, value_idx, value_out, value_in, cols = (
        sem("zeroed"), sem("d_dve"), sem("start_t"), sem("d_turned"), sem("start_out"), sem("end_in"), sem("value_idx"),
        sem("value_out"), sem("value_in"), sem("d_cols"))
    padded, sums_zeroed = sem("padded"), sem("sums_zeroed")
    half = GB // 2
    w1 = m.big[:, L * TW:L * TW + X * 2 * FF].rearrange("p (e k f) -> p e k f", e=X, k=2)
    stage = m.big[:, L * TW + X * 2 * FF:L * TW + X * 2 * FF + GB * WX].rearrange("p (s c) -> p s c", s=GB)
    w2 = m.edge[:, 0:X * FF // P * D].rearrange("p (e f d) -> p e f d", e=X, f=FF // P)
    turns = m.edge[:, X * FF // P * D:X * FF // P * D + 3 * P]
    b1 = m.small[:, 64 * 17:64 * 17 + X * FF // P]
    hid = m.work[:, 0:2048].rearrange("p (b f n) -> p b f n", b=2, f=FF // P)
    y = m.work[:, 2048:3072].rearrange("p (b t d) -> p b t d", b=2, t=NB)
    zero = m.wgnn[:, :, :].rearrange("p k d -> p (k d)")
    xnt = m.mid[:, :].rearrange("p (k n) -> p k n", k=2)
    steps = ST // NB
    W = NB * P
    scatter_at, tail = 4, 6
    free_at = 18
    pos, blk, row = (m.small[:, 640 + 2 * T * k:640 + 2 * T * (k + 1)] for k in range(3))
    blk_i, row_i = blk.bitcast(I32), m.small[:, 64 * 22:64 * 22 + 2 * T].bitcast(I32)
    assert LEAST > max(scatter_at, tail + 2)

    with nc.Block() as block:
        @block.gpsimd
        def _(pool):
            its = pool.value_load(m.length_i[0:1, 1:2], min_val=LEAST, max_val=L // GB)
            staged = pool.alloc_register("staged")
            pool.reg_mov(staged, 1)

            def gathers(lo, hi):
                with pool.Fori(lo, hi):
                    for k in range(GB):
                        if k % half == 0:
                            pool.wait_ge(idx_ready, staged)
                            pool.reg_add(staged, staged, 1)
                        pool.indirect_dma_start(
                            stage[:, k, :], None, a["table"],
                            bass.IndirectOffsetOnAxis(ap=m.idx[:, k // half, k % half:k % half + 1], axis=0))\
                            .then_inc(slot_in[k], 16)

            gathers(0, scatter_at)
            pool.wait_ge(value_idx, 1)
            pool.wait_ge(zeroed, 4 * 16)
            for t in range(T):
                pool.indirect_dma_start(a["values"], bass.IndirectOffsetOnAxis(ap=m.start_i[:, t:t + 1], axis=0),
                                        m.adst[:, t, :], None, bounds_check=E2 - 1, oob_is_err=False)\
                    .then_inc(value_out, 16)
            gathers(scatter_at, its)

        @block.vector
        def _(v):
            its = v.value_load(m.length_i[0:1, 1:2], min_val=LEAST, max_val=L // GB)
            halves, pads = v.alloc_register("halves"), v.alloc_register("pads")
            v.reg_mov(halves, 1)
            v.reg_mov(pads, 1)
            step = Steps(v, dve)
            v.memset(zero, 0.0).then_inc(ones, 1)
            v.memset(m.iota_x[:, :], 1.0).then_inc(ones, 1)
            for h in range(2):
                v.tensor_copy(m.idx[:, h, 0:half], m.ssrc[:, h * half:(h + 1) * half]).then_inc(idx_ready, 1)
            v.wait_ge(turned, 1)
            v.tensor_copy(turns[0:ST, 0:P], m.psum[0:ST, 6, 0:P]).then_inc(start_t, 1)

            def take(it, h, last=False):
                for k in range(h * half, (h + 1) * half):
                    v.wait_ge(slot_in[k], it * 16 + (before + 16))
                v.tensor_copy(m.big[:, bass.ds(it * (GB * TW) + h * half * TW, half * TW)].rearrange("p (s c) -> p s c", c=TW),
                              stage[:, h * half:(h + 1) * half, 0:TW]).then_inc(copied, 1)
                v.wait_ge(copied, halves)
                v.reg_add(halves, halves, 1)
                if not last:
                    v.tensor_copy(m.idx[:, h, 0:half], m.ssrc[:, bass.ds(it * GB + GB + h * half, half)])\
                     .then_inc(idx_ready, 1)

            with v.Fori(0, 2) as it:
                take(it, 0)
                take(it, 1)
            v.wait_ge(turned, 2)
            step(v.tensor_copy(m.end, m.psum[:, 6, P:P + T]))
            step(v.tensor_tensor(m.some, m.end, m.start[:, 0:T], ALU.is_gt))
            step.then(v.reciprocal(m.length[:, 2:3], m.length[:, 1:2]))
            step.then(v.tensor_scalar(m.length[:, 3:4], m.length[:, 0:1], -1.0, float(L), ALU.mult, ALU.add))
            step.then(v.tensor_copy(pos[:, 0:T], m.start[:, 0:T]))
            step(v.tensor_scalar(pos[:, T:2 * T], m.end, -1.0, 0.0, ALU.add, ALU.max))
            step(v.tensor_copy(blk_i, pos))
            step(v.tensor_scalar(blk_i, blk_i, GB.bit_length() - 1, None, ALU.logical_shift_right))
            step(v.tensor_copy(row, blk_i))
            step(v.tensor_copy(blk, row))
            step(v.tensor_scalar(row, row, 0.5, m.length[:, 2:3], ALU.add, ALU.mult))
            step(v.tensor_copy(row_i, row))
            step(v.tensor_copy(row, row_i))
            step(v.scalar_tensor_tensor(blk, row, m.length[:, 1:2], blk, ALU.mult, ALU.is_gt))
            step(v.tensor_tensor(row, row, blk, ALU.subtract))
            step(v.scalar_tensor_tensor(pos, row, m.length[:, 3:4], pos, ALU.mult, ALU.add))
            step(v.scalar_tensor_tensor(m.tmp_s, pos[:, 0:T], float(-BEYOND), m.some, ALU.add, ALU.mult))
            step.then(v.tensor_scalar(m.start_i, m.tmp_s, float(BEYOND), None, ALU.add))
            step(v.scalar_tensor_tensor(m.end_i, pos[:, T:2 * T], float(E2), pos[:, T:2 * T], ALU.is_lt, ALU.mult))
            step(v.tensor_scalar(m.length_i[:, 0:1], m.length_i[:, 1:2], WHOLE + 1, -WHOLE, ALU.max, ALU.add))
            v.memset(m.prev[:, 0:1], 0.0).then_inc(value_idx, 1)
            with v.Fori(2, LEAST - tail - 1) as it:
                take(it, 0)
                take(it, 1)
            v.wait_ge(zeroed, 4 * 16)
            v.wait_ge(sums_zeroed, QL * TW // 1024 * 16)
            v.memset(zero[:, GB * HE:GB * TW], NOTHING).then_inc(padded, 1)
            v.wait_ge(padded, 1)
            with v.If(its < L // GB):
                with v.Fori(its, L // GB) as n:
                    beyond = m.big[:, bass.ds(n * (GB * TW), GB * TW)].rearrange("p (s c) -> p s c", c=TW)
                    v.tensor_copy(beyond[:, :, 0:HE], zero[:, 0:GB * HE].rearrange("p (s c) -> p s c", c=HE))\
                     .then_inc(padded, 1)
                    v.tensor_copy(beyond[:, :, HE:TW], zero[:, GB * HE:GB * TW].rearrange("p (s c) -> p s c", c=H))\
                     .then_inc(padded, 1)
                    v.tensor_scalar(m.skey[:, bass.ds(n * GB, GB)], zero[:, 0:GB], 1.0, None, ALU.add).then_inc(padded, 1)
                    v.reg_add(pads, pads, 3)
            with v.Fori(LEAST - tail - 1, its - tail) as it:
                take(it, 0)
                take(it, 1)
            pre, val, back = m.pre, m.val, m.back
            v.wait_ge(value_in, 16)
            v.wait_ge(padded, pads)
            step(v.memset(m.colp, 0.0))
            step(v.tensor_tensor_scan(pre, m.skey[:, :], m.skey[:, :], 1.0, ALU.mult, ALU.min))
            for h in range(H):
                step.then(v.tensor_tensor_scan(val[:, :, h], m.skey[:, :], val[:, :, h], 0.0, ALU.mult, ALU.add))
            step.wait()
            step.then(v.tensor_copy(m.colp[:, 0:H], val[:, L - 1, :]))
            step(v.tensor_copy(m.flag[:, 0:H], pre[:, L - 1:L].to_broadcast([P, H])))
            v.memset(m.prev[:, 0:1], 0.0).then_inc(cols, 1)
            with v.Fori(its - tail, its - 2) as it:
                take(it, 0)
                take(it, 1)
            v.wait_ge(turned, 3)
            step.then(v.tensor_copy(m.line[0:H, :], m.psum[0:H, 6, P:2 * P]))
            step(v.memset(m.carry[0:H, 0:1], 0.0))
            step(v.tensor_tensor_scan(m.carry[0:H, 1:P + 1], m.line[0:H, :], m.psum[0:H, 6, 0:P], 0.0, ALU.mult, ALU.add))
            v.memset(m.prev[:, 0:1], 0.0).then_inc(cols, 1)
            v.wait_ge(turned, 4)
            step(v.tensor_copy(back[:, 0:H], m.psum[:, 7, 0:H]))
            for h in range(H):
                step.then(v.scalar_tensor_tensor(val[:, :, h], pre, back[:, h:h + 1], val[:, :, h], ALU.mult, ALU.add))
            with v.Fori(its - 2, its - 1) as it:
                take(it, 0)
                take(it, 1)
            with v.Fori(its - 1, its) as it:
                take(it, 0, True)
                take(it, 1, True)

        def experts(eng, stage1, stage2):
            stage1(0, 0, True)
            
            def body(blk, first, last):
                for e in range(X):
                    if not (last and e == X - 1):
                        stage1(blk * X + (e + 1), (e + 1) % X, first and e == 0)
                    stage2(blk * X + e, e, first and e < 2)
            body(0, True, False)
            with eng.Fori(1, steps - 1) as blk:
                body(blk, False, False)
            body(steps - 1, False, True)

        @block.tensor
        def _(pe):
            pe.transpose(m.psum[0:ST, 6, 0:P], m.start, m.ident[:, :]).then_inc(turned, 1)
            pe.wait_ge(end_in, 16)
            pe.transpose(m.psum[:, 6, P:P + T], turns[0:T, P:2 * P], m.ident[0:T, 0:T]).then_inc(turned, 1)
            pe.wait_ge(w_in, 16 * 4)
            pe.wait_ge(ones, 2)

            def hidden(s, e, first):
                if not first:
                    pe.wait_ge(gelu, (s - 1) * (FF // P))
                for f in range(FF // P):
                    for k in range(2):
                        last = pe.matmul(m.psum[:, 2 * (e % 2) + f // 2, (f % 2) * W:(f % 2) * W + W],
                                         w1[:, e, k, f * P:(f + 1) * P], xnt[:, k, bass.ds(node(s, e), W)],
                                         start=(k == 0), stop=(k == 1))
                last.then_inc(up, 1)

            def node(s, e):
                return (s - e) * (W // X)

            def out(s, e, first):
                pe.wait_ge(gelu, s * 4 + 4)
                if not first:
                    pe.wait_ge(y_c, s - 1)
                for t in range(NB):
                    o = m.psum[:, 4 + e % 2, t * D:(t + 1) * D]
                    pe.matmul(o, m.iota_x[0:1, :], m.b2[0:1, e * D:(e + 1) * D], start=True, stop=False)
                    for f in range(FF // P):
                        last = pe.matmul(o, hid[:, e % 2, f, t * P:(t + 1) * P], w2[:, e, f, :], start=False,
                                         stop=(f == FF // P - 1))
                last.then_inc(down, 1)

            experts(pe, hidden, out)
            pe.wait_ge(cols, 1)
            pe.transpose(m.psum[0:H, 6, 0:P], m.colp[:, 0:H], m.ident[:, :])
            pe.transpose(m.psum[0:H, 6, P:2 * P], m.flag[:, 0:H], m.ident[:, :]).then_inc(turned, 1)
            pe.wait_ge(cols, 2)
            pe.transpose(m.psum[:, 7, 0:H], m.carry[0:H, 0:P], m.ident[0:H, 0:H]).then_inc(turned, 1)

        @block.scalar
        def _(act):
            act.wait_ge(w_in, 16 * 4)

            def gelus(s, e, first):
                act.wait_ge(up, s + 1)
                if not first:
                    act.wait_ge(down, s - 1)
                for f in range(FF // P):
                    act.activation(hid[:, e % 2, f, :], m.psum[:, 2 * (e % 2) + f // 2, (f % 2) * W:(f % 2) * W + W],
                                   ACT.Gelu, bias=b1[:, e * 4 + f:e * 4 + f + 1]).then_inc(gelu, 1)

            def keep(s, e, first):
                act.wait_ge(down, s + 1)
                if not first:
                    act.wait_ge(y_out[e % 2], past(s, e))
                act.activation(y[:, e % 2, :, :].rearrange("p t d -> p (t d)"), m.psum[:, 4 + e % 2, :], ACT.Copy)\
                   .then_inc(y_c, 1)

            def past(s, e):
                return (s - e % 2) * 8

            experts(act, gelus, keep)

        @block.sync
        def _(sp):
            sp.wait_ge(ones, 1)
            for i in range(4):
                sp.dma_start(a["values"].rearrange("(p l) c -> p (l c)", p=P)[:, i * 1024:(i + 1) * 1024], zero)\
                  .then_inc(zeroed, 16)
            sp.wait_ge(start_t, 1)
            sp.dma_start(a["starts"].rearrange("(t p) -> t p", p=P), turns[0:ST, 0:P]).then_inc(start_out, 16)
            sp.wait_ge(start_out, 16)
            sp.dma_start(turns[0:T, P:2 * P], a["starts"][1:NP + 1].rearrange("(t p) -> t p", p=P)).then_inc(end_in, 16)
            sp.dma_start(w1, a["L0_ffn_W1"].rearrange("e (k p) f -> p e k f", p=P)).then_inc(w_in, 16)
            sp.dma_start(w2, a["L0_ffn_W2"].rearrange("e (f p) d -> p e f d", p=P)).then_inc(w_in, 16)
            sp.dma_start(b1, a["L0_ffn_b1"].rearrange("e (f p) -> p (e f)", p=P),
                         allow_slow_non_contiguous=True).then_inc(w_in, 16)
            sp.dma_start(m.b2[:, :], a["L0_ffn_b2"].rearrange("(o e) d -> o (e d)", o=1)).then_inc(w_in, 16)
            rest = a["sums"].rearrange("(p l) c -> p (l c)", p=P)[:, (L - QL) * TW:L * TW]
            for i in range(QL * TW // 1024):
                sp.dma_start(rest[:, i * 1024:(i + 1) * 1024], zero).then_inc(sums_zeroed, 16)
            ys = a["y"].rearrange("(t p) e d -> p t e d", p=P)

            def store(lo, hi):
                with sp.Fori(lo, hi) as blk:
                    for e in range(X):
                        sp.wait_ge(y_c, blk * X + (e + 1))
                        sp.dma_start(ys[:, bass.ds(blk * NB, NB), e, :], y[:, e % 2, :, :]).then_inc(y_out[e % 2], 16)

            store(0, free_at)
            sp.wait_ge(value_out, 16 * T)
            sp.dma_start(m.val, a["values"].rearrange("(p l) c -> p l c", p=P)).then_inc(value_in, 16)
            store(free_at, steps)
            for k in range(2):
                sp.wait_ge(y_out[k], steps * X // 2 * 16)



def attention(nc, ctx, m, a):
    def sem(name):
        return ctx.enter_context(nc.semaphore(name))

    dve, turned, cols, act_done, shifted = sem("e_dve"), sem("e_turned"), sem("e_cols"), sem("e_act"), sem("shifted")
    peak_ready, peak_out, peak_end_in, peak_patch, peak_patched, peak_in = (
        sem("peak_ready"), sem("peak_out"), sem("peak_end_in"), sem("peak_patch"), sem("peak_patched"), sem("peak_in"))
    sum_ready, sum_out, sum_end_in, sum_patch, sum_patched = (
        sem("sum_ready"), sem("sum_out"), sem("sum_end_in"), sem("sum_patch"), sem("sum_patched"))
    sum_in, gathered = m.gathered[GB:GB + 2], NG // BODY * 16
    sums_seen = sem("sums_seen")
    own_in, fin_done = sem("own_in"), sem("fin_done")
    fin_out = [sem(f"fin_out{k}") for k in range(FB + 1)]
    fin_in, before = m.loaded, 16
    g = m.big[:, 0:L * TW].rearrange("p (l c) -> p l c", c=TW)
    e, peak, same, pre, bar = m.val, m.peak, m.skey[:, :], m.pre, m.bar
    highest = m.edge[:, 0:L * H].rearrange("p (l c) -> p l c", c=H)
    own = m.work[:, 1840:1840 + T * WX].rearrange("p (t c) -> p t c", t=T)
    own_h, own_src, own_dst = own[:, :, 0:HE], own[:, :, HE:TW], own[:, :, TW:WX]
    node = m.big[:, L * TW:]

    def by_node(at, n):
        return node[:, at:at + T * n].rearrange("p (t c) -> p t c", t=T)

    top, w_edges, w_own, sums = by_node(0, H), by_node(196, H), by_node(392, H), by_node(588, TW)
    weights = node[:, 196:588]
    own_part, agg, sq = by_node(1568, TW), by_node(2548, HE), by_node(3332, HE)
    w = m.work
    es, score, rank, gate, cmp = (w[:, k * 196:(k + 1) * 196].rearrange("p (t c) -> p t c", t=T) for k in range(5))
    inv = w[:, 980:1176].rearrange("p (t c) -> p t c", t=T)
    par = w[:, 1200:1248].rearrange("p (s c) -> p s c", s=3)
    line, carry, prev, carry2 = m.line, m.carry, m.line2, m.carry2
    ratio = w[:, 1300:1300 + 2 * P]
    colp, flag, back, back2 = m.colp, m.flag, m.back, m.back2
    end_row = w[:, 1600:1604]
    end_g, end_s = w[:, 1604:1605].bitcast(I32), w[:, 1605:1606].bitcast(I32)
    end_peak, new_peak = w[:, 1610:1614], w[:, 1614:1618]
    w_end = w[:, 1620:1628]
    end_sum, new_sum, part = w[:, 1632:1652], w[:, 1652:1672], w[:, 1672:1692]
    own_mark = w[:, 1740:1741]
    marks = w[:, 1700:1740]
    room = FG * (X + 1) * D
    place = [m.big[:, b * room:(b + 1) * room] for b in range(FB - 2)] + [m.mid[:, b * room:(b + 1) * room] for b in range(2)]
    slot = [w_[:, 0:FG * X * D].rearrange("p (t e d) -> p t e d", t=FG, e=X) for w_ in place]
    xs = [w_[:, FG * X * D:].rearrange("p (t d) -> p t d", t=FG) for w_ in place]
    slot.append(m.edge[:, 0:X * D].rearrange("p (t e d) -> p t e d", t=1, e=X))
    xs.append(m.edge[:, X * D:(X + 1) * D].rearrange("p (t d) -> p t d", t=1))
    groups = (T - 1) // FG
    assert groups == 2 * FB
    T1 = FB * FG
    halves = ((0, T1), (T1, T))

    def spread(ap, n):
        return ap.unsqueeze(2).to_broadcast([P, T, n])

    with nc.Block() as block:
        @block.sync
        def _(sp):
            sp.dma_start(own, a["table"].rearrange("(t p) c -> p t c", p=P)).then_inc(own_in, 16)
            for k, name in enumerate(("L0_ffn_b_gat", "L0_ffn_ln_gamma", "L0_ffn_ln_beta")):
                sp.dma_start(par[:, k, :], a[name].partition_broadcast(P)).then_inc(own_in, 16)
            sp.wait_ge(peak_ready, 1)
            sp.dma_start(a["peaks"].rearrange("(p l) c -> p l c", p=P), peak).then_inc(peak_out, 16)
            ys = a["y"].rearrange("(t p) e d -> p t e d", p=P)
            x2 = a["x2"].rearrange("(t p) d -> p t d", p=P)

            def load(at, b, n=FG):
                sp.dma_start(slot[b], ys[:, bass.ds(at, n), :, :]).then_inc(fin_in[b], 16)
                sp.dma_start(xs[b], x2[:, bass.ds(at, n), :]).then_inc(fin_in[b], 16)

            sp.wait_ge(peak_out, 16)
            sp.wait_ge(act_done, 2)
            sp.wait_ge(cols, 1)
            for b in range(2):
                load(b * FG, FB - 2 + b)
            load(T - 1, FB, 1)
            rest = sp.value_load(m.length_i[0:1, 0:1], min_val=1, max_val=QL // GB)
            table = a["sums"].rearrange("(p l) c -> p l c", p=P)
            for q in range(L // QL):
                sp.wait_ge(sum_ready, q + 1)
                if q < L // QL - 1:
                    sp.dma_start(table[:, q * QL:(q + 1) * QL, :], g[:, q * QL:(q + 1) * QL, :]).then_inc(sum_out, 16)
            with sp.Fori(0, rest) as n:
                at = n * GB + (L - QL)
                sp.dma_start(table[:, bass.ds(at, GB), :], g[:, bass.ds(at, GB), :]).then_inc(sum_out, 16)
            sp.wait_ge(sum_out, rest * 16 + (L // QL - 1) * 16)
            sp.wait_ge(cols, 3)
            for b in range(FB - 2):
                load((b + 2) * FG, b)
            for n in range(FB):
                b = (n + FB - 2) % FB
                sp.wait_ge(fin_out[b], 16)
                load((n + FB) * FG, b)

        @block.gpsimd
        def _(pool):
            def gather(out, table, idx, done):
                pool.indirect_dma_start(out, None, table, bass.IndirectOffsetOnAxis(ap=idx, axis=0)).then_inc(done, 16)

            def patch(table, idx, value, done):
                pool.indirect_dma_start(table, bass.IndirectOffsetOnAxis(ap=idx, axis=0), value, None,
                                        bounds_check=E2 - 1, oob_is_err=False).then_inc(done, 16)

            rest = pool.value_load(m.length_i[0:1, 0:1], min_val=1, max_val=QL // GB)
            sums_stored = pool.alloc_register("sums_stored")
            pool.reg_mov(sums_stored, rest * 16 + (L // QL - 1) * 16)
            for table, out, ends, new, ends_in, ready, patched, done in (
                    (a["peaks"], top, end_peak, new_peak, peak_end_in, peak_patch, peak_patched, (peak_in, peak_in)),
                    (a["sums"], sums, end_sum, new_sum, sum_end_in, sum_patch, sum_patched, sum_in)):
                if table is a["sums"]:
                    pool.wait_ge(sum_out, sums_stored)
                    pool.tensor_tensor(own_mark, m.length[:, 0:1], m.length[:, 0:1], ALU.add).then_inc(sums_seen, 1)
                    pool.wait_ge(sums_seen, 1)
                else:
                    pool.wait_ge(peak_out, 16)
                gather(ends, table, end_g, ends_in)
                pool.wait_ge(ready, 1)
                patch(table, end_s, new, patched)
                pool.wait_ge(patched, 16)
                for t in range(T):
                    gather(out[:, t, :], table, m.end_i[:, t:t + 1], done[t >= T1])

        @block.tensor
        def _(pe):
            pe.wait_ge(cols, 1)
            pe.transpose(m.psum[0:TW, 0, 0:P], colp, m.ident[:, :])
            pe.transpose(m.psum[0:TW, 0, P:2 * P], flag, m.ident[:, :]).then_inc(turned, 1)
            pe.wait_ge(cols, 2)
            pe.transpose(m.psum[:, 1, 0:TW], carry[0:TW, 0:P], m.ident[0:TW, 0:TW]).then_inc(turned, 1)
            pe.wait_ge(cols, 3)
            pe.transpose(m.psum[0:TW, 2, 0:P], colp, m.ident[:, :]).then_inc(turned, 1)
            pe.wait_ge(cols, 4)
            pe.transpose(m.psum[:, 3, 0:TW], carry2[0:TW, 0:P], m.ident[0:TW, 0:TW]).then_inc(turned, 1)

        @block.scalar
        def _(act):
            def exp(n, out, x):
                act.wait_ge(shifted, n)
                act.activation(out, x, ACT.Exp).then_inc(act_done, 1)

            def store(r):
                for n in range(FB):
                    b, at = (n + FB - 2) % FB, (r * FB + n) * FG
                    act.wait_ge(fin_done, at + FG)
                    act.dma_start(tile[:, at:at + FG, :], xs[b]).then_inc(fin_out[b], 16)

            tile = a["out"][0:(T - 1) * P, :].rearrange("(t p) d -> p t d", p=P)
            hl = L // 2
            exp(1, g[:, 0:hl, HE:TW], e[:, 0:hl, :])
            exp(2, g[:, hl:L, HE:TW], e[:, hl:L, :])
            exp(3, ratio[0:TW, :], ratio[0:TW, :])
            exp(4, w_end, w_end)
            exp(5, weights, weights)
            for n, (lo, hi) in enumerate(halves):
                act.wait_ge(shifted, 6 + 2 * n)
                act.activation(m.rstd[:, lo:hi], m.var[:, lo:hi], ACT.Sqrt).then_inc(act_done, 1)
                exp(7 + 2 * n, gate[:, lo:hi, :], gate[:, lo:hi, :])
                if n == 0:
                    store(0)
            store(1)
            act.wait_ge(fin_done, T)
            act.dma_start(a["out"][(T - 1) * P:N, :], xs[FB][0:N - (T - 1) * P, 0, :]).then_inc(fin_out[FB], 16)
            for b in range(FB + 1):
                act.wait_ge(fin_out[b], 16 * (groups // FB if b < FB else 1))

        @block.vector
        def _(v):
            step = Steps(v, dve)
            hl = L // 2

            signals = iter(range(40))

            def signal(s):
                n = next(signals)
                step.wait()
                v.memset(marks[:, n:n + 1], 0.0).then_inc(s, 1)

            def leaky(out, z):
                return v.scalar_tensor_tensor(out, z, 0.2, z, ALU.mult, ALU.max)

            step(v.tensor_reduce(end_row[:, 0:1], pre, AX.X, ALU.add))
            step(v.tensor_tensor(end_row[:, 0:1], end_row[:, 0:1], m.length[:, 0:1], ALU.min))
            step(v.tensor_tensor(end_row[:, 0:1], end_row[:, 0:1], m.signs[:, 8:9], ALU.add))
            step.then(v.scalar_tensor_tensor(end_g, m.signs[:, 8:9], 1.0, end_row[:, 0:1], ALU.add, ALU.max))
            step(v.scalar_tensor_tensor(end_row[:, 1:2], end_row[:, 0:1], float(-BEYOND), same[:, 0:1], ALU.add, ALU.mult))
            step(v.tensor_scalar(end_s, end_row[:, 1:2], float(BEYOND), None, ALU.add))
            step.then(v.tensor_scalar(bar, same, -1.0, -NEG, ALU.add, ALU.mult))
            step(v.tensor_tensor(e, g[:, :, HE:TW], e, ALU.add))
            step(leaky(e, e))
            for h in range(H):
                step.then(v.tensor_tensor_scan(peak[:, :, h], bar, e[:, :, h], NEG, ALU.add, ALU.max))
            signal(peak_ready)
            for h in range(H):
                step.then(v.tensor_tensor_scan(highest[:, 0:L - 1, h][:, ::-1], bar[:, 1:L][:, ::-1],
                                               peak[:, 0:L - 1, h][:, ::-1], peak[:, L - 1:L, h], ALU.add, ALU.max))
            step.then(v.tensor_copy(highest[:, L - 1, :], peak[:, L - 1, :]))
            step.wait()
            for n, (lo, hi) in enumerate(((0, hl), (hl, L))):
                step(v.tensor_tensor(e[:, lo:hi, :], e[:, lo:hi, :], highest[:, lo:hi, :], ALU.subtract))
                signal(shifted)
            step.then(v.tensor_copy(colp[:, 0:HE].rearrange("p (h e) -> p h e", e=X),
                                    peak[:, L - 1, :].unsqueeze(2).to_broadcast([P, H, X])))
            step.then(v.tensor_copy(colp[:, HE:TW], peak[:, L - 1, :]))
            step.then(v.tensor_copy(flag, pre[:, L - 1:L].to_broadcast([P, TW])))
            signal(cols)
            def scale(lo, hi):
                msg = g[:, lo:hi, 0:HE].rearrange("p l (h e) -> p l h e", e=X)
                step.then(v.tensor_tensor(msg, msg, g[:, lo:hi, HE:TW].unsqueeze(3).to_broadcast([P, hi - lo, H, X]),
                                          ALU.mult))

            v.wait_ge(act_done, 1)
            scale(0, hl)
            v.wait_ge(turned, 1)
            last, kept = m.psum[0:TW, 0, 0:P], m.psum[0:TW, 0, P:2 * P]
            c, r = carry[0:TW, :], ratio[0:TW, :]
            step.then(v.tensor_scalar(line[0:TW, :], kept, -1.0, -NEG, ALU.add, ALU.mult))
            step(v.memset(c[:, 0:1], NEG))
            step(v.tensor_tensor_scan(c[:, 1:P + 1], line[0:TW, :], last, NEG, ALU.add, ALU.max))
            signal(cols)
            step.then(v.tensor_tensor(prev[0:TW, :], c[:, 0:P], line[0:TW, :], ALU.add))
            step(v.tensor_tensor(r[:, P:2 * P], last, c[:, 1:P + 1], ALU.subtract))
            step(v.tensor_tensor(r[:, 0:P], prev[0:TW, :], c[:, 1:P + 1], ALU.subtract))
            signal(shifted)
            v.wait_ge(act_done, 2)
            scale(hl, L)
            v.wait_ge(turned, 2)
            step(v.tensor_copy(back, m.psum[:, 1, 0:TW]))
            v.wait_ge(peak_end_in, 16)
            step(v.tensor_tensor(new_peak, end_peak, back[:, HE:TW], ALU.max))
            signal(peak_patch)
            step.then(v.tensor_tensor(w_end[:, 0:H], end_peak, new_peak, ALU.subtract))
            step.then(v.tensor_tensor(w_end[:, H:2 * H], back[:, HE:TW], new_peak, ALU.subtract))
            signal(shifted)
            for lo in range(0, L, QL):
                part_ = slice(lo, lo + QL)
                for k in range(TW):
                    step.then(v.tensor_tensor_scan(g[:, part_, k], same[:, part_], g[:, part_, k],
                                                   g[:, lo - 1:lo, k] if lo else 0.0, ALU.mult, ALU.add))
                signal(sum_ready)
            step(v.tensor_copy(colp, g[:, L - 1, :]))
            signal(cols)
            v.wait_ge(act_done, 3)
            v.wait_ge(turned, 3)
            step.then(v.memset(carry2[0:TW, 0:1], 0.0))
            step(v.tensor_tensor(prev[0:TW, :], m.psum[0:TW, 2, 0:P], r[:, P:2 * P], ALU.mult))
            step(v.tensor_tensor_scan(carry2[0:TW, 1:P + 1], r[:, 0:P], prev[0:TW, :], 0.0, ALU.mult, ALU.add))
            signal(cols)
            v.wait_ge(turned, 4)
            v.wait_ge(act_done, 4)
            step(v.tensor_copy(back2, m.psum[:, 3, 0:TW]))

            def by_column(out, x, weight):
                step.then(v.tensor_tensor(out[:, 0:HE].rearrange("p (h e) -> p h e", e=X),
                                          x[:, 0:HE].rearrange("p (h e) -> p h e", e=X),
                                          weight.unsqueeze(2).to_broadcast([P, H, X]), ALU.mult))
                step.then(v.tensor_tensor(out[:, HE:TW], x[:, HE:TW], weight, ALU.mult))

            by_column(part, back2, w_end[:, H:2 * H])
            v.wait_ge(sum_end_in, 16)
            by_column(new_sum, end_sum, w_end[:, 0:H])
            step.wait()
            step(v.tensor_tensor(new_sum, new_sum, part, ALU.add))
            signal(sum_patch)
            v.wait_ge(own_in, 64)
            step(v.tensor_tensor(es, own_src, own_dst, ALU.add))
            step(leaky(es, es))
            v.wait_ge(peak_in, 16 * T)
            step(v.tensor_tensor(top, top, spread(m.some, H), ALU.mult))
            step(v.tensor_scalar(m.tmp_s, m.some, -1.0, -NEG, ALU.add, ALU.mult))
            step(v.tensor_tensor(top, top, spread(m.tmp_s, H), ALU.add))
            step(v.tensor_tensor(cmp, top, es, ALU.max))
            step.then(v.tensor_tensor(w_edges, top, cmp, ALU.subtract))
            step.then(v.tensor_tensor(w_own, es, cmp, ALU.subtract))
            signal(shifted)
            v.wait_ge(act_done, 5)

            def heads(ap):
                return ap.rearrange("p t (h e) -> p t h e", e=X)

            def each(ap, tiles=T):
                return ap.unsqueeze(3).to_broadcast([P, tiles, H, X])

            step.then(v.tensor_tensor(heads(own_part[:, :, 0:HE]), heads(own_h), each(w_own), ALU.mult))
            step(v.tensor_scalar(own_part[:, :, HE:TW], w_own, 1e-16, None, ALU.add))

            def node_gates(lo, hi, n):
                tiles = hi - lo
                w_e, own_p, s, i, c, sc, gt, rk = (k[:, lo:hi, :] for k in (w_edges, own_part, sums, inv, agg, score, gate, rank))
                mean, var = m.mean[:, lo:hi], m.var[:, lo:hi]

                def over(ap, n):
                    return ap.unsqueeze(2).to_broadcast([P, tiles, n])

                def param(k):
                    return par[:, k, :].unsqueeze(1).to_broadcast([P, tiles, HE])

                v.wait_ge(sum_in[n], gathered + 16 * tiles)
                step.then(v.tensor_tensor(heads(c), heads(s[:, :, 0:HE]), each(w_e, tiles), ALU.mult))
                step(v.tensor_tensor(i, s[:, :, HE:TW], w_e, ALU.mult))
                step.then(v.tensor_tensor(c, c, own_p[:, :, 0:HE], ALU.add))
                step(v.tensor_tensor(i, i, own_p[:, :, HE:TW], ALU.add))
                step(v.reciprocal(i, i))
                step(v.tensor_tensor(heads(c), heads(c), each(i, tiles), ALU.mult))
                step(v.tensor_tensor(c, c, param(0), ALU.add))
                step(v.tensor_reduce(mean, c, AX.X, ALU.add))
                step(v.tensor_scalar(mean, mean, 1.0 / HE, None, ALU.mult))
                step(v.tensor_tensor(c, c, over(mean, HE), ALU.subtract))
                step(v.tensor_tensor(sq[:, lo:hi, :], c, c, ALU.mult))
                step(v.tensor_reduce(var, sq[:, lo:hi, :], AX.X, ALU.add))
                step(v.tensor_scalar(var, var, 1.0 / HE, EPS, ALU.mult, ALU.add))
                signal(shifted)
                v.wait_ge(act_done, 6 + 2 * n)
                inverse_root(v, m, step, lo, hi)
                step(v.tensor_tensor(c, c, over(m.rstd[:, lo:hi], HE), ALU.mult))
                step(v.tensor_tensor(c, c, param(1), ALU.mult))
                step(v.tensor_tensor(c, c, param(2), ALU.add))
                step(v.tensor_reduce(sc, c.rearrange("p t (h e) -> p t e h", e=X), AX.X, ALU.add))
                step(v.tensor_scalar(sc, sc, 1.0 / H, None, ALU.mult))
                step(v.tensor_reduce(mean, sc, AX.X, ALU.max))
                step(v.tensor_tensor(gt, sc, over(mean, X), ALU.subtract))
                signal(shifted)
                pairs = [(lo_, hi_) for hi_ in range(1, X) for lo_ in range(hi_)]
                wins = sq[:, lo:hi, :].rearrange("p t c -> p c t")
                for x in range(X):
                    step.then(v.memset(rk[:, :, x], float(X - 1 - x)))
                for k, (first, second) in enumerate(pairs):
                    step.then(v.tensor_tensor(wins[:, k, :], sc[:, :, first], sc[:, :, second], ALU.is_ge))
                step.wait()
                for k, (first, second) in enumerate(pairs):
                    step.then(v.tensor_tensor(rk[:, :, second], rk[:, :, second], wins[:, k, :], ALU.add))
                    step.wait()
                    step(v.scalar_tensor_tensor(rk[:, :, first], wins[:, k, :], -1.0, rk[:, :, first], ALU.mult, ALU.add))
                v.wait_ge(act_done, 7 + 2 * n)
                step(v.scalar_tensor_tensor(gt, rk, 2.0, gt, ALU.is_lt, ALU.mult))
                step(v.tensor_reduce(var, gt, AX.X, ALU.add))
                step(v.reciprocal(var, var))
                step(v.tensor_tensor(gt, gt, over(var, X), ALU.mult))

            def combine(t, b, k, x):
                return v.scalar_tensor_tensor(xs[b][:, k, :], slot[b][:, k, x, :], gate[:, t:t + 1, x],
                                              xs[b][:, k, :], ALU.mult, ALU.add)

            for r, (lo, hi) in enumerate(halves):
                node_gates(lo, hi, r)
                for n in range(FB):
                    b = (n + FB - 2) % FB
                    v.wait_ge(fin_in[b], r * 32 + (before + 32))
                    for x in range(X):
                        step.wait()
                        for k in range(FG):
                            ins = combine((r * FB + n) * FG + k, b, k, x)
                            if x < X - 1:
                                step.then(ins)
                            else:
                                ins.then_inc(fin_done, 1)
            v.wait_ge(fin_in[FB], 2 * before + 32)
            for x in range(X - 1):
                step(combine(T - 1, FB, 0, x))
            combine(T - 1, FB, 0, X - 1).then_inc(fin_done, 1)


def program(nc, a):
    ctx = ExitStack()
    m = Mem()
    with ctx:
        allocate(nc, ctx, m)
        load_and_normalise(nc, ctx, m, a)
        gather_and_sort(nc, ctx, m, a)
        first_layer(nc, ctx, m, a)
        gather_and_experts(nc, ctx, m, a)
        attention(nc, ctx, m, a)


def constants():
    p = np.arange(P)

    def sign(k):
        return np.where((p >> (k - LOG_L)) & 1, -1.0, 1.0)

    last = LOG_L + 7
    signs = [sign(LOG_L)] + [sign(k) * sign(k - 1) for k in range(LOG_L + 1, last)] + [sign(last - 1), p * L - 1.0]
    nodes = np.arange(ST)[None, :] * P + p[:, None]
    return {
        "c_ident": np.eye(P, dtype=np.float32),
        "c_iota": np.ascontiguousarray(np.broadcast_to(p.astype(np.float32), (P, P))),
        "c_signs": np.stack(signs, axis=1).astype(np.float32),
        "c_nodekey": ((nodes << SHIFT) | KEY_BASE).astype(np.int32).view(np.float32),
    }


SCRATCH = {"feat": ((NP, D), F32), "rng_i": ((2, GP), I32), "rng_f": ((GP,), F32), "keys": ((E2,), F32), "rows": ((E2,), F32),
           "starts": ((ST * P,), F32), "x2": ((NP, D), F32), "table": ((NP, WX), F32), "values": ((E2, H), F32), "subs": ((P, L // SUB), F32),
           "peaks": ((E2, H), F32), "sums": ((E2, TW), F32), "y": ((ST * P, X, D), F32)}
_INS = ["x", "src", "dst", "edge_weight", "L0_gnn_W", "L0_gnn_b", "L0_ffn_W_gat", "L0_ffn_att_src", "L0_ffn_att_dst",
        "L0_ffn_b_gat", "L0_ffn_ln_gamma", "L0_ffn_ln_beta", "L0_ffn_W1", "L0_ffn_b1", "L0_ffn_W2", "L0_ffn_b2",
        "L0_ffn_edge_index"]


def kernel(**inputs):
    import concourse.bacc as bacc
    from concourse.bass_utils import run_bass_kernel_spmd

    nc = bacc.Bacc("TRN2", target_bir_lowering=False, num_devices=1)
    arrays, a = {}, {}
    for name, value in [(n, inputs[n]) for n in _INS] + list(constants().items()):
        value = np.ascontiguousarray(value)
        arrays[f"in_{name}"] = value
        a[name] = nc.dram_tensor(f"in_{name}", value.shape, mybir.dt.from_np(value.dtype), kind="ExternalInput").ap()
    for name, (shape, dt) in SCRATCH.items():
        a[name] = nc.dram_tensor(f"s_{name}", list(shape), dt, kind="Internal").ap()
    a["out"] = nc.dram_tensor("out_0", [N, D], F32, kind="ExternalOutput").ap()
    program(nc, a)
    return run_bass_kernel_spmd(nc, [arrays], core_ids=[0]).results[0]["out_0"]
```
